# Optimizing a Trainium2 kernel written in Bass

```python
import numpy as np
import jax
import jax.numpy as jnp

def _softmax(x, axis=-1):
    return jax.nn.softmax(x, axis=axis)

def _gelu(x):
    return jax.nn.gelu(x, approximate=True)

def _silu(x):
    return jax.nn.silu(x)

def _sigmoid(x):
    return jax.nn.sigmoid(x)

def _layernorm(x, axis=-1, eps=1e-05):
    m = jnp.mean(x, axis=axis, keepdims=True)
    v = jnp.var(x, axis=axis, keepdims=True)
    return (x - m) / jnp.sqrt(v + eps)

def _scatter_add(tgt, idx, src, axis=0):
    return tgt.at[idx].add(src)

def _segment_sum(src, seg, n):
    return jax.ops.segment_sum(src, seg, n)
kernel_name = 'mk_recurrent_d2_jaxref_r8_0e49ab'

def setup_inputs(seed: int=0):
    np.random.seed(seed)
    _w = jnp.asarray

    def _L0_attn_setup():
        import jax, jax.numpy as jnp
        import numpy as np
        B, T, C = (2, 256, 128)
        N_HEAD = 16
        WINDOW = 64
        ROPE_BASE = 10000.0

        def _apply_rotary(x, cos, sin):
            d = x.shape[-1] // 2
            x1, x2 = (x[..., :d], x[..., d:])
            return jnp.concatenate([x1 * cos + x2 * sin, -x1 * sin + x2 * cos], axis=-1)
        key = jax.random.key(seed)
        k1, k2, k3 = jax.random.split(key, 3)
        x = jax.random.normal(k1, (B, T, C), dtype=jnp.float32)
        w_attn = jax.random.normal(k2, (3 * C, C), dtype=jnp.float32) * 0.02
        w_proj = jax.random.normal(k3, (C, C), dtype=jnp.float32) * 0.02
        return {'x': x, 'w_attn': w_attn, 'w_proj': w_proj}
    _L0_attn_in = _L0_attn_setup()

    def _L0_ffn_setup():
        import jax, jax.numpy as jnp
        import numpy as np
        THRESH_FACTOR = 0.7

        def ternary_quantize(w):
            delta = THRESH_FACTOR * jnp.mean(jnp.abs(w))
            return jnp.where(w > delta, 1.0, jnp.where(w < -delta, -1.0, 0.0)).astype(w.dtype)
        key = jax.random.key(seed)
        k1, k2, k3 = jax.random.split(key, 3)
        B, S, D_IN, D_OUT = (8, 512, 128, 128)
        inp = {'input': jax.random.normal(k1, (B, S, D_IN), dtype=jnp.float32), 'weight': jax.random.normal(k2, (D_OUT, D_IN), dtype=jnp.float32) * (1.0 / np.sqrt(D_IN)), 'alpha': jnp.ones((1,), dtype=jnp.float32), 'bias': jax.random.normal(k3, (D_OUT,), dtype=jnp.float32) * (1.0 / np.sqrt(D_IN))}
        return inp
    _L0_ffn_in = _L0_ffn_setup()

    def _L1_attn_setup():
        import jax, jax.numpy as jnp
        import numpy as np
        D_MODEL = 128
        N_HEADS = 16
        ORDER = 6
        P2 = 2 * ORDER - 1
        EPS_CLAMP = 1e-06
        EPS_DEN = 1e-07

        def _beta_np():
            j = np.arange(ORDER, dtype=np.float32)
            alpha = (j + 1.0) ** (-1.5)
            tail = np.flip(np.cumsum(np.flip(alpha)))
            beta = np.concatenate([np.zeros(1, np.float32), tail[1:].astype(np.float32), np.zeros(ORDER - 1, np.float32)])
            return beta / beta.sum()

        def _cheb(x):
            T = [jnp.ones_like(x), x]
            for _ in range(2, P2):
                T.append(2.0 * x * T[-1] - T[-2])
            return jnp.stack(T, axis=3)
        key = jax.random.key(seed)
        k1, k2, k3 = jax.random.split(key, 3)
        B, S, D = (2, 128, D_MODEL)
        x = jax.random.normal(k1, (B, S, D), dtype=jnp.float32)
        W_in = jax.random.normal(k2, (3 * D, D), dtype=jnp.float32) * 0.02
        W_out = jax.random.normal(k3, (D, D), dtype=jnp.float32) * 0.02
        return {'x': x, 'W_in': W_in, 'W_out': W_out}
    _L1_attn_in = _L1_attn_setup()

    def _L1_ffn_setup():
        import jax, jax.numpy as jnp
        import numpy as np
        B, S, H = (8, 128, 128)
        FF = 512
        E = 8
        TOP_K = 2
        LN_EPS = 1e-12

        def _layernorm(x, w, b):
            mu = jnp.mean(x, axis=-1, keepdims=True)
            var = jnp.mean(jnp.square(x - mu), axis=-1, keepdims=True)
            return (x - mu) * jax.lax.rsqrt(var + LN_EPS) * w + b
        key = jax.random.key(seed)
        ks = jax.random.split(key, 8)
        sc_h = 1.0 / np.sqrt(H)
        sc_ff = 1.0 / np.sqrt(FF)
        return {'hidden_states': jax.random.normal(ks[0], (B, S, H), jnp.float32), 'router_w': jax.random.normal(ks[1], (E, H), jnp.float32) * sc_h, 'router_b': jnp.zeros((E,), jnp.float32), 'w1': jax.random.normal(ks[2], (E, FF, H), jnp.float32) * sc_h, 'b1': jax.random.normal(ks[3], (E, FF), jnp.float32) * 0.01, 'w2': jax.random.normal(ks[4], (E, H, FF), jnp.float32) * sc_ff, 'b2': jax.random.normal(ks[5], (E, H), jnp.float32) * 0.01, 'ln_w': jnp.ones((H,), jnp.float32), 'ln_b': jnp.zeros((H,), jnp.float32)}
    _L1_ffn_in = _L1_ffn_setup()
    _d = {'L0_attn_x': _L0_attn_in['x'], 'L0_attn_w_attn': _L0_attn_in['w_attn'], 'L0_attn_w_proj': _L0_attn_in['w_proj'], 'L0_ffn_weight': _L0_ffn_in['weight'], 'L0_ffn_alpha': _L0_ffn_in['alpha'], 'L0_ffn_bias': _L0_ffn_in['bias'], 'L1_attn_W_in': _L1_attn_in['W_in'], 'L1_attn_W_out': _L1_attn_in['W_out'], 'L1_ffn_router_w': _L1_ffn_in['router_w'], 'L1_ffn_router_b': _L1_ffn_in['router_b'], 'L1_ffn_w1': _L1_ffn_in['w1'], 'L1_ffn_b1': _L1_ffn_in['b1'], 'L1_ffn_w2': _L1_ffn_in['w2'], 'L1_ffn_b2': _L1_ffn_in['b2'], 'L1_ffn_ln_w': _L1_ffn_in['ln_w'], 'L1_ffn_ln_b': _L1_ffn_in['ln_b']}
    _x0 = _d['L0_attn_x']
    _d['L0_attn_x'] = jax.random.normal(jax.random.fold_in(jax.random.key(seed), 1), (4, 1024, 128), dtype=_x0.dtype)
    del _x0
    return _d

def reference(L0_attn_x, L0_attn_w_attn, L0_attn_w_proj, L0_ffn_weight, L0_ffn_alpha, L0_ffn_bias, L1_attn_W_in, L1_attn_W_out, L1_ffn_router_w, L1_ffn_router_b, L1_ffn_w1, L1_ffn_b1, L1_ffn_w2, L1_ffn_b2, L1_ffn_ln_w, L1_ffn_ln_b):

    def _L0_attn_ref(x, w_attn, w_proj):
        import jax, jax.numpy as jnp
        import numpy as np
        B, T, C = (2, 256, 128)
        N_HEAD = 16
        WINDOW = 64
        ROPE_BASE = 10000.0

        def _apply_rotary(x, cos, sin):
            d = x.shape[-1] // 2
            x1, x2 = (x[..., :d], x[..., d:])
            return jnp.concatenate([x1 * cos + x2 * sin, -x1 * sin + x2 * cos], axis=-1)
        Bb, Tt, Cc = x.shape
        H = N_HEAD
        D = Cc // H
        qkv = x @ w_attn.T
        q, k, v = jnp.split(qkv, 3, axis=2)
        q = q.reshape(Bb, Tt, H, D)
        k = k.reshape(Bb, Tt, H, D)
        v = v.reshape(Bb, Tt, H, D)
        inv_freq = 1.0 / ROPE_BASE ** (jnp.arange(0, D, 2, dtype=jnp.float32) / D)
        freqs = jnp.outer(jnp.arange(Tt, dtype=jnp.float32), inv_freq)
        cos = jnp.cos(freqs)[None, :, None, :]
        sin = jnp.sin(freqs)[None, :, None, :]
        q = _apply_rotary(q, cos, sin)
        k = _apply_rotary(k, cos, sin)
        pos = jnp.arange(Tt)
        diff = pos[:, None] - pos[None, :]
        mask = (diff >= 0) & (diff <= WINDOW)
        scale = 1.0 / jnp.sqrt(jnp.asarray(D, dtype=q.dtype))
        scores = jnp.einsum('bqhd,bkhd->bhqk', q, k) * scale
        scores = jnp.where(mask[None, None, :, :], scores, jnp.asarray(-1e+30, scores.dtype))
        attn = jax.nn.softmax(scores, axis=-1)
        y = jnp.einsum('bhqk,bkhd->bqhd', attn, v).reshape(Bb, Tt, Cc)
        return y @ w_proj.T

    def _L0_ffn_ref(input, weight, alpha, bias):
        import jax, jax.numpy as jnp
        import numpy as np
        THRESH_FACTOR = 0.7

        def ternary_quantize(w):
            delta = THRESH_FACTOR * jnp.mean(jnp.abs(w))
            return jnp.where(w > delta, 1.0, jnp.where(w < -delta, -1.0, 0.0)).astype(w.dtype)
        w_ternary = ternary_quantize(weight)
        w_eff = w_ternary * alpha
        out = jnp.einsum('bsd,od->bso', input, w_eff) + bias
        return out

    def _L1_attn_ref(x, W_in, W_out):
        import jax, jax.numpy as jnp
        import numpy as np
        D_MODEL = 128
        N_HEADS = 16
        ORDER = 6
        P2 = 2 * ORDER - 1
        EPS_CLAMP = 1e-06
        EPS_DEN = 1e-07

        def _beta_np():
            j = np.arange(ORDER, dtype=np.float32)
            alpha = (j + 1.0) ** (-1.5)
            tail = np.flip(np.cumsum(np.flip(alpha)))
            beta = np.concatenate([np.zeros(1, np.float32), tail[1:].astype(np.float32), np.zeros(ORDER - 1, np.float32)])
            return beta / beta.sum()

        def _cheb(x):
            T = [jnp.ones_like(x), x]
            for _ in range(2, P2):
                T.append(2.0 * x * T[-1] - T[-2])
            return jnp.stack(T, axis=3)
        B, S, D = x.shape
        H, Dh = (N_HEADS, D // N_HEADS)
        qkv = jnp.einsum('bsd,ed->bse', x, W_in)
        q, k, v = jnp.split(qkv, 3, axis=-1)
        q = q.reshape(B, S, H, Dh).transpose(0, 2, 1, 3)
        k = k.reshape(B, S, H, Dh).transpose(0, 2, 1, 3)
        v = v.reshape(B, S, H, Dh).transpose(0, 2, 1, 3)
        inv_sqrt_d = 1.0 / jnp.sqrt(jnp.float32(Dh))
        xq = jnp.clip(q * inv_sqrt_d, -1.0 + EPS_CLAMP, 1.0 - EPS_CLAMP)
        xk = jnp.clip(k * inv_sqrt_d, -1.0 + EPS_CLAMP, 1.0 - EPS_CLAMP)
        Tq = _cheb(xq)
        Tk = _cheb(xk)
        beta = jnp.asarray(_beta_np())
        Tv = Tk * v[:, :, :, None, :]
        kv_prefix = jnp.cumsum(Tv, axis=2)
        ks_prefix = jnp.cumsum(Tk.sum(axis=-1), axis=2)
        kv_beta = kv_prefix * beta[None, None, None, :, None]
        k_beta = ks_prefix * beta[None, None, None, :]
        num = (Tq * kv_beta).sum(axis=3)
        den = (Tq.sum(axis=-1) * k_beta).sum(axis=3)
        out_h = num / (den[..., None] + EPS_DEN)
        out = out_h.transpose(0, 2, 1, 3).reshape(B, S, H * Dh)
        return jnp.einsum('bsd,ed->bse', out, W_out)

    def _L1_ffn_ref(hidden_states, router_w, router_b, w1, b1, w2, b2, ln_w, ln_b):
        import jax, jax.numpy as jnp
        import numpy as np
        B, S, H = (8, 128, 128)
        FF = 512
        E = 8
        TOP_K = 2
        LN_EPS = 1e-12

        def _layernorm(x, w, b):
            mu = jnp.mean(x, axis=-1, keepdims=True)
            var = jnp.mean(jnp.square(x - mu), axis=-1, keepdims=True)
            return (x - mu) * jax.lax.rsqrt(var + LN_EPS) * w + b
        b, s, h = hidden_states.shape
        flat = hidden_states.reshape(-1, h)
        logits = flat @ router_w.T + router_b
        topk_vals, topk_idx = jax.lax.top_k(logits, TOP_K)
        topk_w = jax.nn.softmax(topk_vals, axis=-1)
        out = jnp.zeros_like(flat)
        n_exp = w1.shape[0]
        for e in range(n_exp):
            cw = jnp.sum(jnp.where(topk_idx == e, topk_w, 0.0), axis=-1)
            y = jax.nn.gelu(flat @ w1[e].T + b1[e], approximate=False)
            y = y @ w2[e].T + b2[e]
            out = out + y * cw[:, None]
        out = out.reshape(b, s, h) + hidden_states
        return _layernorm(out, ln_w, ln_b)
    x = L0_attn_x
    xn = _layernorm(x, axis=-1)
    s = _L0_attn_ref(xn, L0_attn_w_attn, L0_attn_w_proj)
    g = _silu(_L0_ffn_ref(xn, L0_ffn_weight, L0_ffn_alpha, L0_ffn_bias))
    x = x + s * g
    xn = _layernorm(x, axis=-1)
    s = _L1_attn_ref(xn, L1_attn_W_in, L1_attn_W_out)
    g = _silu(_L1_ffn_ref(xn, L1_ffn_router_w, L1_ffn_router_b, L1_ffn_w1, L1_ffn_b1, L1_ffn_w2, L1_ffn_b2, L1_ffn_ln_w, L1_ffn_ln_b))
    x = x + s * g
    return x

_drawn_inputs = setup_inputs


def setup_inputs(seed=0):
    import zlib

    import numpy as np

    out = dict(_drawn_inputs(seed))
    spreads = {'L1_ffn_router_b': (0.0, 0.8), 'L1_ffn_ln_w': (1.0, 0.6), 'L1_ffn_ln_b': (0.0, 0.8)}
    factors = {'L0_ffn_bias': 8.0,
     'L1_attn_W_in': 8.0,
     'L1_attn_W_out': 8.0,
     'L1_ffn_router_w': 8.0,
     'L1_ffn_w1': 8.0,
     'L1_ffn_b1': 64.0,
     'L1_ffn_w2': 8.0,
     'L1_ffn_b2': 200.0}
    for name, (base, spread) in spreads.items():
        noise = np.random.default_rng([zlib.crc32(name.encode()), seed]).standard_normal(out[name].shape)
        drawn = base * np.exp(spread * noise) if base else spread * noise
        out[name] = jnp.asarray(drawn.astype(out[name].dtype))
    for name, factor in factors.items():
        out[name] = (out[name] * factor).astype(out[name].dtype)
    return out
```

```python
from contextlib import ExitStack

import concourse.bass as bass
import numpy as np
from concourse import mybir

F32 = mybir.dt.float32
F16 = mybir.dt.float16
BF16 = mybir.dt.bfloat16
ALU = mybir.AluOpType
ACT = mybir.ActivationFunctionType
AX = mybir.AxisListType

P = 128
B, T, C = 4, 1024, 128
NT = B * T // P
TAUS = T // P
H, D = 16, 8
W = 64
NG = 4
NPAIR = H // 2
VW = 32
EPS0 = 1e-5
IL = 4
NEG = -1e30

ORD = 5
SW = C + H
E, FF = 8, 512
FB = FF // P
CHEB1, CHEB2 = 13, 12
ROUTE = 20
_ALPHA = np.arange(1, ORD + 2, dtype=np.float32) ** -1.5
_BETA = np.cumsum(_ALPHA[::-1])[::-1][1:].astype(np.float32)
BETA = [float(v) for v in _BETA / _BETA.sum()]
INV = float(D) ** -0.5
CLIP = 1.0 - 1e-6
SLOTS = [[], [("CS", 0), ("CP", 1)], [("OT", 0)], [("SO", 0), ("CS", 1), ("CP", 2)], [("OT", 1)],
         [("SO", 1), ("CS", 2), ("CP", 3)], [("OT", 2), ("SO", 2)], [("CS", 3)]]
DVE_ORDER = [("keys", 0), ("residual", 0), ("sum", 0), ("gate", 0), ("sum", 1), ("out", 0), ("keys", 1), ("sum", 2),
             ("sum", 3), ("out", 1), ("keys", 2), ("sum", 4), ("sum", 5), ("out", 2), ("keys", 3), ("sum", 6),
             ("sum", 7), ("out", 3)]


class Tile:

    def __init__(self, t, m):
        self.static = isinstance(t, int)
        if self.static:
            t, m = (4 * t + m) // 4, (4 * t + m) % 4
        self.t, self.m = t, m
        self.batch = m % 4
        self.tau = t + m // 4
        self.index = t * 4 + m
        self.exists = not self.static or 0 <= self.index < NT
        self.first = self.static and self.tau == 0

    def before(self, lag):
        return Tile(self.t, self.m - lag)

    def count(self, per, k):
        return self.t * (4 * per) + (self.m * per + k)


class Stage:

    def __init__(self, sem, per=1):
        self.sem, self.per = sem, per

    def wait(self, engine, tile, k=None):
        if tile.static and tile.index < 0:
            return
        k = self.per if k is None else k
        if tile.static and tile.index >= NT:
            tile, k = Tile(TAUS - 1, 3), self.per
        engine.wait_ge(self.sem, tile.count(self.per, k))


def pipeline(engine, step, lags):
    for n in range(8):
        step(Tile(0, n))
    with engine.Fori(2, TAUS) as t:
        for k in range(4):
            step(Tile(t, k))
    for n in range(lags):
        step(Tile(TAUS, n))


class Round:

    def __init__(self, t):
        self.static = isinstance(t, int)
        self.t, self.index, self.tiles = t, t, bass.ts(t, B)
        self.first = self.static and t == 0

    def before(self, rounds):
        return Round(self.t - rounds)

    def count(self, per, k):
        return self.t * per + k

    def at(self, i, items, each=1):
        return (self, (i + 1) * each) if i >= 0 else (self.before(1), (i + items + 1) * each)

    def at_acc(self, e):
        return (self, 1 + B * (e + 1)) if e >= 0 else (self.before(1), 1 + B * (e + E + 1))

    def wait_dma(self, engine, sem):
        if not self.first:
            engine.wait_ge(sem, self.t * 16)

    def wait_carry(self, engine, sems, b):
        if b >= 0:
            engine.wait_ge(sems[b], self.t * 16 + 16)
        else:
            self.wait_dma(engine, sems[b + B])


def rounds(engine, mix):
    mix(Round(0))
    with engine.Fori(1, TAUS) as t:
        mix(Round(t))


def turn(engine, sem):
    engine.sem_inc(sem, 1)


def program(nc, x, proj_w, ffn_w, alpha, bias0, out_w, rope, eye, win_max, win_exp, pair_sel,
            router_w, router_b, cheb_w, cheb_out_w, tri, descend, w1, b1, w2, b2, ln_w, ln_b, out):
    ctx = ExitStack()
    with ctx:
        def sb(name, shape, dt=F32):
            return ctx.enter_context(nc.sbuf_tensor(name, shape, dt))

        def bank(name, shape, dt=F32):
            return ctx.enter_context(nc.psum_tensor(name, shape, dt))

        def sem(name):
            return ctx.enter_context(nc.semaphore(name))

        def stage(name, per=1):
            return Stage(sem(name), per)

        x_all = sb("x_all", [P, NT, C])
        xn1_all = sb("xn1_all", [P, NT, C])
        xn1t_all = sb("xn1t_all", [P, NT, P])
        logits = sb("logits", [P, NT, 8])

        wp = sb("wp", [P, 3 * C + C])
        wraw = sb("wraw", [P, C])
        wneg = sb("wneg", [P, C])
        wsum = sb("wsum", [P, 2])
        alpha_sb = sb("alpha_sb", [P, 1])
        bias0_sb = sb("bias0_sb", [P, C])
        wo = sb("wo", [P, C])
        rope_sb = sb("rope_sb", [P, TAUS, 2 * D])
        eye_sb = sb("eye_sb", [P, P])
        eye16_sb = sb("eye16_sb", [P, P], F16)
        eyeb_sb = sb("eyeb_sb", [P, P], BF16)
        ones_sb = sb("ones_sb", [P, P])
        winm_sb = sb("winm_sb", [P, NG, P], BF16)
        mm_sb = sb("mm_sb", [P, 4, 2 * P], BF16)
        hide_sb = sb("hide_sb", [P, NG, W], BF16)
        pair_sb = sb("pair_sb", [P, NPAIR, P], BF16)
        rw = sb("rw", [P, 8])
        rb = sb("rb", [P, 8])
        half_sb = sb("half_sb", [P, 1])

        stats = sb("stats", [P, 4, 6])
        mv = sb("mv", [P, 4, 2])
        rstd = sb("rstd", [P, 4, 2])
        xn = sb("xn", [P, 4, C])
        xnt = sb("xnt", [P, 4, P])
        rot = sb("rot", [P, 2, 2, 2 * C])
        xs = sb("xs", [P, 4, 2 * H, 4, D], F16)
        qt = sb("qt", [P, 4, NG, P], F16)
        kt = sb("kt", [P, 4, NG, W + P], F16)
        vd = sb("vd", [P, 4, 3, NPAIR, VW])
        mneg = sb("mneg", [P, 4, 2, NPAIR], BF16)
        pexp = sb("pexp", [P, 4, 2, 2 * P])
        yts = sb("yts", [P, 2 * P])
        rden = sb("rden", [P, H])
        yn = sb("yn", [P, C])
        ynt = sb("ynt", [P, P])
        z = sb("z", [P, 4, C])
        ez = sb("ez", [P, C])
        gd = sb("gd", [P, 3, C])
        sg = sb("sg", [P, C])
        stats1 = sb("stats1", [P, 4, 6])
        mv1 = sb("mv1", [P, 4, 2])
        rstd1 = sb("rstd1", [P, 4, 2])
        xn1 = sb("xn1", [P, 4, C])
        xn1t = sb("xn1t", [P, 4, P])

        w_in = sb("w_in", [P, 3 * C])
        w_out = sb("w_out", [P, C])
        tri_sb = sb("tri_sb", [P, P])
        desc_sb = sb("desc_sb", [P, E])
        w1_sb = sb("w1_sb", [P, E, FF])
        b1_sb = sb("b1_sb", [P, E, FB])
        w2_sb = sb("w2_sb", [P, E, FB, C])
        b2_sb = sb("b2_sb", [E, C])
        lnw_sb = sb("lnw_sb", [P, C])
        lnb_sb = sb("lnb_sb", [P, C])
        cw = sb("cw", [P, NT, E])
        rt = sb("rt", [P, 5, NT, E])
        rs = sb("rs", [P, 8, NT])
        xg = sb("xg", [P, B, P])
        cwg = sb("cwg", [P, B, E])
        cwt = sb("cwt", [E, B, P])
        vs = sb("vs", [P, 2, C])
        xc = sb("xc", [P, 2 * C])
        kv = sb("kv", [P, 2, ORD * SW])
        tq = sb("tq", [P, ORD, SW])
        pr = sb("pr", [P, ORD, SW])
        nd = sb("nd", [P, SW])
        dn = sb("dn", [P, 2, H])
        oc = sb("oc", [P, C])
        oct_ = sb("oct", [P, P])
        s1 = sb("s1", [P, B, C])
        last_sb = sb("last_sb", [P, 2, ORD * SW])
        carry = sb("carry", [1, B, ORD * SW])
        stats2 = sb("stats2", [P, B, 6])
        mv2 = sb("mv2", [P, B, 2])
        rstd2 = sb("rstd2", [P, 2, B])
        eps2_sb = sb("eps2_sb", [P, B])

        m_ps = [bank(f"m_ps{i}", [P, NG, P]) for i in range(2)]
        e_ps = [bank(f"e_ps{i}", [P, 2, 2 * P]) for i in range(2)]
        p_ps = bank("p_ps", [P, 4 * C])
        q_ps = bank("q_ps", [P, 2 * NG, P], F16)
        t_ps = bank("t_ps", [P, 4, P])
        y_ps = bank("y_ps", [P, 4, P])
        tb_ps = t_ps[:, :, :].rearrange("p a b -> p (a b)").bitcast(BF16)

        y2, e2, res, acc = (xs[:, i, :, :, :].rearrange("p h s d -> p (h s d)").bitcast(F32).rearrange("p (b c) -> p b c", b=B)
                            for i in range(4))
        tc = kt[:, :, :, :].rearrange("p b g t -> p (b g t)").bitcast(F32)[:, 0:ORD * 2 * C].rearrange("p (j c) -> p j c", j=ORD)
        hid = [pexp[:, :, :, :].rearrange("p j a b -> p j (a b)"),
               vd[:, :, :, :, :].rearrange("p a b i w -> p (a b i w)")[:, 0:FB * B * P].rearrange("p (f t) -> p f t", f=FB)]
        u_ps = [m_ps[i][:, :, :].rearrange("p a b -> p (a b)") for i in range(2)]
        d_ps = [e_ps[i][:, :, :].rearrange("p a (h b) -> p (a h) b", b=P) for i in range(2)]
        cc_ps = [y_ps[:, :, :].rearrange("p a b -> p (a b)"), q_ps[:, :, :].rearrange("p a b -> p (a b)").bitcast(F32)]

        CP, XG, CL, CA, C1, C2 = (stage(*a) for a in (("cheb_projected", 4), ("gathered", 2), ("last_row", 4), ("carried", 4), ("cheb_keys", 4 * CHEB1), ("cheb_out", 4 * CHEB2)))
        CS, OT, SO, CW = (stage(*a) for a in (("prefix_sums", 4), ("cheb_transposed", 4), ("cheb_out_projected", 4), ("weights_transposed", 2)))
        UP, DN, GE, VC = (stage(*a) for a in (("up", E * FB), ("down", E), ("gelu", E * FB), ("v_copied", 4)))
        OE, SE1, CT, AC = (stage(*a) for a in (("cheb_out_copied", 4), ("s1_copied", 4), ("weights_copied", 1), ("accumulated", 1 + 4 * E)))
        F1, F2, R2, EX2 = (stage(*a) for a in (("ln_steps", 18), ("result", 1), ("rstd2", 2), ("last_exp", 1)))
        s_carry = [sem(f"s_carry{b}") for b in range(B)]
        s_out = sem("s_out")
        s_w2 = sem("s_w2")
        s_cw = sem("s_cw")
        s_we = sem("s_we")

        s_x = [sem(f"s_x{i}") for i in range(3)]
        s_w = sem("s_w")
        s_win = sem("s_win")
        s_zero = sem("s_zero")
        s_init = sem("s_init")
        s_ps = sem("s_ps")
        s_turn_pool, s_turn_dve = sem("s_turn_pool"), sem("s_turn_dve")
        TX, PR, TQ, MX, TM = stage("xn_transposed"), stage("projected"), stage("qk_transposed"), stage("max_scored", 4), stage("max_transposed")
        SE, PV, TY, T2 = stage("scored", 4), stage("weighted", 4), stage("y_transposed"), stage("yn_transposed")
        OP, TX1, LM = stage("out_projected"), stage("xn1_transposed"), stage("routed")
        XT, HI, VB, QK, EX = stage("xnt_copied"), stage("high_parts"), stage("values_placed", 4), stage("qk_copied", 3), stage("exponentials", 4)
        EZ, YT, Y2, X1T = stage("gate_exp"), stage("yt_copied"), stage("ynt_copied"), stage("xn1t_copied")
        ST, XN, RED, MMR, RP = stage("stats0", 2), stage("xn_ready"), stage("maxima", 4), stage("maxima_placed", 2), stage("rotated", 6)
        ZG, YN, GT, XN1, LG = stage("gate_in"), stage("y_normed", 2), stage("gated", 10), stage("xn1_ready"), stage("logits_ready")
        R0, DUP, VP, R1, SX = stage("rstd0", 2), stage("parts_doubled", 2), stage("values_kept"), stage("rstd1", 2), stage("xn1_stored", 2)

        block = ctx.enter_context(nc.Block())

        @block.sync
        def _(sp):
            xv = x.rearrange("b (t p) c -> p t b c", p=P)
            xo = x_all[:, :, :].rearrange("p (t b) c -> p t b c", b=B)
            weights = [(wp[:, 0:3 * C], proj_w), (wraw[:, :], ffn_w), (alpha_sb[:, :], alpha), (bias0_sb[:, :], bias0),
                       (wo[:, :], out_w), (rope_sb[:, :, :], rope), (eye_sb[:, :], eye), (rw[:, :], router_w),
                       (rb[:, :], router_b)]
            sp.dma_start(xo[:, 0, :, :], xv[:, 0, :, :]).then_inc(s_x[0], 16)
            for dst, src in weights:
                sp.dma_start(dst, src).then_inc(s_w, 16)
            sp.dma_start(xo[:, 1, :, :], xv[:, 1, :, :]).then_inc(s_x[1], 16)
            for t in range(2, TAUS):
                sp.dma_start(xo[:, t, :, :], xv[:, t, :, :]).then_inc(s_x[2], 16)
            for dst, src in [(w_in[:, :], cheb_w), (w_out[:, :], cheb_out_w), (tri_sb[:, :], tri), (desc_sb[:, :], descend),
                             (w1_sb[:, :, :], w1), (b1_sb[:, :, :], b1), (w2_sb[:, :, :, :], w2), (b2_sb[:, :], b2),
                             (lnw_sb[:, :], ln_w), (lnb_sb[:, :], ln_b)]:
                sp.dma_start(dst, src).then_inc(s_w2, 16)

            def move(n):
                for b in range(B):
                    CL.wait(sp, n, b + 1)
                    CA.wait(sp, n, b + 1)
                    sp.dma_start(carry[0:1, b, :], last_sb[P - 1:P, b % 2, :]).then_inc(s_carry[b], 16)
                F2.wait(sp, n)
                sp.dma_start(out.rearrange("b (t p) c -> p t b c", p=P)[:, n.t, :, :], res[:, :, :]).then_inc(s_out, 16)

            rounds(sp, move)
            sp.wait_ge(s_out, 16 * TAUS)

        @block.gpsimd
        def _(pool):
            pool.wait_ge(s_zero, 5)
            pool.dma_start(eye16_sb[:, :], eye).then_inc(s_win, 16)
            pool.dma_start(eyeb_sb[:, :], eye).then_inc(s_win, 16)
            pool.dma_start(winm_sb[:, :, :], win_max).then_inc(s_win, 16)
            pool.dma_start(pair_sb[:, :, :], pair_sel).then_inc(s_win, 16)
            for b in range(4):
                pool.dma_start(mm_sb[0:W, b, :], win_exp).then_inc(s_win, 16)

            def step(n):
                if n.exists:
                    ST.wait(pool, n)
                    turn(pool, s_turn_pool)
                    nc.gpsimd.tensor_scalar(rstd[:, n.batch, 0:1], mv[:, n.batch, 1:2], EPS0, None, ALU.add).then_inc(R0.sem, 1)
                    R0.wait(pool, n, 1)
                    nc.gpsimd.tensor_tensor(rstd[:, n.batch, 1:2], rstd[:, n.batch, 0:1], half_sb[:, 0:1], ALU.pow).then_inc(R0.sem, 1)
                    PV.wait(pool, n.before(4))
                    VB.wait(pool, n.before(4))
                    turn(pool, s_turn_pool)
                    nc.gpsimd.tensor_copy(vd[:, n.batch, 0, :, :], vd[:, n.batch, 2, :, :]).then_inc(VP.sem, 1)
                l1 = n.before(3)
                l4 = n.before(4)
                if l4.exists:
                    XN1.wait(pool, l4)
                    turn(pool, s_turn_pool)
                    nc.gpsimd.tensor_copy(xn1_all[:, l4.index, :].rearrange("p (a b) -> p a b", b=IL), xn1[:, l4.batch, :].rearrange("p (b a) -> p a b", b=IL)).then_inc(SX.sem, 1)
                    X1T.wait(pool, l4)
                    turn(pool, s_turn_pool)
                    nc.gpsimd.tensor_copy(xn1t_all[:, l4.index, :], xn1t[:, l4.batch, :]).then_inc(SX.sem, 1)
                if n.exists:
                    HI.wait(pool, n)
                    TQ.wait(pool, n.before(4))
                    turn(pool, s_turn_pool)
                    nc.gpsimd.tensor_copy(xs[:, n.batch, 0:H, 2, :], xs[:, n.batch, 0:H, 0, :]).then_inc(DUP.sem, 1)
                    turn(pool, s_turn_pool)
                    nc.gpsimd.tensor_copy(xs[:, n.batch, H:2 * H, 1, :], xs[:, n.batch, H:2 * H, 0, :]).then_inc(DUP.sem, 1)
                if l1.exists:
                    GT.wait(pool, l1, 10)
                    turn(pool, s_turn_pool)
                    nc.gpsimd.tensor_scalar(rstd1[:, l1.batch, 0:1], mv1[:, l1.batch, 1:2], 1.0 / C, EPS0, ALU.mult, ALU.add).then_inc(R1.sem, 1)
                    R1.wait(pool, l1, 1)
                    nc.gpsimd.tensor_tensor(rstd1[:, l1.batch, 1:2], rstd1[:, l1.batch, 0:1], half_sb[:, 0:1], ALU.pow).then_inc(R1.sem, 1)

            pipeline(pool, step, 5)

            def deviation(n):
                F1.wait(pool, n, 8)
                turn(pool, s_turn_pool)
                nc.gpsimd.tensor_tensor(rstd2[:, 0, :], mv2[:, :, 1], eps2_sb[:, :], ALU.add).then_inc(R2.sem, 1)
                R2.wait(pool, n, 1)
                nc.gpsimd.tensor_tensor(rstd2[:, 1, :], rstd2[:, 0, :], half_sb[:, 0:1].to_broadcast([P, B]), ALU.pow).then_inc(R2.sem, 1)

            def mix(n):
                CP.wait(pool, n.before(1))
                turn(pool, s_turn_pool)
                nc.gpsimd.tensor_copy(xg[:, :, :], xn1t_all[:, n.tiles, :]).then_inc(XG.sem, 1)
                CW.wait(pool, n.before(1), 1)
                AC.wait(pool, n.before(1))
                turn(pool, s_turn_pool)
                nc.gpsimd.tensor_copy(cwg[:, :, :], cw[:, n.tiles, :]).then_inc(XG.sem, 1)
                if not n.first:
                    deviation(n.before(1))
                for b in range(B):
                    C1.wait(pool, n, CHEB1 * (b + 1))
                    n.wait_dma(pool, s_carry[b])
                    nc.gpsimd.tensor_tensor(kv[0:1, b % 2, :], kv[0:1, b % 2, :], carry[0:1, b, :], ALU.add).then_inc(CA.sem, 1)

            pool.wait_ge(SX.sem, 2 * NT)
            pool.wait_ge(s_cw, ROUTE)
            rounds(pool, mix)
            deviation(Round(TAUS - 1))

        @block.scalar
        def _(act):
            def step(n):
                l2, l3, l4 = n.before(2), n.before(3), n.before(4)
                if l4.exists:
                    TX1.wait(act, l4)
                    LM.wait(act, l4.before(4))
                    SX.wait(act, l4.before(4))
                    nc.scalar.copy(xn1t[:, l4.batch, :], t_ps[:, 0, :]).then_inc(X1T.sem, 1)

                def exponentials(j):
                    SE.wait(act, l2, j + 1)
                    PV.wait(act, l2.before(1), j + 1)
                    nc.scalar.activation(pexp[:, j, :, :], e_ps[j % 2][:, :, :], ACT.Exp,
                                         scale=float(D) ** -0.5).then_inc(EX.sem, 1)

                if l2.exists:
                    exponentials(0)
                if n.exists:
                    TX.wait(act, n)
                    PR.wait(act, n.before(4))
                    nc.scalar.copy(xnt[:, n.batch, :], t_ps[:, 1, :]).then_inc(XT.sem, 1)
                if l2.exists:
                    exponentials(1)
                if l3.exists:
                    ZG.wait(act, l3)
                    GT.wait(act, l3.before(1), 1)
                    nc.scalar.activation(ez[:, :], z[:, l3.batch, :], ACT.Exp, scale=-1.0).then_inc(EZ.sem, 1)
                if n.exists:
                    ZG.wait(act, n)
                    VP.wait(act, n)
                    for blk in range(2):
                        for a in range(2):
                            src = p_ps[W * blk:W * blk + W, 2 * C:3 * C].rearrange("p (i a d) -> p i a d", a=2, d=D)
                            nc.scalar.copy(vd[W * a:W * a + W, n.batch, 1 + blk, :, 9 * a:9 * a + D],
                                           src[:, :, a, :]).then_inc(VB.sem, 1)
                    RP.wait(act, n, 4)
                    TQ.wait(act, n.before(4))
                    DUP.wait(act, n.before(4))
                    nc.scalar.copy(xs[:, n.batch, :, 0, :],
                                   rot[:, n.batch % 2, 0, :].rearrange("p (h d) -> p h d", d=D)).then_inc(HI.sem, 1)
                if l2.exists:
                    exponentials(2)
                    exponentials(3)
                if l3.exists:
                    T2.wait(act, l3)
                    OP.wait(act, l3.before(1))
                    nc.scalar.copy(ynt[:, :], t_ps[:, 3, :]).then_inc(Y2.sem, 1)
                if n.exists:
                    SE.wait(act, n.before(4))
                    QK.wait(act, n.before(4))
                    nc.scalar.copy(kt[:, n.batch, :, 0:W], kt[:, n.batch, :, P:W + P]).then_inc(QK.sem, 1) if not n.first else \
                        nc.scalar.copy(kt[:, n.batch, :, 0:W], kt[:, n.batch, :, 0:W]).then_inc(QK.sem, 1)
                    TQ.wait(act, n)
                    nc.scalar.copy(qt[:, n.batch, :, :], q_ps[:, 0:NG, :]).then_inc(QK.sem, 1)
                    QK.wait(act, n, 1)
                    nc.scalar.copy(kt[:, n.batch, :, W:W + P], q_ps[:, NG:2 * NG, :]).then_inc(QK.sem, 1)
                if l2.exists:
                    PV.wait(act, l2)
                    TY.wait(act, l2.before(1))
                    nc.scalar.copy(yts[:, :], y_ps[:, 0:2, :].rearrange("p a b -> p (a b)")).then_inc(YT.sem, 1)

            act.wait_ge(s_zero, 5)
            pipeline(act, step, 5)

            act.wait_ge(s_cw, 8)
            nc.scalar.activation(rs[:, 5, :], rs[:, 4, :], ACT.Exp).then_inc(s_we, 1)
            act.wait_ge(s_w2, 16 * 10)
            PV.wait(act, Tile(TAUS, 0))
            VP.wait(act, Tile(TAUS, 0))

            def oct_copy(n, b):
                OT.wait(act, n, b + 1)
                SO.wait(act, *n.at(b - 1, 4))
                nc.scalar.copy(oct_[:, :], t_ps[:, 0, :]).then_inc(OE.sem, 1)

            def s1_copy(n, b):
                SO.wait(act, n, b + 1)
                F1.wait(act, n.before(1))
                nc.scalar.copy(s1[:, b, :], t_ps[:, 1, :]).then_inc(SE1.sem, 1)

            def finish(n):
                oct_copy(n, B - 1)
                s1_copy(n, B - 1)

            def silu_exp(n):
                F1.wait(act, n, 14)
                nc.scalar.activation(e2[:, :, :], y2[:, :, :], ACT.Exp, scale=-1.0).then_inc(EX2.sem, 1)

            def mix(n):
                def gelus(e):
                    for f in range(FB):
                        UP.wait(act, n, e * FB + f + 1)
                        DN.wait(act, *n.at(e - 2, E))
                        nc.scalar.activation(hid[e % 2][:, f, :], u_ps[f % 2], ACT.Gelu,
                                             bias=b1_sb[:, e, f:f + 1]).then_inc(GE.sem, 1)

                def task(what, b):
                    if what == "CP":
                        CP.wait(act, n, b + 1)
                        C1.wait(act, *n.at(b - 2, 4, CHEB1))
                        nc.scalar.copy(vs[:, b % 2, :], p_ps[:, 2 * C:3 * C]).then_inc(VC.sem, 1)
                    if what == "CS":
                        CS.wait(act, n, b + 1)
                        n.wait_carry(act, s_carry, b - 2)
                        nc.scalar.copy(last_sb[96:P, b % 2, 0:3 * SW], cc_ps[0][96:P, 0:3 * SW])
                        nc.scalar.copy(last_sb[96:P, b % 2, 3 * SW:5 * SW], cc_ps[1][96:P, 0:2 * SW]).then_inc(CL.sem, 1)
                    if what == "OT":
                        oct_copy(n, b)
                    if what == "SO":
                        s1_copy(n, b)

                task("CP", 0)
                gelus(0)
                if not n.first:
                    finish(n.before(1))
                gelus(1)
                CW.wait(act, n, 1)
                CW.wait(act, n.before(1), 2)
                nc.scalar.copy(cwt[:, :, :], t_ps[0:E, :, :]).then_inc(CT.sem, 1)
                if not n.first:
                    silu_exp(n.before(1))
                for e in range(E):
                    if 0 < e < E - 1:
                        gelus(e + 1)
                    for what, b in SLOTS[e]:
                        task(what, b)

            rounds(act, mix)
            finish(Round(TAUS - 1))
            silu_exp(Round(TAUS - 1))

        @block.tensor
        def _(pe):
            pe.wait_ge(s_init, 1)
            pe.wait_ge(s_zero, 5)
            nc.tensor.matmul(t_ps[:, 0, 0:1], ones_sb[:, :], wsum[:, 0:1], start=True, stop=True).then_inc(s_ps, 1)
            pe.wait_ge(s_init, 5)
            pe.wait_ge(s_w, 16 * 9)
            pe.wait_ge(s_win, 16 * 8)

            def max_scores(n, j):
                c, jp = j // 2, j % 2
                ps = m_ps[j % 2]
                QK.wait(pe, n)
                RED.wait(pe, n.before(1), 3 + j) if j < 2 else RED.wait(pe, n, j - 1)
                nc.tensor.matmul(ps[:, :, :], eyeb_sb[:, :], winm_sb[:, :, :], start=True, stop=True)
                lo = W if n.first and c == 0 else 0
                if lo:
                    nc.tensor.matmul(ps[:, :, 0:W], eyeb_sb[:, :], hide_sb[:, :, :], start=False, stop=True, skip_group_check=True)
                for g in range(NG):
                    for a in range(2):
                        r = 32 * (2 * jp + a)
                        last = nc.tensor.matmul(ps[W * a:W * a + W, g, lo:P],
                                                qt[r:r + 32, n.batch, g, c * W:c * W + W],
                                                kt[r:r + 32, n.batch, g, c * W + lo:c * W + P],
                                                start=False, stop=True, skip_group_check=True)
                last.then_inc(MX.sem, 1)

            def scores(n, j):
                jp, gg = j // 2, j % 2
                ps = e_ps[j % 2]
                MMR.wait(pe, n)
                EX.wait(pe, n.before(1), 3 + j) if j < 2 else EX.wait(pe, n, j - 1)
                for i in range(2):
                    g = 2 * gg + i
                    nc.tensor.matmul(ps[:, i, :], pair_sb[:, jp * NG + g, :], mm_sb[:, n.batch, :],
                                     start=True, stop=True, skip_group_check=True)
                    if n.first:
                        nc.tensor.matmul(ps[:, i, P:P + W], eyeb_sb[:, :], hide_sb[:, 0, :], start=False, stop=True, skip_group_check=True)
                    for a in range(2):
                        r = 32 * (2 * jp + a)
                        o = ps[W * a:W * a + W, i, :]
                        q, k = qt[r:r + 32, n.batch, g, :], kt[r:r + 32, n.batch, g, :]
                        nc.tensor.matmul(o[:, 0:P], k[:, W:2 * W], q[:, 0:P], start=False, stop=True, skip_group_check=True)
                        if not n.first:
                            nc.tensor.matmul(o[:, P:P + W], k[:, 0:W], q[:, 0:W], start=False, stop=True, skip_group_check=True)
                        last = nc.tensor.matmul(o[:, P + W:2 * P], k[:, 2 * W:3 * W], q[:, W:P], start=False, stop=True, skip_group_check=True)
                last.then_inc(SE.sem, 1)

            def weigh(n, j):
                jp, gg = j // 2, j % 2
                EX.wait(pe, n, j + 1)
                VB.wait(pe, n)
                YT.wait(pe, n.before(1))
                for part in range(3):
                    for i in range(2):
                        g = 2 * gg + i
                        o = y_ps[VW * g:VW * g + VW, jp, :]
                        v = vd[:, n.batch, :, jp * NG + g, :]
                        w = pexp[:, j, i, :]
                        if part == 0:
                            nc.tensor.matmul(o, v[:, 1, :], w[:, 0:P], start=True, stop=True, skip_group_check=True)
                        elif part == 1:
                            if not n.first:
                                nc.tensor.matmul(o[:, 0:W], v[:, 0, :], w[:, P:P + W], start=False, stop=True, skip_group_check=True)
                        else:
                            last = nc.tensor.matmul(o[:, W:P], v[:, 2, :], w[:, P + W:2 * P], start=False, stop=True, skip_group_check=True)
                last.then_inc(PV.sem, 1)

            def step(n):
                l1, l2, l3, l4 = (n.before(i) for i in (1, 2, 3, 4))
                if l4.exists:
                    XN1.wait(pe, l4)
                    LG.wait(pe, l4.before(1))
                    nc.tensor.transpose(t_ps[:, 0, :], xn1[:, l4.batch, :], eye_sb[:, :]).then_inc(TX1.sem, 1)
                if l1.exists:
                    max_scores(l1, 0)
                    max_scores(l1, 1)
                if l2.exists:
                    scores(l2, 0)
                if n.exists:
                    XN.wait(pe, n)
                    X1T.wait(pe, l4)
                    nc.tensor.transpose(t_ps[:, 1, :], xn[:, n.batch, :], eye_sb[:, :]).then_inc(TX.sem, 1)
                if l2.exists:
                    scores(l2, 1)
                if n.exists:
                    XT.wait(pe, n)
                    GT.wait(pe, l4, 4)
                    nc.tensor.matmul(p_ps[:, :], xnt[:, n.batch, :], wp[:, :], start=True, stop=True).then_inc(PR.sem, 1)
                if l3.exists:
                    YT.wait(pe, l3)
                    XT.wait(pe, n)
                    if not n.exists:
                        X1T.wait(pe, l4)
                    nc.tensor.transpose(t_ps[:, 2, :], yts[:, 0:P], eye_sb[:, :])
                    nc.tensor.transpose(t_ps[:, 3, :], yts[:, P:2 * P], eye_sb[:, :]).then_inc(TY.sem, 1)
                if l1.exists:
                    max_scores(l1, 2)
                    max_scores(l1, 3)
                if l2.exists:
                    weigh(l2, 0)
                    scores(l2, 2)
                    weigh(l2, 1)
                    scores(l2, 3)
                if l1.exists:
                    RED.wait(pe, l1)
                    YN.wait(pe, l3)
                    XT.wait(pe, n)
                    for c in range(2):
                        last = nc.tensor.transpose(tb_ps[0:NPAIR, c * P:c * P + P], mneg[:, l1.batch, c, :], eyeb_sb[:, :])
                    last.then_inc(TM.sem, 1)
                if l3.exists:
                    YN.wait(pe, l3)
                    MMR.wait(pe, l1)
                    if not l1.exists:
                        X1T.wait(pe, l4)
                    nc.tensor.transpose(t_ps[:, 3, :], yn[:, :], eye_sb[:, :]).then_inc(T2.sem, 1)
                if l2.exists:
                    weigh(l2, 2)
                    weigh(l2, 3)
                if l3.exists:
                    Y2.wait(pe, l3)
                    RP.wait(pe, n, 3)
                    VB.wait(pe, n)
                    ZG.wait(pe, n)
                    nc.tensor.matmul(p_ps[:, 0:C], ynt[:, :], wo[:, :], start=True, stop=True).then_inc(OP.sem, 1)
                if n.exists:
                    RP.wait(pe, n)
                    DUP.wait(pe, n)
                    HI.wait(pe, n)
                    QK.wait(pe, l1)
                    for i in range(2 * NG):
                        last = nc.tensor.transpose(q_ps[:, i, :], xs[:, n.batch, 4 * i:4 * i + 4, :, :].rearrange("p h s d -> p (h s d)"),
                                                   eye16_sb[:, :])
                    last.then_inc(TQ.sem, 1)
                if l4.exists:
                    X1T.wait(pe, l4)
                    Y2.wait(pe, l3)
                    nc.tensor.matmul(t_ps[:, 0, 0:8], xn1t[:, l4.batch, :], rw[:, :], start=True, stop=True).then_inc(LM.sem, 1)

            pipeline(pe, step, 5)

            def transpose_out(n, b):
                C2.wait(pe, n, CHEB2 * (b + 1))
                SE1.wait(pe, *n.at(b - 1, 4))
                AC.wait(pe, n, 1)
                nc.tensor.transpose(t_ps[:, 0, :], oc[:, :], eye_sb[:, :]).then_inc(OT.sem, 1)

            def project_out(n, b):
                OE.wait(pe, n, b + 1)
                nc.tensor.matmul(t_ps[:, 1, :], oct_[:, :], w_out[:, :], start=True, stop=True).then_inc(SO.sem, 1)

            def finish(n):
                transpose_out(n, B - 1)
                project_out(n, B - 1)

            def mix(n):
                def up(e):
                    for f in range(FB):
                        GE.wait(pe, *n.at(e * FB + f - 2, E * FB))
                        nc.tensor.matmul(u_ps[f % 2], w1_sb[:, e, f * P:f * P + P], xn1t_all[:, n.tiles, :],
                                         start=True, stop=True).then_inc(UP.sem, 1)

                def down(e):
                    GE.wait(pe, n, e * FB + FB)
                    AC.wait(pe, *n.at_acc(e - 2))
                    for b in range(B):
                        for f in range(FB):
                            last = nc.tensor.matmul(d_ps[e % 2][:, b, :], hid[e % 2][:, f, b * P:b * P + P], w2_sb[:, e, f, :],
                                                    start=f == 0, stop=f == FB - 1)
                    last.then_inc(DN.sem, 1)

                def task(what, b):
                    if what == "CP":
                        VC.wait(pe, *n.at(b - 1, 4))
                        C1.wait(pe, n if b else n.before(1), CHEB1 * ((b - 1) % B) + 1)
                        nc.tensor.matmul(p_ps[:, 0:3 * C], xg[:, b, :], w_in[:, :], start=True, stop=True).then_inc(CP.sem, 1)
                    if what == "CS":
                        C1.wait(pe, n, CHEB1 * (b + 1))
                        C2.wait(pe, *n.at(b - 1, 4, CHEB2))
                        CL.wait(pe, *n.at(b - 1, 4))
                        CA.wait(pe, n, b + 1)
                        nc.tensor.matmul(cc_ps[0][:, 0:3 * SW], tri_sb[:, :], kv[:, b % 2, 0:3 * SW], start=True, stop=True)
                        nc.tensor.matmul(cc_ps[1][:, 0:2 * SW], tri_sb[:, :], kv[:, b % 2, 3 * SW:5 * SW], start=True, stop=True).then_inc(CS.sem, 1)
                    if what == "OT":
                        transpose_out(n, b)
                    if what == "SO":
                        project_out(n, b)

                XG.wait(pe, n, 1)
                task("CP", 0)
                up(0)
                if not n.first:
                    finish(n.before(1))
                XG.wait(pe, n)
                up(1)
                SE1.wait(pe, n.before(1))
                for b in range(B):
                    last = nc.tensor.transpose(t_ps[0:E, b, :], cwg[:, b, :], eye_sb[:, :])
                last.then_inc(CW.sem, 1)
                down(0)
                CT.wait(pe, n)
                for b in range(B):
                    last = nc.tensor.matmul(t_ps[:, b, :], cwt[:, b, :], b2_sb[:, :], start=True, stop=True)
                last.then_inc(CW.sem, 1)
                for e in range(E):
                    if e > 0:
                        if e + 1 < E:
                            up(e + 1)
                        down(e)
                    for what, b in SLOTS[e]:
                        task(what, b)

            pe.wait_ge(s_w2, 16 * 10)
            LG.wait(pe, Tile(TAUS, 0))
            rounds(pe, mix)
            finish(Round(TAUS - 1))

        @block.vector
        def _(dve):
            nc.vector.memset(ones_sb[:, :], 1.0).then_inc(s_zero, 1)
            nc.vector.memset(half_sb[:, :], -0.5)
            nc.vector.memset(carry[:, :, :], 0.0)
            nc.vector.memset(xs[:, :, :, :, :], 0.0)
            nc.vector.memset(kt[:, :, :, :], 0.0)
            nc.vector.memset(mm_sb[:, :, :], 0.0).then_inc(s_zero, 1)
            nc.vector.memset(hide_sb[:, :, :], NEG).then_inc(s_zero, 1)
            nc.vector.memset(vd[:, :, :, :, :], 0.0).then_inc(s_zero, 1)
            dve.wait_ge(s_zero, 4)
            nc.vector.memset(vd[0:W, :, :, :, 8:9], 1.0)
            nc.vector.memset(vd[W:P, :, :, :, 17:18], 1.0).then_inc(s_zero, 1)
            dve.wait_ge(s_w, 16 * 9)
            nc.vector.tensor_reduce(wsum[:, 0:1], wraw[:, :], AX.X, ALU.add, apply_absolute_value=True).then_inc(s_init, 1)
            dve.wait_ge(s_ps, 1)
            nc.vector.tensor_scalar(wsum[:, 1:2], t_ps[:, 0, 0:1], 1.0 / (C * C), 0.7, ALU.mult, ALU.mult).then_inc(s_init, 1)
            dve.wait_ge(s_init, 2)
            nc.vector.tensor_scalar(wneg[:, :], wraw[:, :], -1.0, wsum[:, 1:2], ALU.mult, ALU.is_gt).then_inc(s_init, 1)
            dve.wait_ge(s_init, 3)
            nc.vector.scalar_tensor_tensor(wneg[:, :], wraw[:, :], wsum[:, 1:2], wneg[:, :], ALU.is_gt, ALU.subtract).then_inc(s_init, 1)
            dve.wait_ge(s_init, 4)
            nc.vector.tensor_scalar(wp[:, 3 * C:4 * C], wneg[:, :], alpha_sb[:, 0:1], None, ALU.mult).then_inc(s_init, 1)

            def maxima(n, j):
                MX.wait(dve, n, j + 1)
                TM.wait(dve, n.before(4))
                nc.vector.tensor_reduce(mneg[:, n.batch, j // 2, (j % 2) * NG:(j % 2) * NG + NG], m_ps[j % 2][:, :, :],
                                        AX.X, ALU.max, negate=True).then_inc(RED.sem, 1)

            def step(n):
                l1, l3, l4, l5 = (n.before(i) for i in (1, 3, 4, 5))
                if n.exists:
                    if n.static and n.batch == 0:
                        dve.wait_ge(s_x[n.tau], 16)
                    turn(dve, s_turn_dve)
                    nc.vector.bn_stats(stats[:, n.batch, :], x_all[:, n.index, :]).then_inc(ST.sem, 1)
                    ST.wait(dve, n, 1)
                    R0.wait(dve, n.before(4), 1)
                    turn(dve, s_turn_dve)
                    nc.vector.bn_aggr(mv[:, n.batch, :], stats[:, n.batch, :]).then_inc(ST.sem, 1)
                if l5.exists:
                    LM.wait(dve, l5)
                    nc.vector.tensor_tensor(logits[:, l5.index, :], t_ps[:, 0, 0:8], rb[:, :], ALU.add).then_inc(LG.sem, 1)
                if l4.exists:
                    R1.wait(dve, l4)
                    SX.wait(dve, l4.before(4))
                    TX1.wait(dve, l4.before(4))
                    nc.vector.tensor_scalar(xn1[:, l4.batch, :], xn1[:, l4.batch, :], rstd1[:, l4.batch, 1:2], None,
                                            ALU.mult).then_inc(XN1.sem, 1)
                if l1.exists:
                    maxima(l1, 0)
                    maxima(l1, 1)
                if n.exists:
                    R0.wait(dve, n)
                    TX.wait(dve, n.before(4))
                    nc.vector.tensor_scalar(xn[:, n.batch, :], x_all[:, n.index, :], mv[:, n.batch, 0:1], rstd[:, n.batch, 1:2],
                                            ALU.subtract, ALU.mult).then_inc(XN.sem, 1)
                if l3.exists:
                    TY.wait(dve, l3)
                    T2.wait(dve, l3.before(1))
                    yv = t_ps[:, 2:4, :].rearrange("p j (g w) -> p (j g) w", w=VW)[:, :, 0:18].rearrange("p i (a e) -> p i a e", a=2)
                    nc.vector.reciprocal(rden[:, :].rearrange("p (i a) -> p i a", a=2), yv[:, :, :, 8]).then_inc(YN.sem, 1)
                    YN.wait(dve, l3, 1)
                    nc.vector.tensor_tensor(yn[:, :].rearrange("p (i a d) -> p i a d", a=2, d=D), yv[:, :, :, 0:8],
                                            rden[:, :].rearrange("p (i a) -> p i a", a=2).unsqueeze(3).to_broadcast([P, NPAIR, 2, D]),
                                            ALU.mult).then_inc(YN.sem, 1)
                if l1.exists:
                    maxima(l1, 2)
                    maxima(l1, 3)
                if l3.exists:
                    EZ.wait(dve, l3)
                    nc.vector.tensor_scalar(gd[:, 0, :], ez[:, :], 1.0, None, ALU.add).then_inc(GT.sem, 1)
                    GT.wait(dve, l3, 1)
                    nc.vector.reciprocal(gd[:, 1, :], gd[:, 0, :]).then_inc(GT.sem, 1)
                    GT.wait(dve, l3, 2)
                    nc.vector.tensor_tensor(gd[:, 2, :], z[:, l3.batch, :], gd[:, 1, :], ALU.mult).then_inc(GT.sem, 1)
                if n.exists:
                    PR.wait(dve, n)
                    r = n.batch % 2
                    qk = p_ps[:, 0:2 * C].rearrange("p (h e f) -> p h e f", e=2, f=D // 2)
                    ra = rot[:, r, 0, :].rearrange("p (h d) -> p h d", d=D)
                    rbt = rot[:, r, 1, :].rearrange("p (h e f) -> p h e f", e=2, f=D // 2)
                    cos = rope_sb[:, n.tau, 0:D].unsqueeze(1).to_broadcast([P, 2 * H, D])
                    HI.wait(dve, n.before(2))
                    nc.vector.tensor_tensor(ra, p_ps[:, 0:2 * C].rearrange("p (h d) -> p h d", d=D), cos, ALU.mult).then_inc(RP.sem, 1)
                    for e in range(2):
                        sin = rope_sb[:, n.tau, D + 4 * e:D + 4 * e + 4].unsqueeze(1).to_broadcast([P, 2 * H, D // 2])
                        nc.vector.tensor_tensor(rbt[:, :, e, :], qk[:, :, 1 - e, :], sin, ALU.mult).then_inc(RP.sem, 1)
                    GT.wait(dve, n.before(4), 3)
                    nc.vector.tensor_tensor(z[:, n.batch, :], p_ps[:, 3 * C:4 * C], bias0_sb[:, :], ALU.add).then_inc(ZG.sem, 1)
                    RP.wait(dve, n, 3)
                    nc.vector.tensor_tensor(rot[:, r, 0, :], rot[:, r, 0, :], rot[:, r, 1, :], ALU.add).then_inc(RP.sem, 1)
                if l1.exists:
                    TM.wait(dve, l1)
                    SE.wait(dve, l1.before(4))
                    if l1.static:
                        dve.wait_ge(s_win, 16 * 8)
                    mt = tb_ps[0:NPAIR, 0:2 * P].rearrange("p (c a q) -> p a c q", c=2, a=2)
                    for a in range(2):
                        nc.vector.tensor_copy(mm_sb[W + 32 * a:W + 32 * a + NPAIR, l1.batch, :].rearrange("p (r c q) -> p r c q", r=2, c=2),
                                              mt[:, a, :, :].unsqueeze(1).to_broadcast([NPAIR, 2, 2, W])).then_inc(MMR.sem, 1)
                if n.exists:
                    RP.wait(dve, n, 4)
                    HI.wait(dve, n)
                    rv = rot[:, r, 0, :].rearrange("p (h d) -> p h d", d=D)
                    nc.vector.tensor_tensor(xs[:, n.batch, 0:H, 1, :], rv[:, 0:H, :], xs[:, n.batch, 0:H, 0, :], ALU.subtract).then_inc(RP.sem, 1)
                    nc.vector.tensor_tensor(xs[:, n.batch, H:2 * H, 2, :], rv[:, H:2 * H, :], xs[:, n.batch, H:2 * H, 0, :], ALU.subtract).then_inc(RP.sem, 1)
                if l3.exists:
                    OP.wait(dve, l3)
                    GT.wait(dve, l3, 3)
                    nc.vector.tensor_tensor(sg[:, :], p_ps[:, 0:C], gd[:, 2, :], ALU.mult).then_inc(GT.sem, 1)
                    GT.wait(dve, l3, 4)
                    nc.vector.tensor_tensor(x_all[:, l3.index, :], x_all[:, l3.index, :], sg[:, :], ALU.add).then_inc(GT.sem, 1)
                    GT.wait(dve, l3, 5)
                    turn(dve, s_turn_dve)
                    nc.vector.bn_stats(stats1[:, l3.batch, :], x_all[:, l3.index, :]).then_inc(GT.sem, 1)
                    GT.wait(dve, l3, 6)
                    turn(dve, s_turn_dve)
                    nc.vector.bn_aggr(mv1[:, l3.batch, :], stats1[:, l3.batch, :]).then_inc(GT.sem, 1)
                    GT.wait(dve, l3, 7)
                    SX.wait(dve, l3.before(4))
                    TX1.wait(dve, l3.before(4))
                    nc.vector.tensor_scalar(xn1[:, l3.batch, :].rearrange("p (b a) -> p a b", b=IL), x_all[:, l3.index, :].rearrange("p (a b) -> p a b", b=IL), mv1[:, l3.batch, 0:1], None, ALU.subtract).then_inc(GT.sem, 1)
                    GT.wait(dve, l3, 8)
                    nc.vector.tensor_tensor(sg[:, :], xn1[:, l3.batch, :], xn1[:, l3.batch, :], ALU.mult).then_inc(GT.sem, 1)
                    GT.wait(dve, l3, 9)
                    nc.vector.tensor_reduce(mv1[:, l3.batch, 1:2], sg[:, :], AX.X, ALU.add).then_inc(GT.sem, 1)

            for n in range(8):
                step(Tile(0, n))
            dve.wait_ge(s_x[2], 16 * (TAUS - 2))
            with dve.Fori(2, TAUS) as t:
                for k in range(4):
                    step(Tile(t, k))
            for n in range(5):
                step(Tile(TAUS, n))

            route = [0]

            def link(ins):
                route[0] += 1
                ins.then_inc(s_cw, 1)
                dve.wait_ge(s_cw, route[0])

            def wide(ap):
                return ap.unsqueeze(2).to_broadcast([P, NT, E])

            LG.wait(dve, Tile(TAUS, 0))
            dve.wait_ge(s_w2, 16 * 10)
            left = logits[:, :, :]
            for k in range(2):
                link(nc.vector.tensor_reduce(rs[:, 2 * k, :], left, AX.X, ALU.max))
                link(nc.vector.tensor_tensor(rt[:, 0, :, :], left, wide(rs[:, 2 * k, :]), ALU.is_equal))
                link(nc.vector.tensor_tensor(rt[:, 1, :, :], rt[:, 0, :, :], desc_sb[:, :].unsqueeze(1).to_broadcast([P, NT, E]), ALU.mult))
                link(nc.vector.tensor_reduce(rs[:, 1, :], rt[:, 1, :, :], AX.X, ALU.max))
                link(nc.vector.tensor_tensor(rt[:, 2 + k, :, :], rt[:, 1, :, :], wide(rs[:, 1, :]), ALU.is_equal))
                if k == 0:
                    link(nc.vector.scalar_tensor_tensor(rt[:, 4, :, :], rt[:, 2, :, :], -3e38, logits[:, :, :], ALU.mult, ALU.add))
                    left = rt[:, 4, :, :]
                    link(nc.vector.tensor_reduce(rs[:, 3, :], left, AX.X, ALU.max))
                    link(nc.vector.tensor_tensor(rs[:, 4, :], rs[:, 3, :], rs[:, 0, :], ALU.subtract))
            dve.wait_ge(s_we, 1)
            link(nc.vector.tensor_scalar(rs[:, 6, :], rs[:, 5, :], 1.0, None, ALU.add))
            link(nc.vector.reciprocal(rs[:, 7, :], rs[:, 6, :]))
            link(nc.vector.tensor_tensor(rs[:, 6, :], rs[:, 5, :], rs[:, 7, :], ALU.mult))
            link(nc.vector.tensor_tensor(rt[:, 2, :, :], rt[:, 2, :, :], wide(rs[:, 7, :]), ALU.mult))
            link(nc.vector.tensor_tensor(rt[:, 3, :, :], rt[:, 3, :, :], wide(rs[:, 6, :]), ALU.mult))
            link(nc.vector.tensor_tensor(cw[:, :, :], rt[:, 2, :, :], rt[:, 3, :, :], ALU.add))
            link(nc.vector.memset(eps2_sb[:, :], 1e-12))
            assert route[0] == ROUTE

            def final_step(n, at, ins, wait=True):
                ins.then_inc(F1.sem, 1)
                if wait:
                    F1.wait(dve, n, at)

            def normalise(n):
                AC.wait(dve, n)
                for b in range(B):
                    final_step(n, b + 1, nc.vector.bn_stats(stats2[:, b, :], acc[:, b, :]), b == B - 1)
                for b in range(B):
                    turn(dve, s_turn_dve)
                    final_step(n, B + b + 1, nc.vector.bn_aggr(mv2[:, b, :], stats2[:, b, :]), False)
                R2.wait(dve, n)
                for b in range(B):
                    final_step(n, 2 * B + b + 1, nc.vector.tensor_scalar(y2[:, b, :], acc[:, b, :], mv2[:, b, 0:1], rstd2[:, 1, b:b + 1],
                                                                         ALU.subtract, ALU.mult), b == B - 1)
                final_step(n, 13, nc.vector.tensor_tensor(y2[:, :, :], y2[:, :, :], lnw_sb[:, :].unsqueeze(1).to_broadcast([P, B, C]), ALU.mult))
                final_step(n, 14, nc.vector.tensor_tensor(y2[:, :, :], y2[:, :, :], lnb_sb[:, :].unsqueeze(1).to_broadcast([P, B, C]), ALU.add))

            def gate(n):
                EX2.wait(dve, n)
                final_step(n, 15, nc.vector.tensor_scalar(e2[:, :, :], e2[:, :, :], 1.0, None, ALU.add))
                final_step(n, 16, nc.vector.reciprocal(e2[:, :, :], e2[:, :, :]))
                final_step(n, 17, nc.vector.tensor_tensor(y2[:, :, :], y2[:, :, :], e2[:, :, :], ALU.mult))
                SE1.wait(dve, n)
                final_step(n, 18, nc.vector.tensor_tensor(y2[:, :, :], y2[:, :, :], s1[:, :, :], ALU.mult))
                n.wait_dma(dve, s_out)
                nc.vector.tensor_tensor(res[:, :, :], y2[:, :, :], x_all[:, n.tiles, :], ALU.add).then_inc(F2.sem, 1)

            def mix(n):
                def cheb_keys(b):
                    at = [CHEB1 * b]

                    def done(ins, wait=True):
                        at[0] += 1
                        ins.then_inc(C1.sem, 1)
                        if wait:
                            C1.wait(dve, n, at[0])

                    VC.wait(dve, n, b + 1)
                    x = tc[:, 0, :]
                    done(nc.vector.tensor_scalar(xc[:, :], p_ps[:, 0:2 * C], INV, CLIP, ALU.mult, ALU.min))
                    done(nc.vector.tensor_scalar(x, xc[:, :], -CLIP, None, ALU.max))
                    done(nc.vector.scalar_tensor_tensor(xc[:, :], x, 2.0, x, ALU.mult, ALU.mult))
                    done(nc.vector.tensor_scalar(tc[:, 1, :], xc[:, :], 1.0, None, ALU.subtract))
                    for j in range(2, ORD):
                        done(nc.vector.scalar_tensor_tensor(xc[:, :], x, 2.0, tc[:, j - 1, :], ALU.mult, ALU.mult))
                        done(nc.vector.tensor_tensor(tc[:, j, :], xc[:, :], tc[:, j - 2, :], ALU.subtract))
                    CS.wait(dve, *n.at(b - 2, 4))
                    kvb = kv[:, b % 2, :].rearrange("p (j w) -> p j w", w=SW)
                    done(nc.vector.tensor_tensor(kvb[:, :, 0:C], tc[:, :, C:2 * C], vs[:, b % 2, :].unsqueeze(1).to_broadcast([P, ORD, C]), ALU.mult), False)
                    done(nc.vector.tensor_reduce(kvb[:, :, C:SW], tc[:, :, C:2 * C].rearrange("p j (h d) -> p j h d", d=D), AX.X, ALU.add), False)
                    done(nc.vector.tensor_reduce(tq[:, :, C:SW], tc[:, :, 0:C].rearrange("p j (h d) -> p j h d", d=D), AX.X, ALU.add))
                    assert at[0] == CHEB1 * (b + 1)

                def cheb_out(b):
                    at = [CHEB2 * b]

                    def done(ins, wait=True):
                        at[0] += 1
                        ins.then_inc(C2.sem, 1)
                        if wait:
                            C2.wait(dve, n, at[0])

                    CS.wait(dve, n, b + 1)
                    CL.wait(dve, n, b + 1)
                    c0 = cc_ps[0][:, 0:3 * SW].rearrange("p (j w) -> p j w", w=SW)
                    c1 = cc_ps[1][:, 0:2 * SW].rearrange("p (j w) -> p j w", w=SW)
                    done(nc.vector.tensor_tensor(pr[:, 0:3, 0:C], tc[:, 0:3, 0:C], c0[:, :, 0:C], ALU.mult), False)
                    done(nc.vector.tensor_tensor(pr[:, 0:3, C:SW], tq[:, 0:3, C:SW], c0[:, :, C:SW], ALU.mult), False)
                    done(nc.vector.tensor_tensor(pr[:, 3:5, 0:C], tc[:, 3:5, 0:C], c1[:, :, 0:C], ALU.mult), False)
                    done(nc.vector.tensor_tensor(pr[:, 3:5, C:SW], tq[:, 3:5, C:SW], c1[:, :, C:SW], ALU.mult))
                    done(nc.vector.tensor_scalar(nd[:, :], pr[:, 0, :], BETA[0], None, ALU.mult))
                    for j in range(1, ORD):
                        done(nc.vector.scalar_tensor_tensor(nd[:, :], pr[:, j, :], BETA[j], nd[:, :], ALU.mult, ALU.add))
                    done(nc.vector.tensor_scalar(dn[:, 0, :], nd[:, C:SW], 1e-7, None, ALU.add))
                    done(nc.vector.reciprocal(dn[:, 1, :], dn[:, 0, :]))
                    OT.wait(dve, *n.at(b - 1, 4))
                    done(nc.vector.tensor_tensor(oc[:, :].rearrange("p (h d) -> p h d", d=D), nd[:, 0:C].rearrange("p (h d) -> p h d", d=D),
                                                 dn[:, 1, :].unsqueeze(2).to_broadcast([P, H, D]), ALU.mult))
                    assert at[0] == CHEB2 * (b + 1)

                def accumulate(e):
                    DN.wait(dve, n, e + 1)
                    for b in range(B):
                        AC.wait(dve, n, 1 if e == 0 else 1 + 4 * (e - 1) + b + 1)
                        nc.vector.scalar_tensor_tensor(acc[:, b, :], d_ps[e % 2][:, b, :], cwg[:, b, e:e + 1], acc[:, b, :],
                                                       ALU.mult, ALU.add).then_inc(AC.sem, 1)

                def residual():
                    CW.wait(dve, n, 2)
                    F1.wait(dve, n.before(1), 12)
                    nc.vector.tensor_tensor(acc[:, :, :], xn1_all[:, n.tiles, :], t_ps[:, :, :], ALU.add).then_inc(AC.sem, 1)

                for what, i in DVE_ORDER:
                    if what == "keys":
                        cheb_keys(i)
                    elif what == "residual":
                        residual()
                    elif what == "sum":
                        accumulate(i)
                    elif what == "out":
                        cheb_out(i)
                    elif what == "gate" and not n.first:
                        gate(n.before(1))
                normalise(n)

            rounds(dve, mix)
            gate(Round(TAUS - 1))


def constants():
    import numpy as np
    inv = (1.0 / np.float32(10000.0) ** (np.arange(0, D, 2, dtype=np.float32) / np.float32(D))).astype(np.float32)
    ang = np.outer(np.arange(T, dtype=np.float32), inv).astype(np.float32)
    cos, sin = np.cos(ang), np.sin(ang)
    rope = np.concatenate([cos, cos, sin, -sin], 1).astype(np.float32).reshape(TAUS, P, 2 * D).transpose(1, 0, 2)
    q, k = np.arange(W)[:, None], np.arange(W)[None, :]
    before, own = np.where(k >= q, 0, NEG), np.where(k <= q, 0, NEG)
    win_max = np.tile(np.concatenate([before, own], 1)[:, None, :], (2, NG, 1))
    win_exp = np.concatenate([own.T, before.T, before.T, own.T], 1)
    sel = np.zeros((P, NPAIR, P))
    for r in range(W):
        sel[r, :, r] = sel[r, :, W + r] = 1
    for i in range(NPAIR):
        sel[W + i, i, 0:W] = sel[W + 32 + i, i, W:P] = 1
    f = np.float32
    return {"rope": np.ascontiguousarray(rope), "eye": np.eye(P, dtype=f), "win_max": win_max.astype(f),
            "win_exp": win_exp.astype(f), "pair_sel": sel.astype(f),
            "tri": np.triu(np.ones((P, P), f)), "descend": np.tile(np.arange(E, 0, -1).astype(f), (P, 1))}


def kernel(L0_attn_x, L0_attn_w_attn, L0_attn_w_proj, L0_ffn_weight, L0_ffn_alpha, L0_ffn_bias, L1_attn_W_in,
           L1_attn_W_out, L1_ffn_router_w, L1_ffn_router_b, L1_ffn_w1, L1_ffn_b1, L1_ffn_w2, L1_ffn_b2, L1_ffn_ln_w,
           L1_ffn_ln_b):
    import numpy as np
    import concourse.bacc as bacc
    from concourse.bass_utils import run_bass_kernel_spmd

    order = [(4 * g + 2 * jp + a) * D + d for jp in range(2) for g in range(NG) for a in range(2) for d in range(D)]
    w_attn = np.asarray(L0_attn_w_attn)

    runs = np.arange(C).reshape(-1, IL).T.reshape(-1)

    def rows(a):
        return np.tile(np.asarray(a)[None, :], (P, 1))

    arrays = {
        "x": np.asarray(L0_attn_x),
        "proj_w": np.concatenate([w_attn[0:2 * C], w_attn[2 * C:3 * C][order]]).T,
        "ffn_w": np.asarray(L0_ffn_weight).T,
        "alpha": rows(L0_ffn_alpha),
        "bias0": rows(L0_ffn_bias),
        "out_w": np.asarray(L0_attn_w_proj).T[order],
        "router_w": np.asarray(L1_ffn_router_w).T[runs],
        "router_b": rows(L1_ffn_router_b),
        "cheb_w": np.asarray(L1_attn_W_in).T[runs],
        "cheb_out_w": np.asarray(L1_attn_W_out).T,
        "w1": np.asarray(L1_ffn_w1).transpose(2, 0, 1)[runs],
        "b1": np.asarray(L1_ffn_b1).reshape(E, FB, P).transpose(2, 0, 1),
        "w2": np.asarray(L1_ffn_w2).reshape(E, C, FB, P).transpose(3, 0, 2, 1),
        "b2": np.asarray(L1_ffn_b2),
        "ln_w": rows(L1_ffn_ln_w),
        "ln_b": rows(L1_ffn_ln_b),
        **constants(),
    }
    nc = bacc.Bacc("TRN2", target_bir_lowering=False, num_devices=1)
    given, args = {}, {}
    for name, a in arrays.items():
        given[f"in_{name}"] = a = np.ascontiguousarray(a)
        args[name] = nc.dram_tensor(f"in_{name}", a.shape, mybir.dt.from_np(a.dtype), kind="ExternalInput").ap()
    args["out"] = nc.dram_tensor("out_0", (B, T, C), F32, kind="ExternalOutput").ap()
    program(nc, **args)
    return run_bass_kernel_spmd(nc, [given], core_ids=[0]).results[0]["out_0"]
```

```python
from contextlib import ExitStack

import concourse.bass as bass
import numpy as np
from concourse import mybir

F32 = mybir.dt.float32
F16 = mybir.dt.float16
BF16 = mybir.dt.bfloat16
ALU = mybir.AluOpType
ACT = mybir.ActivationFunctionType
AX = mybir.AxisListType

P = 128
B, T, C = 4, 1024, 128
NT = B * T // P
TAUS = T // P
H, D = 16, 8
W = 64
NG = 4
NPAIR = H // 2
VW = 32
EPS0 = 1e-5
IL = 4
NEG = -1e30

ORD = 5
SW = C + H
E, FF = 8, 512
FB = FF // P
CHEB1, CHEB2 = 14, 12
ROUTE = 20
_ALPHA = np.arange(1, ORD + 2, dtype=np.float32) ** -1.5
_BETA = np.cumsum(_ALPHA[::-1])[::-1][1:].astype(np.float32)
BETA = [float(v) for v in _BETA / _BETA.sum()]
INV = float(D) ** -0.5
CLIP = 1.0 - 1e-6
PARTS = [(0, 0), (1, 0), (0, 1)]
MIX = [('up', 0), ('down', 0), ('up', 1), ('down', 1), ('up', 2), ('down', 2), ('up', 3), ('down', 3)]
TASKS_AT = ("down", 3)
BIAS_AT = 3
POOL_ORDER = [('low', 0), ('deviation', 0), ('low', 1), ('gate', 0), ('low', 2), ('result', 0), ('low', 3), ('low', 4), ('parts', 0), ('low', 5), ('low', 6), ('low', 7), ('gather', 0)]
SLOTS = [[], [('CS', 0), ('CP', 1)], [('OT', 0)], [('SO', 0), ('CS', 1), ('CP', 2)], [('OT', 1)], [('SO', 1), ('CS', 2), ('CP', 3)], [('OT', 2), ('SO', 2)], [('CS', 3)]]
DVE_ORDER = [('keys', 0), ('residual', 0), ('sum', 0), ('gate', 0), ('sum', 1), ('out', 0), ('keys', 1), ('sum', 2), ('sum', 3), ('out', 1), ('keys', 2), ('sum', 4), ('sum', 5), ('out', 2), ('keys', 3), ('sum', 6), ('sum', 7), ('out', 3)]


class Tile:

    def __init__(self, t, m):
        self.static = isinstance(t, int)
        if self.static:
            t, m = (4 * t + m) // 4, (4 * t + m) % 4
        self.t, self.m = t, m
        self.batch = m % 4
        self.tau = t + m // 4
        self.index = t * 4 + m
        self.exists = not self.static or 0 <= self.index < NT
        self.first = self.static and self.tau == 0

    def before(self, lag):
        return Tile(self.t, self.m - lag)

    def count(self, per, k):
        return self.t * (4 * per) + (self.m * per + k)


class Stage:

    def __init__(self, sem, per=1):
        self.sem, self.per = sem, per

    def wait(self, engine, tile, k=None):
        if tile.static and tile.index < 0:
            return
        k = self.per if k is None else k
        if tile.static and tile.index >= NT:
            tile, k = Tile(TAUS - 1, 3), self.per
        engine.wait_ge(self.sem, tile.count(self.per, k))


def pipeline(engine, step, lags):
    for n in range(8):
        step(Tile(0, n))
    with engine.Fori(2, TAUS) as t:
        for k in range(4):
            step(Tile(t, k))
    for n in range(lags):
        step(Tile(TAUS, n))


class Round:

    def __init__(self, t, parity=0):
        self.static = isinstance(t, int)
        self.t, self.index, self.tiles = t, t, bass.ts(t, B)
        self.first = self.static and t == 0
        self.last = self.static and t == TAUS - 1
        self.parity = t % 2 if self.static else parity

    def before(self, rounds):
        return Round(self.t - rounds, (self.parity - rounds) % 2)

    def count(self, per, k):
        return self.t * per + k

    def at(self, i, items, each=1):
        return (self, (i + 1) * each) if i >= 0 else (self.before(1), (i + items + 1) * each)

    def at_acc(self, e):
        return (self, 1 + B * (e + 1)) if e >= 0 else (self.before(1), 1 + B * (e + E + 1))

    def wait_dma(self, engine, sem):
        if not self.first:
            engine.wait_ge(sem, self.t * 16)

    def wait_carry(self, engine, sems, b):
        if b >= 0:
            engine.wait_ge(sems[b], self.t * 16 + 16)
        else:
            self.wait_dma(engine, sems[b + B])


def rounds(engine, mix, buffers=2):
    mix(Round(0))
    if buffers == 1:
        with engine.Fori(1, TAUS) as t:
            mix(Round(t))
        return
    with engine.Fori(0, TAUS // 2 - 1) as t:
        mix(Round(t * 2 + 1, 1))
        mix(Round(t * 2 + 2, 0))
    mix(Round(TAUS - 1))


def turn(engine, sem):
    engine.sem_inc(sem, 1)


def program(nc, x, proj_w, ffn_w, alpha, bias0, out_w, rope, eye, win_max, win_exp, pair_sel,
            router_w, router_b, cheb_w, cheb_out_w, tri, descend, experts_w, b1, b2, ln_w, ln_b, out):
    ctx = ExitStack()
    with ctx:
        def sb(name, shape, dt=F32):
            return ctx.enter_context(nc.sbuf_tensor(name, shape, dt))

        def bank(name, shape, dt=F32):
            return ctx.enter_context(nc.psum_tensor(name, shape, dt))

        def sem(name):
            return ctx.enter_context(nc.semaphore(name))

        def stage(name, per=1):
            return Stage(sem(name), per)

        x_all = sb("x_all", [P, NT, C])
        xn1_all = sb("xn1_all", [P, NT, C])
        xn1t_all = sb("xn1t_all", [P, NT, P])
        logits = sb("logits", [P, NT, 8])

        wp = sb("wp", [P, 3 * C + C])
        wraw = sb("wraw", [P, C])
        wneg = sb("wneg", [P, C])
        wsum = sb("wsum", [P, 2])
        alpha_sb = sb("alpha_sb", [P, 1])
        bias0_sb = sb("bias0_sb", [P, C])
        wo = sb("wo", [P, C])
        rope_sb = sb("rope_sb", [P, TAUS, 2 * D])
        eye_sb = sb("eye_sb", [P, P])
        eye16_sb = sb("eye16_sb", [P, P], F16)
        eyeb_sb = sb("eyeb_sb", [P, P], BF16)
        ones_sb = sb("ones_sb", [P, P])
        winm_sb = sb("winm_sb", [P, NG, P], BF16)
        mm_sb = sb("mm_sb", [P, 4, 2 * P], BF16)
        hide_sb = sb("hide_sb", [P, NG, W], BF16)
        pair_sb = sb("pair_sb", [P, NPAIR, P], BF16)
        rw = sb("rw", [P, 8])
        rb = sb("rb", [P, 8])
        half_sb = sb("half_sb", [P, 1])

        stats = sb("stats", [P, 4, 6])
        mv = sb("mv", [P, 4, 2])
        rstd = sb("rstd", [P, 4, 2])
        xn = sb("xn", [P, 4, C])
        xnt = sb("xnt", [P, 4, P])
        rot = sb("rot", [P, 2, 2, 2 * C])
        xs = sb("xs", [P, 4, 2 * H, 4, D], F16)
        qt = sb("qt", [P, 4, NG, P], F16)
        kt = sb("kt", [P, 4, NG, W + P], F16)
        vd = sb("vd", [P, 4, 3, NPAIR, VW])
        mneg = sb("mneg", [P, 4, 2, NPAIR], BF16)
        pexp = sb("pexp", [P, 4, 2, 2 * P])
        yts = sb("yts", [P, 2 * P])
        rden = sb("rden", [P, H])
        yn = sb("yn", [P, C])
        ynt = sb("ynt", [P, P])
        z = sb("z", [P, 4, C])
        ez = sb("ez", [P, C])
        gd = sb("gd", [P, 3, C])
        sg = sb("sg", [P, C])
        stats1 = sb("stats1", [P, 4, 6])
        mv1 = sb("mv1", [P, 4, 2])
        rstd1 = sb("rstd1", [P, 4, 2])
        xn1 = sb("xn1", [P, 4, C])
        xn1t = sb("xn1t", [P, 4, P])

        w_in = sb("w_in", [P, 3 * C])
        w_out = sb("w_out", [P, C])
        tri_sb = sb("tri_sb", [P, P])
        desc_sb = sb("desc_sb", [P, E])
        experts_sb = sb("experts_sb", [P, 2 * E * FB, P])
        split_sb = sb("split_sb", [P, 2, 2, P], F16)
        b1_sb = sb("b1_sb", [P, E, FB])
        b2_sb = sb("b2_sb", [E, C])
        lnw_sb = sb("lnw_sb", [P, C])
        lnb_sb = sb("lnb_sb", [P, C])
        cw = sb("cw", [P, NT, E])
        rt = sb("rt", [P, 5, NT, E])
        rs = sb("rs", [P, 8, NT])
        xg = sb("xg", [P, B, P])
        xg16 = sb("xg16", [P, 2, 2, B * P], F16)
        cwg = sb("cwg", [P, B, E])
        cwt = sb("cwt", [E, B, P])
        vs = sb("vs", [P, 2, C])
        xc = sb("xc", [P, 2 * C])
        kv = sb("kv", [P, 2, ORD * SW])
        tq = sb("tq", [P, ORD, SW])
        pr = sb("pr", [P, ORD, SW])
        nd = sb("nd", [P, SW])
        dn = sb("dn", [P, 2, H])
        oc = sb("oc", [P, C])
        oct_ = sb("oct", [P, P])
        s1 = sb("s1", [P, B, C])
        last_sb = sb("last_sb", [P, 2, ORD * SW])
        carry = sb("carry", [1, B, ORD * SW])
        stats2 = sb("stats2", [P, B, 6])
        mv2 = sb("mv2", [P, B, 2])
        rstd2 = sb("rstd2", [P, 2, B])
        eps2_sb = sb("eps2_sb", [P, B])

        m_ps = [bank(f"m_ps{i}", [P, NG, P]) for i in range(2)]
        e_ps = [bank(f"e_ps{i}", [P, 2, 2 * P]) for i in range(2)]
        p_ps = bank("p_ps", [P, 4 * C])
        q_ps = bank("q_ps", [P, 2 * NG, P], F16)
        t_ps = bank("t_ps", [P, 4, P])
        y_ps = bank("y_ps", [P, 4, P])
        tb_ps = t_ps[:, :, :].rearrange("p a b -> p (a b)").bitcast(BF16)

        y2, e2, res, acc = (xs[:, i, :, :, :].rearrange("p h s d -> p (h s d)").bitcast(F32).rearrange("p (b c) -> p b c", b=B)
                            for i in range(4))
        tc = kt[:, :, :, :].rearrange("p b g t -> p (b g t)").bitcast(F32)[:, 0:ORD * 2 * C].rearrange("p (j c) -> p j c", j=ORD)
        hid = [pexp[:, :, :, :].rearrange("p j a b -> p (j a b)"),
               vd[:, :, :, :, :].rearrange("p a b i w -> p (a b i w)")[:, 0:FB * B * P]]
        hid = [a.bitcast(F16).rearrange("p (s f t) -> p s f t", s=2, f=FB) for a in hid]
        gel = [rot[:, i, :, :].rearrange("p a b -> p (a b)") for i in range(2)] + \
              [qt[:, 2 * i:2 * i + 2, :, :].rearrange("p b g t -> p (b g t)").bitcast(F32) for i in range(2)]
        w16 = experts_sb[:, :, :].bitcast(F16).rearrange("p k (s c) -> p k s c", s=2)
        u_ps = [m_ps[i][:, :, :].rearrange("p a b -> p (a b)") for i in range(2)]
        d_ps = [e_ps[i][:, :, :].rearrange("p a (h b) -> p (a h) b", b=P) for i in range(2)]
        cc_ps = [y_ps[:, :, :].rearrange("p a b -> p (a b)"), q_ps[:, :, :].rearrange("p a b -> p (a b)").bitcast(F32)]

        CP, XG, CL, C1, C2 = (stage(*a) for a in (("cheb_projected", 4), ("gathered", 4), ("last_row", 4), ("cheb_keys", 4 * CHEB1), ("cheb_out", 4 * CHEB2)))
        CS, OT, SO, CW = (stage(*a) for a in (("prefix_sums", 4), ("cheb_transposed", 4), ("cheb_out_projected", 4), ("weights_transposed", 2)))
        UP, DN, GE, VC = (stage(*a) for a in (("up", E * FB), ("down", E), ("gelu", 2 * E * FB), ("v_copied", 4)))
        OE, SE1, CT, AC = (stage(*a) for a in (("cheb_out_copied", 4), ("s1_copied", 4), ("weights_copied", 1), ("accumulated", 1 + 4 * E)))
        F1, GA, R2, EX2 = (stage(*a) for a in (("ln_steps", 15), ("gated_s1", 1), ("rstd2", 2), ("last_exp", 1)))
        F2 = stage("result", 1)
        s_carry = [sem(f"s_carry{b}") for b in range(B)]
        s_out = sem("s_out")
        s_w2 = sem("s_w2")
        s_cw = sem("s_cw")
        s_we = sem("s_we")
        s_experts = sem("s_experts")
        WS = stage("weights_split", 3)
        LO = stage("low_parts", E * FB)

        s_x = [sem(f"s_x{i}") for i in range(3)]
        s_w = sem("s_w")
        s_win = sem("s_win")
        s_zero = sem("s_zero")
        s_init = sem("s_init")
        s_ps = sem("s_ps")
        s_turn_pool, s_turn_dve = sem("s_turn_pool"), sem("s_turn_dve")
        TX, PR, TQ, MX, TM = stage("xn_transposed"), stage("projected"), stage("qk_transposed"), stage("max_scored", 4), stage("max_transposed")
        SE, PV, TY, T2 = stage("scored", 4), stage("weighted", 4), stage("y_transposed"), stage("yn_transposed")
        OP, TX1, LM = stage("out_projected"), stage("xn1_transposed"), stage("routed")
        XT, HI, VB, QK, EX = stage("xnt_copied"), stage("high_parts"), stage("values_placed", 4), stage("qk_copied", 3), stage("exponentials", 4)
        EZ, YT, Y2, X1T = stage("gate_exp"), stage("yt_copied"), stage("ynt_copied"), stage("xn1t_copied")
        ST, XN, RED, MMR, RP = stage("stats0", 2), stage("xn_ready"), stage("maxima", 4), stage("maxima_placed", 2), stage("rotated", 6)
        ZG, YN, GT, XN1, LG = stage("gate_in"), stage("y_normed", 2), stage("gated", 10), stage("xn1_ready"), stage("logits_ready")
        R0, DUP, VP, R1, SX = stage("rstd0", 2), stage("parts_doubled", 2), stage("values_kept"), stage("rstd1", 2), stage("xn1_stored", 2)

        block = ctx.enter_context(nc.Block())

        @block.sync
        def _(sp):
            xv = x.rearrange("b (t p) c -> p t b c", p=P)
            xo = x_all[:, :, :].rearrange("p (t b) c -> p t b c", b=B)
            weights = [(wp[:, 0:3 * C], proj_w), (wraw[:, :], ffn_w), (alpha_sb[:, :], alpha), (bias0_sb[:, :], bias0),
                       (wo[:, :], out_w), (rope_sb[:, :, :], rope), (eye_sb[:, :], eye), (rw[:, :], router_w),
                       (rb[:, :], router_b)]
            sp.dma_start(xo[:, 0, :, :], xv[:, 0, :, :]).then_inc(s_x[0], 16)
            for dst, src in weights:
                sp.dma_start(dst, src).then_inc(s_w, 16)
            sp.dma_start(xo[:, 1, :, :], xv[:, 1, :, :]).then_inc(s_x[1], 16)
            for t in range(2, TAUS):
                sp.dma_start(xo[:, t, :, :], xv[:, t, :, :]).then_inc(s_x[2], 16)
            for dst, src in [(w_in[:, :], cheb_w), (w_out[:, :], cheb_out_w), (tri_sb[:, :], tri), (desc_sb[:, :], descend),
                             (b1_sb[:, :, :], b1), (b2_sb[:, :], b2),
                             (lnw_sb[:, :], ln_w), (lnb_sb[:, :], ln_b)]:
                sp.dma_start(dst, src).then_inc(s_w2, 16)
            for e in range(E):
                k = slice(2 * FB * e, 2 * FB * e + 2 * FB)
                sp.dma_start(experts_sb[:, k, :], experts_w[:, k, :]).then_inc(s_experts, 16)

            def move(n):
                for b in range(B):
                    CL.wait(sp, n, b + 1)
                    sp.dma_start(carry[0:1, b, :], last_sb[P - 1:P, b % 2, :]).then_inc(s_carry[b], 16)
                F2.wait(sp, n)
                sp.dma_start(out.rearrange("b (t p) c -> p t b c", p=P)[:, n.t, :, :], res[:, :, :]).then_inc(s_out, 16)

            rounds(sp, move, buffers=1)
            sp.wait_ge(s_out, 16 * TAUS)

        @block.gpsimd
        def _(pool):
            pool.wait_ge(s_zero, 5)
            pool.dma_start(eye16_sb[:, :], eye).then_inc(s_win, 16)
            pool.dma_start(eyeb_sb[:, :], eye).then_inc(s_win, 16)
            pool.dma_start(winm_sb[:, :, :], win_max).then_inc(s_win, 16)
            pool.dma_start(pair_sb[:, :, :], pair_sel).then_inc(s_win, 16)
            for b in range(4):
                pool.dma_start(mm_sb[0:W, b, :], win_exp).then_inc(s_win, 16)

            def step(head):
                n, l3, l4 = (head.before(i) for i in (1, 4, 5))
                if n.exists:
                    PV.wait(pool, n.before(4))
                    VB.wait(pool, n.before(4))
                    turn(pool, s_turn_pool)
                    nc.gpsimd.tensor_copy(vd[:, n.batch, 0, :, :], vd[:, n.batch, 2, :, :]).then_inc(VP.sem, 1)
                if l4.exists:
                    XN1.wait(pool, l4)
                    turn(pool, s_turn_pool)
                    nc.gpsimd.tensor_copy(xn1_all[:, l4.index, :].rearrange("p (a b) -> p a b", b=IL), xn1[:, l4.batch, :].rearrange("p (b a) -> p a b", b=IL)).then_inc(SX.sem, 1)
                    X1T.wait(pool, l4)
                    turn(pool, s_turn_pool)
                    nc.gpsimd.tensor_copy(xn1t_all[:, l4.index, :], xn1t[:, l4.batch, :]).then_inc(SX.sem, 1)
                if n.exists:
                    HI.wait(pool, n)
                    TQ.wait(pool, n.before(4))
                    turn(pool, s_turn_pool)
                    nc.gpsimd.tensor_copy(xs[:, n.batch, 0:H, 2, :], xs[:, n.batch, 0:H, 0, :]).then_inc(DUP.sem, 1)
                    turn(pool, s_turn_pool)
                    nc.gpsimd.tensor_copy(xs[:, n.batch, H:2 * H, 1, :], xs[:, n.batch, H:2 * H, 0, :]).then_inc(DUP.sem, 1)
                if head.exists:
                    ST.wait(pool, head)
                    turn(pool, s_turn_pool)
                    nc.gpsimd.tensor_scalar(rstd[:, head.batch, 0:1], mv[:, head.batch, 1:2], EPS0, None, ALU.add).then_inc(R0.sem, 1)
                    R0.wait(pool, head, 1)
                    nc.gpsimd.tensor_tensor(rstd[:, head.batch, 1:2], rstd[:, head.batch, 0:1], half_sb[:, 0:1], ALU.pow).then_inc(R0.sem, 1)
                if l3.exists:
                    if l3.static and l3.index == 0:
                        pool.wait_ge(s_experts, 16 * E)
                    blocks = bass.ds(l3.index * 2, 2)
                    WS.wait(pool, l3.before(1))
                    turn(pool, s_turn_pool)
                    nc.gpsimd.tensor_copy(split_sb[:, :, 0, :], experts_sb[:, blocks, :]).then_inc(WS.sem, 1)
                    WS.wait(pool, l3, 1)
                    turn(pool, s_turn_pool)
                    nc.gpsimd.tensor_tensor(split_sb[:, :, 1, :], experts_sb[:, blocks, :], split_sb[:, :, 0, :], ALU.subtract).then_inc(WS.sem, 1)
                    WS.wait(pool, l3, 2)
                    turn(pool, s_turn_pool)
                    nc.gpsimd.tensor_copy(w16[:, blocks, :, :], split_sb[:, :, :, :]).then_inc(WS.sem, 1)
                if l3.exists:
                    GT.wait(pool, l3, 10)
                    turn(pool, s_turn_pool)
                    nc.gpsimd.tensor_scalar(rstd1[:, l3.batch, 0:1], mv1[:, l3.batch, 1:2], 1.0 / C, EPS0, ALU.mult, ALU.add).then_inc(R1.sem, 1)
                    R1.wait(pool, l3, 1)
                    nc.gpsimd.tensor_tensor(rstd1[:, l3.batch, 1:2], rstd1[:, l3.batch, 0:1], half_sb[:, 0:1], ALU.pow).then_inc(R1.sem, 1)

            pipeline(pool, step, 5)

            def gate(n):
                F1.wait(pool, n, 14)
                SE1.wait(pool, n)
                n.wait_dma(pool, s_out)
                nc.gpsimd.tensor_tensor(res[:, :, :], y2[:, :, :], s1[:, :, :], ALU.mult).then_inc(GA.sem, 1)

            def result(n):
                F1.wait(pool, n)
                turn(pool, s_turn_pool)
                nc.gpsimd.tensor_tensor(res[:, :, :], e2[:, :, :], x_all[:, n.tiles, :], ALU.add).then_inc(F2.sem, 1)

            def deviation(n):
                F1.wait(pool, n, 8)
                turn(pool, s_turn_pool)
                nc.gpsimd.tensor_tensor(rstd2[:, 0, :], mv2[:, :, 1], eps2_sb[:, :], ALU.add).then_inc(R2.sem, 1)
                R2.wait(pool, n, 1)
                nc.gpsimd.tensor_tensor(rstd2[:, 1, :], rstd2[:, 0, :], half_sb[:, 0:1].to_broadcast([P, B]), ALU.pow).then_inc(R2.sem, 1)

            def gather_parts(n):
                UP.wait(pool, n.before(2))
                turn(pool, s_turn_pool)
                nc.gpsimd.tensor_copy(xg16[:, n.parity, 0, :].rearrange("p (b t) -> p b t", b=B), xn1t_all[:, n.tiles, :]).then_inc(XG.sem, 1)
                XG.wait(pool, n, 1)
                turn(pool, s_turn_pool)
                nc.gpsimd.tensor_tensor(xg16[:, n.parity, 1, :].rearrange("p (b t) -> p b t", b=B), xn1t_all[:, n.tiles, :],
                                        xg16[:, n.parity, 0, :].rearrange("p (b t) -> p b t", b=B), ALU.subtract).then_inc(XG.sem, 1)

            def gather(n):
                CP.wait(pool, n.before(1))
                turn(pool, s_turn_pool)
                nc.gpsimd.tensor_copy(xg[:, :, :], xn1t_all[:, n.tiles, :]).then_inc(XG.sem, 1)

            def mix(n):
                def low_parts(e):
                    for f in range(FB):
                        i = e * FB + f
                        GE.wait(pool, n, 2 * i + 2)
                        DN.wait(pool, *n.at(e - 2, E))
                        turn(pool, s_turn_pool)
                        nc.gpsimd.tensor_tensor(hid[e % 2][:, 1, f, :], gel[i % 4], hid[e % 2][:, 0, f, :], ALU.subtract).then_inc(LO.sem, 1)

                if n.first:
                    gather_parts(n)
                    gather(n)
                CW.wait(pool, n.before(1), 1)
                AC.wait(pool, n.before(1))
                turn(pool, s_turn_pool)
                nc.gpsimd.tensor_copy(cwg[:, :, :], cw[:, n.tiles, :]).then_inc(XG.sem, 1)
                for what, e in POOL_ORDER:
                    if what == "low":
                        low_parts(e)
                    elif what == "parts" and not n.last:
                        gather_parts(n.before(-1))
                    elif what == "gather" and not n.last:
                        gather(n.before(-1))
                    elif what == "deviation" and not n.first:
                        deviation(n.before(1))
                    elif what == "gate" and not n.first:
                        gate(n.before(1))
                    elif what == "result" and not n.first:
                        result(n.before(1))

            pool.wait_ge(SX.sem, 2 * NT)
            pool.wait_ge(s_cw, ROUTE)
            rounds(pool, mix)
            deviation(Round(TAUS - 1))
            gate(Round(TAUS - 1))
            result(Round(TAUS - 1))

        @block.scalar
        def _(act):
            def step(head):
                n, l2, l3, l4 = (head.before(i) for i in (1, 3, 4, 5))

                def exponentials(j):
                    SE.wait(act, l2, j + 1)
                    PV.wait(act, l2.before(1), j + 1)
                    nc.scalar.activation(pexp[:, j, :, :], e_ps[j % 2][:, :, :], ACT.Exp,
                                         scale=float(D) ** -0.5).then_inc(EX.sem, 1)

                if l2.exists:
                    exponentials(0)
                TX.wait(act, n)
                if l4.exists:
                    TX1.wait(act, l4)
                    LM.wait(act, l4.before(4))
                    SX.wait(act, l4.before(4))
                    nc.scalar.copy(xn1t[:, l4.batch, :], t_ps[:, 0, :]).then_inc(X1T.sem, 1)
                if n.exists:
                    PR.wait(act, n.before(4))
                    nc.scalar.copy(xnt[:, n.batch, :], t_ps[:, 1, :]).then_inc(XT.sem, 1)
                if l2.exists:
                    exponentials(1)
                if l3.exists:
                    ZG.wait(act, l3)
                    GT.wait(act, l3.before(1), 1)
                    nc.scalar.activation(ez[:, :], z[:, l3.batch, :], ACT.Exp, scale=-1.0).then_inc(EZ.sem, 1)
                if n.exists:
                    ZG.wait(act, n)
                    VP.wait(act, n)
                    for blk in range(2):
                        for a in range(2):
                            src = p_ps[W * blk:W * blk + W, 2 * C:3 * C].rearrange("p (i a d) -> p i a d", a=2, d=D)
                            nc.scalar.copy(vd[W * a:W * a + W, n.batch, 1 + blk, :, 9 * a:9 * a + D],
                                           src[:, :, a, :]).then_inc(VB.sem, 1)
                    RP.wait(act, n, 4)
                    TQ.wait(act, n.before(4))
                    DUP.wait(act, n.before(4))
                    nc.scalar.copy(xs[:, n.batch, :, 0, :],
                                   rot[:, n.batch % 2, 0, :].rearrange("p (h d) -> p h d", d=D)).then_inc(HI.sem, 1)
                if l2.exists:
                    exponentials(2)
                if l3.exists:
                    T2.wait(act, l3)
                    OP.wait(act, l3.before(1))
                    nc.scalar.copy(ynt[:, :], t_ps[:, 3, :]).then_inc(Y2.sem, 1)
                if l2.exists:
                    exponentials(3)
                if n.exists:
                    SE.wait(act, n.before(4))
                    QK.wait(act, n.before(4))
                    nc.scalar.copy(kt[:, n.batch, :, 0:W], kt[:, n.batch, :, P:W + P]).then_inc(QK.sem, 1) if not n.first else \
                        nc.scalar.copy(kt[:, n.batch, :, 0:W], kt[:, n.batch, :, 0:W]).then_inc(QK.sem, 1)
                    TQ.wait(act, n)
                    nc.scalar.copy(qt[:, n.batch, :, :], q_ps[:, 0:NG, :]).then_inc(QK.sem, 1)
                    QK.wait(act, n, 1)
                    nc.scalar.copy(kt[:, n.batch, :, W:W + P], q_ps[:, NG:2 * NG, :]).then_inc(QK.sem, 1)
                if l2.exists:
                    PV.wait(act, l2)
                    TY.wait(act, l2.before(1))
                    nc.scalar.copy(yts[:, :], y_ps[:, 0:2, :].rearrange("p a b -> p (a b)")).then_inc(YT.sem, 1)

            act.wait_ge(s_zero, 5)
            pipeline(act, step, 5)

            act.wait_ge(s_cw, 8)
            nc.scalar.activation(rs[:, 5, :], rs[:, 4, :], ACT.Exp).then_inc(s_we, 1)
            act.wait_ge(s_w2, 16 * 8)
            PV.wait(act, Tile(TAUS, 0))
            VP.wait(act, Tile(TAUS, 0))

            def oct_copy(n, b):
                OT.wait(act, n, b + 1)
                SO.wait(act, *n.at(b - 1, 4))
                nc.scalar.copy(oct_[:, :], t_ps[:, 0, :]).then_inc(OE.sem, 1)

            def s1_copy(n, b):
                SO.wait(act, n, b + 1)
                GA.wait(act, n.before(1))
                nc.scalar.mul(s1[:, b, :], t_ps[:, 1, :], 0.5).then_inc(SE1.sem, 1)

            def finish(n):
                oct_copy(n, B - 1)
                s1_copy(n, B - 1)

            def silu_tanh(n):
                F1.wait(act, n, 14)
                F2.wait(act, n.before(1))
                nc.scalar.activation(e2[:, :, :], y2[:, :, :], ACT.Tanh, scale=0.5).then_inc(EX2.sem, 1)

            def mix(n):
                def gelus(e, blocks=range(FB)):
                    for f in blocks:
                        UP.wait(act, n, e * FB + f + 1)
                        LO.wait(act, *n.at(e * FB + f - 4, E * FB))
                        nc.scalar.activation(gel[f], u_ps[f % 2], ACT.Gelu, bias=b1_sb[:, e, f:f + 1]).then_inc(GE.sem, 1)
                        DN.wait(act, *n.at(e - 2, E))
                        nc.scalar.activation(hid[e % 2][:, 0, f, :], u_ps[f % 2], ACT.Gelu, bias=b1_sb[:, e, f:f + 1]).then_inc(GE.sem, 1)

                def task(what, b):
                    if what == "CP":
                        CP.wait(act, n, b + 1)
                        C1.wait(act, *n.at(b - 2, 4, CHEB1))
                        nc.scalar.copy(vs[:, b % 2, :], p_ps[:, 2 * C:3 * C]).then_inc(VC.sem, 1)
                    if what == "CS":
                        CS.wait(act, n, b + 1)
                        n.wait_carry(act, s_carry, b - 2)
                        nc.scalar.copy(last_sb[96:P, b % 2, 0:3 * SW], cc_ps[0][96:P, 0:3 * SW])
                        nc.scalar.copy(last_sb[96:P, b % 2, 3 * SW:5 * SW], cc_ps[1][96:P, 0:2 * SW]).then_inc(CL.sem, 1)
                    if what == "OT":
                        oct_copy(n, b)
                    if what == "SO":
                        s1_copy(n, b)

                task("CP", 0)
                gelus(0, (0, 1))
                if not n.first:
                    finish(n.before(1))
                gelus(0, (2, 3))
                gelus(1, (0,))
                CW.wait(act, n, 1)
                CW.wait(act, n.before(1), 2)
                nc.scalar.copy(cwt[:, :, :], t_ps[0:E, :, :]).then_inc(CT.sem, 1)
                gelus(1, (1, 2, 3))
                if not n.first:
                    silu_tanh(n.before(1))
                for e in range(E):
                    if 0 < e < E - 1:
                        gelus(e + 1)
                    for what, b in SLOTS[e]:
                        task(what, b)

            rounds(act, mix)
            finish(Round(TAUS - 1))
            silu_tanh(Round(TAUS - 1))

        @block.tensor
        def _(pe):
            pe.wait_ge(s_init, 1)
            pe.wait_ge(s_zero, 5)
            nc.tensor.matmul(t_ps[:, 0, 0:1], ones_sb[:, :], wsum[:, 0:1], start=True, stop=True).then_inc(s_ps, 1)
            pe.wait_ge(s_init, 5)
            pe.wait_ge(s_w, 16 * 9)
            pe.wait_ge(s_win, 16 * 8)

            def max_scores(n, j):
                c, jp = j // 2, j % 2
                ps = m_ps[j % 2]
                QK.wait(pe, n)
                RED.wait(pe, n.before(1), 3 + j) if j < 2 else RED.wait(pe, n, j - 1)
                nc.tensor.matmul(ps[:, :, :], eyeb_sb[:, :], winm_sb[:, :, :], start=True, stop=True)
                lo = W if n.first and c == 0 else 0
                if lo:
                    nc.tensor.matmul(ps[:, :, 0:W], eyeb_sb[:, :], hide_sb[:, :, :], start=False, stop=True, skip_group_check=True)
                for g in range(NG):
                    for a in range(2):
                        r = 32 * (2 * jp + a)
                        last = nc.tensor.matmul(ps[W * a:W * a + W, g, lo:P],
                                                qt[r:r + 32, n.batch, g, c * W:c * W + W],
                                                kt[r:r + 32, n.batch, g, c * W + lo:c * W + P],
                                                start=False, stop=True, skip_group_check=True)
                last.then_inc(MX.sem, 1)

            def scores(n, j):
                jp, gg = j // 2, j % 2
                ps = e_ps[j % 2]
                MMR.wait(pe, n)
                EX.wait(pe, n.before(1), 3 + j) if j < 2 else EX.wait(pe, n, j - 1)
                for i in range(2):
                    g = 2 * gg + i
                    nc.tensor.matmul(ps[:, i, :], pair_sb[:, jp * NG + g, :], mm_sb[:, n.batch, :],
                                     start=True, stop=True, skip_group_check=True)
                    if n.first:
                        nc.tensor.matmul(ps[:, i, P:P + W], eyeb_sb[:, :], hide_sb[:, 0, :], start=False, stop=True, skip_group_check=True)
                    for a in range(2):
                        r = 32 * (2 * jp + a)
                        o = ps[W * a:W * a + W, i, :]
                        q, k = qt[r:r + 32, n.batch, g, :], kt[r:r + 32, n.batch, g, :]
                        nc.tensor.matmul(o[:, 0:P], k[:, W:2 * W], q[:, 0:P], start=False, stop=True, skip_group_check=True)
                        if not n.first:
                            nc.tensor.matmul(o[:, P:P + W], k[:, 0:W], q[:, 0:W], start=False, stop=True, skip_group_check=True)
                        last = nc.tensor.matmul(o[:, P + W:2 * P], k[:, 2 * W:3 * W], q[:, W:P], start=False, stop=True, skip_group_check=True)
                last.then_inc(SE.sem, 1)

            def weigh(n, j):
                jp, gg = j // 2, j % 2
                EX.wait(pe, n, j + 1)
                VB.wait(pe, n)
                YT.wait(pe, n.before(1))
                for part in range(3):
                    for i in range(2):
                        g = 2 * gg + i
                        o = y_ps[VW * g:VW * g + VW, jp, :]
                        v = vd[:, n.batch, :, jp * NG + g, :]
                        w = pexp[:, j, i, :]
                        if part == 0:
                            nc.tensor.matmul(o, v[:, 1, :], w[:, 0:P], start=True, stop=True, skip_group_check=True)
                        elif part == 1:
                            if not n.first:
                                nc.tensor.matmul(o[:, 0:W], v[:, 0, :], w[:, P:P + W], start=False, stop=True, skip_group_check=True)
                        else:
                            last = nc.tensor.matmul(o[:, W:P], v[:, 2, :], w[:, P + W:2 * P], start=False, stop=True, skip_group_check=True)
                last.then_inc(PV.sem, 1)

            def step(head):
                n, l1, l2, l3, l4 = (head.before(i) for i in (1, 2, 3, 4, 5))
                if l1.exists:
                    max_scores(l1, 0)
                if l2.exists:
                    scores(l2, 0)
                if l1.exists:
                    max_scores(l1, 1)
                LG.wait(pe, l4.before(1))
                MMR.wait(pe, l1.before(1))
                if head.static:
                    Y2.wait(pe, l3.before(1))
                if l4.exists:
                    XN1.wait(pe, l4)
                    nc.tensor.transpose(t_ps[:, 0, :], xn1[:, l4.batch, :], eye_sb[:, :]).then_inc(TX1.sem, 1)
                if n.exists:
                    XN.wait(pe, n)
                    nc.tensor.transpose(t_ps[:, 1, :], xn[:, n.batch, :], eye_sb[:, :]).then_inc(TX.sem, 1)
                if l2.exists:
                    weigh(l2, 0)
                if l2.exists:
                    scores(l2, 1)
                if n.exists:
                    XT.wait(pe, n)
                    GT.wait(pe, l4, 4)
                    nc.tensor.matmul(p_ps[:, :], xnt[:, n.batch, :], wp[:, :], start=True, stop=True).then_inc(PR.sem, 1)
                XT.wait(pe, n)
                X1T.wait(pe, l4)
                if l3.exists:
                    YT.wait(pe, l3)
                    nc.tensor.transpose(t_ps[:, 2, :], yts[:, 0:P], eye_sb[:, :])
                    nc.tensor.transpose(t_ps[:, 3, :], yts[:, P:2 * P], eye_sb[:, :]).then_inc(TY.sem, 1)
                if l2.exists:
                    scores(l2, 2)
                if l1.exists:
                    max_scores(l1, 2)
                if l2.exists:
                    weigh(l2, 1)
                if l3.exists:
                    YN.wait(pe, l3)
                    nc.tensor.transpose(t_ps[:, 3, :], yn[:, :], eye_sb[:, :]).then_inc(T2.sem, 1)
                if l1.exists:
                    max_scores(l1, 3)
                if l2.exists:
                    scores(l2, 3)
                if n.exists:
                    RP.wait(pe, n)
                    DUP.wait(pe, n)
                    HI.wait(pe, n)
                    QK.wait(pe, l1)
                    for i in range(2 * NG):
                        last = nc.tensor.transpose(q_ps[:, i, :], xs[:, n.batch, 4 * i:4 * i + 4, :, :].rearrange("p h s d -> p (h s d)"),
                                                   eye16_sb[:, :])
                    last.then_inc(TQ.sem, 1)
                if l3.exists:
                    Y2.wait(pe, l3)
                    RP.wait(pe, n, 3)
                    VB.wait(pe, n)
                    ZG.wait(pe, n)
                    nc.tensor.matmul(p_ps[:, 0:C], ynt[:, :], wo[:, :], start=True, stop=True).then_inc(OP.sem, 1)
                if l4.exists:
                    XT.wait(pe, n)
                    X1T.wait(pe, l4)
                    Y2.wait(pe, l3)
                    nc.tensor.matmul(t_ps[:, 1, 0:8], xn1t[:, l4.batch, :], rw[:, :], start=True, stop=True).then_inc(LM.sem, 1)
                if l1.exists:
                    RED.wait(pe, l1)
                    Y2.wait(pe, l3)
                    for c in range(2):
                        last = nc.tensor.transpose(tb_ps[0:NPAIR, c * P:c * P + P], mneg[:, l1.batch, c, :], eyeb_sb[:, :])
                    last.then_inc(TM.sem, 1)
                if l2.exists:
                    weigh(l2, 2)
                if l2.exists:
                    weigh(l2, 3)

            pipeline(pe, step, 5)

            def transpose_out(n, b):
                C2.wait(pe, n, CHEB2 * (b + 1))
                SE1.wait(pe, *n.at(b - 1, 4))
                AC.wait(pe, n, 1)
                nc.tensor.transpose(t_ps[:, 0, :], oc[:, :], eye_sb[:, :]).then_inc(OT.sem, 1)

            def project_out(n, b):
                OE.wait(pe, n, b + 1)
                nc.tensor.matmul(t_ps[:, 1, :], oct_[:, :], w_out[:, :], start=True, stop=True).then_inc(SO.sem, 1)

            def finish(n):
                transpose_out(n, B - 1)
                project_out(n, B - 1)

            def mix(n):
                def up(e, f):
                    GE.wait(pe, *n.at(e * FB + f - 2, E * FB, 2))
                    for i, (a, b) in enumerate(PARTS):
                        last = nc.tensor.matmul(u_ps[f % 2], w16[:, 2 * FB * e + f, a, :], xg16[:, n.parity, b, :],
                                                start=i == 0, stop=i == len(PARTS) - 1)
                    last.then_inc(UP.sem, 1)

                def down(e, b):
                    LO.wait(pe, n, e * FB + FB)
                    if b == 0:
                        AC.wait(pe, *n.at_acc(e - 2))
                    for f in range(FB):
                        for i, (w, x) in enumerate(PARTS):
                            last = nc.tensor.matmul(d_ps[e % 2][:, b, :], hid[e % 2][:, x, f, b * P:b * P + P], w16[:, 2 * FB * e + FB + f, w, :],
                                                    start=f == 0 and i == 0, stop=f == FB - 1 and i == len(PARTS) - 1)
                    if b == B - 1:
                        last.then_inc(DN.sem, 1)

                def task(what, b):
                    if what == "CP":
                        VC.wait(pe, *n.at(b - 1, 4))
                        C1.wait(pe, n if b else n.before(1), CHEB1 * ((b - 1) % B) + 1)
                        nc.tensor.matmul(p_ps[:, 0:3 * C], xg[:, b, :], w_in[:, :], start=True, stop=True).then_inc(CP.sem, 1)
                    if what == "CS":
                        C1.wait(pe, n, CHEB1 * (b + 1))
                        C2.wait(pe, *n.at(b - 1, 4, CHEB2))
                        CL.wait(pe, *n.at(b - 1, 4))
                        nc.tensor.matmul(cc_ps[0][:, 0:3 * SW], tri_sb[:, :], kv[:, b % 2, 0:3 * SW], start=True, stop=True)
                        nc.tensor.matmul(cc_ps[1][:, 0:2 * SW], tri_sb[:, :], kv[:, b % 2, 3 * SW:5 * SW], start=True, stop=True).then_inc(CS.sem, 1)
                    if what == "OT":
                        transpose_out(n, b)
                    if what == "SO":
                        project_out(n, b)

                XG.wait(pe, n, 3)
                task("CP", 0)
                up(0, 0)
                up(0, 1)
                if not n.first:
                    finish(n.before(1))
                up(0, 2)
                up(0, 3)
                XG.wait(pe, n)
                SE1.wait(pe, n.before(1))
                for b in range(B):
                    last = nc.tensor.transpose(t_ps[0:E, b, :], cwg[:, b, :], eye_sb[:, :])
                last.then_inc(CW.sem, 1)
                for e in range(E):
                    for half, block in MIX:
                        if half == "up" and e + 1 < E:
                            up(e + 1, block)
                        if half == "down":
                            down(e, block)
                        if e == 0 and half == "up" and block == BIAS_AT:
                            CT.wait(pe, n)
                            for b in range(B):
                                last = nc.tensor.matmul(t_ps[:, b, :], cwt[:, b, :], b2_sb[:, :], start=True, stop=True)
                            last.then_inc(CW.sem, 1)
                        for what, b in SLOTS[e] if (half, block) == TASKS_AT else []:
                            task(what, b)

            pe.wait_ge(s_w2, 16 * 8)
            WS.wait(pe, Tile(TAUS, 0))
            LG.wait(pe, Tile(TAUS, 0))
            rounds(pe, mix)
            finish(Round(TAUS - 1))

        @block.vector
        def _(dve):
            nc.vector.memset(ones_sb[:, :], 1.0).then_inc(s_zero, 1)
            nc.vector.memset(half_sb[:, :], -0.5)
            nc.vector.memset(carry[:, :, :], 0.0)
            nc.vector.memset(xs[:, :, :, :, :], 0.0)
            nc.vector.memset(kt[:, :, :, :], 0.0)
            nc.vector.memset(mm_sb[:, :, :], 0.0).then_inc(s_zero, 1)
            nc.vector.memset(hide_sb[:, :, :], NEG).then_inc(s_zero, 1)
            nc.vector.memset(vd[:, :, :, :, :], 0.0).then_inc(s_zero, 1)
            dve.wait_ge(s_zero, 4)
            nc.vector.memset(vd[0:W, :, :, :, 8:9], 1.0)
            nc.vector.memset(vd[W:P, :, :, :, 17:18], 1.0).then_inc(s_zero, 1)
            dve.wait_ge(s_w, 16 * 9)
            nc.vector.tensor_reduce(wsum[:, 0:1], wraw[:, :], AX.X, ALU.add, apply_absolute_value=True).then_inc(s_init, 1)
            dve.wait_ge(s_ps, 1)
            nc.vector.tensor_scalar(wsum[:, 1:2], t_ps[:, 0, 0:1], 1.0 / (C * C), 0.7, ALU.mult, ALU.mult).then_inc(s_init, 1)
            dve.wait_ge(s_init, 2)
            nc.vector.tensor_scalar(wneg[:, :], wraw[:, :], -1.0, wsum[:, 1:2], ALU.mult, ALU.is_gt).then_inc(s_init, 1)
            dve.wait_ge(s_init, 3)
            nc.vector.scalar_tensor_tensor(wneg[:, :], wraw[:, :], wsum[:, 1:2], wneg[:, :], ALU.is_gt, ALU.subtract).then_inc(s_init, 1)
            dve.wait_ge(s_init, 4)
            nc.vector.tensor_scalar(wp[:, 3 * C:4 * C], wneg[:, :], alpha_sb[:, 0:1], None, ALU.mult).then_inc(s_init, 1)

            def maxima(n, j):
                MX.wait(dve, n, j + 1)
                TM.wait(dve, n.before(4))
                nc.vector.tensor_reduce(mneg[:, n.batch, j // 2, (j % 2) * NG:(j % 2) * NG + NG], m_ps[j % 2][:, :, :],
                                        AX.X, ALU.max, negate=True).then_inc(RED.sem, 1)

            def step(head):
                n, l1, l3, l4 = (head.before(i) for i in (1, 2, 4, 5))
                if l4.exists:
                    R1.wait(dve, l4)
                    nc.vector.tensor_scalar(xn1[:, l4.batch, :], xn1[:, l4.batch, :], rstd1[:, l4.batch, 1:2], None,
                                            ALU.mult).then_inc(XN1.sem, 1)
                if l1.exists:
                    maxima(l1, 0)
                if l1.exists:
                    maxima(l1, 1)
                if head.exists:
                    if head.static and head.batch == 0:
                        dve.wait_ge(s_x[head.tau], 16)
                    turn(dve, s_turn_dve)
                    nc.vector.bn_stats(stats[:, head.batch, :], x_all[:, head.index, :]).then_inc(ST.sem, 1)
                    ST.wait(dve, head, 1)
                    R0.wait(dve, head.before(4), 1)
                    turn(dve, s_turn_dve)
                    nc.vector.bn_aggr(mv[:, head.batch, :], stats[:, head.batch, :]).then_inc(ST.sem, 1)
                if n.exists:
                    PR.wait(dve, n)
                    r = n.batch % 2
                    qk = p_ps[:, 0:2 * C].rearrange("p (h e f) -> p h e f", e=2, f=D // 2)
                    ra = rot[:, r, 0, :].rearrange("p (h d) -> p h d", d=D)
                    rbt = rot[:, r, 1, :].rearrange("p (h e f) -> p h e f", e=2, f=D // 2)
                    cos = rope_sb[:, n.tau, 0:D].unsqueeze(1).to_broadcast([P, 2 * H, D])
                    HI.wait(dve, n.before(2))
                    nc.vector.tensor_tensor(ra, p_ps[:, 0:2 * C].rearrange("p (h d) -> p h d", d=D), cos, ALU.mult).then_inc(RP.sem, 1)
                    for e in range(2):
                        sin = rope_sb[:, n.tau, D + 4 * e:D + 4 * e + 4].unsqueeze(1).to_broadcast([P, 2 * H, D // 2])
                        nc.vector.tensor_tensor(rbt[:, :, e, :], qk[:, :, 1 - e, :], sin, ALU.mult).then_inc(RP.sem, 1)
                    GT.wait(dve, n.before(4), 3)
                    nc.vector.tensor_tensor(z[:, n.batch, :], p_ps[:, 3 * C:4 * C], bias0_sb[:, :], ALU.add).then_inc(ZG.sem, 1)
                    RP.wait(dve, n, 3)
                    nc.vector.tensor_tensor(rot[:, r, 0, :], rot[:, r, 0, :], rot[:, r, 1, :], ALU.add).then_inc(RP.sem, 1)
                if l3.exists:
                    TY.wait(dve, l3)
                    T2.wait(dve, l3.before(1))
                    yv = t_ps[:, 2:4, :].rearrange("p j (g w) -> p (j g) w", w=VW)[:, :, 0:18].rearrange("p i (a e) -> p i a e", a=2)
                    nc.vector.reciprocal(rden[:, :].rearrange("p (i a) -> p i a", a=2), yv[:, :, :, 8]).then_inc(YN.sem, 1)
                    YN.wait(dve, l3, 1)
                    nc.vector.tensor_tensor(yn[:, :].rearrange("p (i a d) -> p i a d", a=2, d=D), yv[:, :, :, 0:8],
                                            rden[:, :].rearrange("p (i a) -> p i a", a=2).unsqueeze(3).to_broadcast([P, NPAIR, 2, D]),
                                            ALU.mult).then_inc(YN.sem, 1)
                if l1.exists:
                    maxima(l1, 2)
                if n.exists:
                    HI.wait(dve, n)
                    rv = rot[:, r, 0, :].rearrange("p (h d) -> p h d", d=D)
                    nc.vector.tensor_tensor(xs[:, n.batch, 0:H, 1, :], rv[:, 0:H, :], xs[:, n.batch, 0:H, 0, :], ALU.subtract).then_inc(RP.sem, 1)
                    nc.vector.tensor_tensor(xs[:, n.batch, H:2 * H, 2, :], rv[:, H:2 * H, :], xs[:, n.batch, H:2 * H, 0, :], ALU.subtract).then_inc(RP.sem, 1)
                if l3.exists:
                    EZ.wait(dve, l3)
                    nc.vector.tensor_scalar(gd[:, 0, :], ez[:, :], 1.0, None, ALU.add).then_inc(GT.sem, 1)
                    GT.wait(dve, l3, 1)
                    nc.vector.reciprocal(gd[:, 1, :], gd[:, 0, :]).then_inc(GT.sem, 1)
                    GT.wait(dve, l3, 2)
                    nc.vector.tensor_tensor(gd[:, 2, :], z[:, l3.batch, :], gd[:, 1, :], ALU.mult).then_inc(GT.sem, 1)
                if l1.exists:
                    maxima(l1, 3)
                if l3.exists:
                    OP.wait(dve, l3)
                    GT.wait(dve, l3, 3)
                    nc.vector.tensor_tensor(sg[:, :], p_ps[:, 0:C], gd[:, 2, :], ALU.mult).then_inc(GT.sem, 1)
                    GT.wait(dve, l3, 4)
                    nc.vector.tensor_tensor(x_all[:, l3.index, :], x_all[:, l3.index, :], sg[:, :], ALU.add).then_inc(GT.sem, 1)
                    GT.wait(dve, l3, 5)
                    turn(dve, s_turn_dve)
                    nc.vector.bn_stats(stats1[:, l3.batch, :], x_all[:, l3.index, :]).then_inc(GT.sem, 1)
                if l1.exists:
                    TM.wait(dve, l1)
                    SE.wait(dve, l1.before(4))
                    if l1.static:
                        dve.wait_ge(s_win, 16 * 8)
                    mt = tb_ps[0:NPAIR, 0:2 * P].rearrange("p (c a q) -> p a c q", c=2, a=2)
                    for a in range(2):
                        nc.vector.tensor_copy(mm_sb[W + 32 * a:W + 32 * a + NPAIR, l1.batch, :].rearrange("p (r c q) -> p r c q", r=2, c=2),
                                              mt[:, a, :, :].unsqueeze(1).to_broadcast([NPAIR, 2, 2, W])).then_inc(MMR.sem, 1)
                if l3.exists:
                    GT.wait(dve, l3, 6)
                    turn(dve, s_turn_dve)
                    nc.vector.bn_aggr(mv1[:, l3.batch, :], stats1[:, l3.batch, :]).then_inc(GT.sem, 1)
                    GT.wait(dve, l3, 7)
                    SX.wait(dve, l3.before(4))
                    TX1.wait(dve, l3.before(4))
                    nc.vector.tensor_scalar(xn1[:, l3.batch, :].rearrange("p (b a) -> p a b", b=IL), x_all[:, l3.index, :].rearrange("p (a b) -> p a b", b=IL), mv1[:, l3.batch, 0:1], None, ALU.subtract).then_inc(GT.sem, 1)
                    GT.wait(dve, l3, 8)
                    nc.vector.tensor_tensor(sg[:, :], xn1[:, l3.batch, :], xn1[:, l3.batch, :], ALU.mult).then_inc(GT.sem, 1)
                    GT.wait(dve, l3, 9)
                    nc.vector.tensor_reduce(mv1[:, l3.batch, 1:2], sg[:, :], AX.X, ALU.add).then_inc(GT.sem, 1)
                if head.exists:
                    R0.wait(dve, head)
                    TX.wait(dve, head.before(4))
                    nc.vector.tensor_scalar(xn[:, head.batch, :], x_all[:, head.index, :], mv[:, head.batch, 0:1], rstd[:, head.batch, 1:2],
                                            ALU.subtract, ALU.mult).then_inc(XN.sem, 1)
                if l4.exists:
                    LM.wait(dve, l4)
                    TM.wait(dve, l1)
                    nc.vector.tensor_tensor(logits[:, l4.index, :], t_ps[:, 1, 0:8], rb[:, :], ALU.add).then_inc(LG.sem, 1)

            for n in range(8):
                step(Tile(0, n))
            dve.wait_ge(s_x[2], 16 * (TAUS - 2))
            with dve.Fori(2, TAUS) as t:
                for k in range(4):
                    step(Tile(t, k))
            for n in range(5):
                step(Tile(TAUS, n))

            route = [0]

            def link(ins):
                route[0] += 1
                ins.then_inc(s_cw, 1)
                dve.wait_ge(s_cw, route[0])

            def wide(ap):
                return ap.unsqueeze(2).to_broadcast([P, NT, E])

            LG.wait(dve, Tile(TAUS, 0))
            dve.wait_ge(s_w2, 16 * 8)
            left = logits[:, :, :]
            for k in range(2):
                link(nc.vector.tensor_reduce(rs[:, 2 * k, :], left, AX.X, ALU.max))
                link(nc.vector.tensor_tensor(rt[:, 0, :, :], left, wide(rs[:, 2 * k, :]), ALU.is_equal))
                link(nc.vector.tensor_tensor(rt[:, 1, :, :], rt[:, 0, :, :], desc_sb[:, :].unsqueeze(1).to_broadcast([P, NT, E]), ALU.mult))
                link(nc.vector.tensor_reduce(rs[:, 1, :], rt[:, 1, :, :], AX.X, ALU.max))
                link(nc.vector.tensor_tensor(rt[:, 2 + k, :, :], rt[:, 1, :, :], wide(rs[:, 1, :]), ALU.is_equal))
                if k == 0:
                    link(nc.vector.scalar_tensor_tensor(rt[:, 4, :, :], rt[:, 2, :, :], -3e38, logits[:, :, :], ALU.mult, ALU.add))
                    left = rt[:, 4, :, :]
                    link(nc.vector.tensor_reduce(rs[:, 3, :], left, AX.X, ALU.max))
                    link(nc.vector.tensor_tensor(rs[:, 4, :], rs[:, 3, :], rs[:, 0, :], ALU.subtract))
            dve.wait_ge(s_we, 1)
            link(nc.vector.tensor_scalar(rs[:, 6, :], rs[:, 5, :], 1.0, None, ALU.add))
            link(nc.vector.reciprocal(rs[:, 7, :], rs[:, 6, :]))
            link(nc.vector.tensor_tensor(rs[:, 6, :], rs[:, 5, :], rs[:, 7, :], ALU.mult))
            link(nc.vector.tensor_tensor(rt[:, 2, :, :], rt[:, 2, :, :], wide(rs[:, 7, :]), ALU.mult))
            link(nc.vector.tensor_tensor(rt[:, 3, :, :], rt[:, 3, :, :], wide(rs[:, 6, :]), ALU.mult))
            link(nc.vector.tensor_tensor(cw[:, :, :], rt[:, 2, :, :], rt[:, 3, :, :], ALU.add))
            link(nc.vector.memset(eps2_sb[:, :], 1e-12))
            assert route[0] == ROUTE

            def final_step(n, at, ins, wait=True):
                ins.then_inc(F1.sem, 1)
                if wait:
                    F1.wait(dve, n, at)

            def normalise(n):
                AC.wait(dve, n)
                for b in range(B):
                    final_step(n, b + 1, nc.vector.bn_stats(stats2[:, b, :], acc[:, b, :]), b == B - 1)
                for b in range(B):
                    turn(dve, s_turn_dve)
                    final_step(n, B + b + 1, nc.vector.bn_aggr(mv2[:, b, :], stats2[:, b, :]), False)
                R2.wait(dve, n)
                GA.wait(dve, n.before(1))
                for b in range(B):
                    final_step(n, 2 * B + b + 1, nc.vector.tensor_scalar(y2[:, b, :], acc[:, b, :], mv2[:, b, 0:1], rstd2[:, 1, b:b + 1],
                                                                         ALU.subtract, ALU.mult), b == B - 1)
                final_step(n, 13, nc.vector.tensor_tensor(y2[:, :, :], y2[:, :, :], lnw_sb[:, :].unsqueeze(1).to_broadcast([P, B, C]), ALU.mult))
                final_step(n, 14, nc.vector.tensor_tensor(y2[:, :, :], y2[:, :, :], lnb_sb[:, :].unsqueeze(1).to_broadcast([P, B, C]), ALU.add))

            def gate(n):
                EX2.wait(dve, n)
                GA.wait(dve, n, 1)
                final_step(n, 15, nc.vector.scalar_tensor_tensor(e2[:, :, :], e2[:, :, :], 1.0, res[:, :, :], ALU.add, ALU.mult), False)

            def mix(n):
                def cheb_keys(b):
                    at = [CHEB1 * b]

                    def done(ins, wait=True):
                        at[0] += 1
                        ins.then_inc(C1.sem, 1)
                        if wait:
                            C1.wait(dve, n, at[0])

                    VC.wait(dve, n, b + 1)
                    x = tc[:, 0, :]
                    done(nc.vector.tensor_scalar(xc[:, :], p_ps[:, 0:2 * C], INV, CLIP, ALU.mult, ALU.min))
                    done(nc.vector.tensor_scalar(x, xc[:, :], -CLIP, None, ALU.max))
                    done(nc.vector.scalar_tensor_tensor(xc[:, :], x, 2.0, x, ALU.mult, ALU.mult))
                    done(nc.vector.tensor_scalar(tc[:, 1, :], xc[:, :], 1.0, None, ALU.subtract))
                    for j in range(2, ORD):
                        done(nc.vector.scalar_tensor_tensor(xc[:, :], x, 2.0, tc[:, j - 1, :], ALU.mult, ALU.mult))
                        done(nc.vector.tensor_tensor(tc[:, j, :], xc[:, :], tc[:, j - 2, :], ALU.subtract))
                    CS.wait(dve, *n.at(b - 2, 4))
                    kvb = kv[:, b % 2, :].rearrange("p (j w) -> p j w", w=SW)
                    done(nc.vector.tensor_tensor(kvb[:, :, 0:C], tc[:, :, C:2 * C], vs[:, b % 2, :].unsqueeze(1).to_broadcast([P, ORD, C]), ALU.mult), False)
                    done(nc.vector.tensor_reduce(kvb[:, :, C:SW], tc[:, :, C:2 * C].rearrange("p j (h d) -> p j h d", d=D), AX.X, ALU.add), False)
                    done(nc.vector.tensor_reduce(tq[:, :, C:SW], tc[:, :, 0:C].rearrange("p j (h d) -> p j h d", d=D), AX.X, ALU.add))
                    n.wait_dma(dve, s_carry[b])
                    done(nc.vector.tensor_tensor(kv[0:1, b % 2, :], kv[0:1, b % 2, :], carry[0:1, b, :], ALU.add), False)
                    assert at[0] == CHEB1 * (b + 1)

                def cheb_out(b):
                    at = [CHEB2 * b]

                    def done(ins, wait=True):
                        at[0] += 1
                        ins.then_inc(C2.sem, 1)
                        if wait:
                            C2.wait(dve, n, at[0])

                    CS.wait(dve, n, b + 1)
                    CL.wait(dve, n, b + 1)
                    c0 = cc_ps[0][:, 0:3 * SW].rearrange("p (j w) -> p j w", w=SW)
                    c1 = cc_ps[1][:, 0:2 * SW].rearrange("p (j w) -> p j w", w=SW)
                    done(nc.vector.tensor_tensor(pr[:, 0:3, 0:C], tc[:, 0:3, 0:C], c0[:, :, 0:C], ALU.mult), False)
                    done(nc.vector.tensor_tensor(pr[:, 0:3, C:SW], tq[:, 0:3, C:SW], c0[:, :, C:SW], ALU.mult), False)
                    done(nc.vector.tensor_tensor(pr[:, 3:5, 0:C], tc[:, 3:5, 0:C], c1[:, :, 0:C], ALU.mult), False)
                    done(nc.vector.tensor_tensor(pr[:, 3:5, C:SW], tq[:, 3:5, C:SW], c1[:, :, C:SW], ALU.mult))
                    done(nc.vector.tensor_scalar(nd[:, :], pr[:, 0, :], BETA[0], None, ALU.mult))
                    for j in range(1, ORD):
                        done(nc.vector.scalar_tensor_tensor(nd[:, :], pr[:, j, :], BETA[j], nd[:, :], ALU.mult, ALU.add))
                    done(nc.vector.tensor_scalar(dn[:, 0, :], nd[:, C:SW], 1e-7, None, ALU.add))
                    done(nc.vector.reciprocal(dn[:, 1, :], dn[:, 0, :]))
                    OT.wait(dve, *n.at(b - 1, 4))
                    done(nc.vector.tensor_tensor(oc[:, :].rearrange("p (h d) -> p h d", d=D), nd[:, 0:C].rearrange("p (h d) -> p h d", d=D),
                                                 dn[:, 1, :].unsqueeze(2).to_broadcast([P, H, D]), ALU.mult))
                    assert at[0] == CHEB2 * (b + 1)

                def accumulate(e):
                    DN.wait(dve, n, e + 1)
                    for b in range(B):
                        AC.wait(dve, n, 1 if e == 0 else 1 + 4 * (e - 1) + b + 1)
                        nc.vector.scalar_tensor_tensor(acc[:, b, :], d_ps[e % 2][:, b, :], cwg[:, b, e:e + 1], acc[:, b, :],
                                                       ALU.mult, ALU.add).then_inc(AC.sem, 1)

                def residual():
                    CW.wait(dve, n, 2)
                    F1.wait(dve, n.before(1), 12)
                    nc.vector.tensor_tensor(acc[:, :, :], xn1_all[:, n.tiles, :], t_ps[:, :, :], ALU.add).then_inc(AC.sem, 1)

                for what, i in DVE_ORDER:
                    if what == "keys":
                        cheb_keys(i)
                    elif what == "residual":
                        residual()
                    elif what == "sum":
                        accumulate(i)
                    elif what == "out":
                        cheb_out(i)
                    elif what == "gate" and not n.first:
                        gate(n.before(1))
                normalise(n)

            rounds(dve, mix)
            gate(Round(TAUS - 1))


def constants():
    import numpy as np
    inv = (1.0 / np.float32(10000.0) ** (np.arange(0, D, 2, dtype=np.float32) / np.float32(D))).astype(np.float32)
    ang = np.outer(np.arange(T, dtype=np.float32), inv).astype(np.float32)
    cos, sin = np.cos(ang), np.sin(ang)
    rope = np.concatenate([cos, cos, sin, -sin], 1).astype(np.float32).reshape(TAUS, P, 2 * D).transpose(1, 0, 2)
    q, k = np.arange(W)[:, None], np.arange(W)[None, :]
    before, own = np.where(k >= q, 0, NEG), np.where(k <= q, 0, NEG)
    win_max = np.tile(np.concatenate([before, own], 1)[:, None, :], (2, NG, 1))
    win_exp = np.concatenate([own.T, before.T, before.T, own.T], 1)
    sel = np.zeros((P, NPAIR, P))
    for r in range(W):
        sel[r, :, r] = sel[r, :, W + r] = 1
    for i in range(NPAIR):
        sel[W + i, i, 0:W] = sel[W + 32 + i, i, W:P] = 1
    f = np.float32
    return {"rope": np.ascontiguousarray(rope), "eye": np.eye(P, dtype=f), "win_max": win_max.astype(f),
            "win_exp": win_exp.astype(f), "pair_sel": sel.astype(f),
            "tri": np.triu(np.ones((P, P), f)), "descend": np.tile(np.arange(E, 0, -1).astype(f), (P, 1))}


def kernel(L0_attn_x, L0_attn_w_attn, L0_attn_w_proj, L0_ffn_weight, L0_ffn_alpha, L0_ffn_bias, L1_attn_W_in,
           L1_attn_W_out, L1_ffn_router_w, L1_ffn_router_b, L1_ffn_w1, L1_ffn_b1, L1_ffn_w2, L1_ffn_b2, L1_ffn_ln_w,
           L1_ffn_ln_b):
    import numpy as np
    import concourse.bacc as bacc
    from concourse.bass_utils import run_bass_kernel_spmd

    order = [(4 * g + 2 * jp + a) * D + d for jp in range(2) for g in range(NG) for a in range(2) for d in range(D)]
    w_attn = np.asarray(L0_attn_w_attn)

    runs = np.arange(C).reshape(-1, IL).T.reshape(-1)

    w1 = np.asarray(L1_ffn_w1).transpose(2, 0, 1)[runs].reshape(P, E, FB, P)
    w2 = np.asarray(L1_ffn_w2).reshape(E, C, FB, P).transpose(3, 0, 2, 1)

    def rows(a):
        return np.tile(np.asarray(a)[None, :], (P, 1))

    arrays = {
        "x": np.asarray(L0_attn_x),
        "proj_w": np.concatenate([w_attn[0:2 * C], w_attn[2 * C:3 * C][order]]).T,
        "ffn_w": np.asarray(L0_ffn_weight).T,
        "alpha": rows(L0_ffn_alpha),
        "bias0": rows(L0_ffn_bias),
        "out_w": np.asarray(L0_attn_w_proj).T[order],
        "router_w": np.asarray(L1_ffn_router_w).T[runs],
        "router_b": rows(L1_ffn_router_b),
        "cheb_w": np.asarray(L1_attn_W_in).T[runs],
        "cheb_out_w": np.asarray(L1_attn_W_out).T,
        "experts_w": np.concatenate([w1, w2], 2).reshape(P, 2 * E * FB, P),
        "b1": np.asarray(L1_ffn_b1).reshape(E, FB, P).transpose(2, 0, 1),
        "b2": np.asarray(L1_ffn_b2),
        "ln_w": rows(L1_ffn_ln_w),
        "ln_b": rows(L1_ffn_ln_b),
        **constants(),
    }
    nc = bacc.Bacc("TRN2", target_bir_lowering=False, num_devices=1)
    given, args = {}, {}
    for name, a in arrays.items():
        given[f"in_{name}"] = a = np.ascontiguousarray(a)
        args[name] = nc.dram_tensor(f"in_{name}", a.shape, mybir.dt.from_np(a.dtype), kind="ExternalInput").ap()
    args["out"] = nc.dram_tensor("out_0", (B, T, C), F32, kind="ExternalOutput").ap()
    program(nc, **args)
    return run_bass_kernel_spmd(nc, [given], core_ids=[0]).results[0]["out_0"]
```

```python
from contextlib import ExitStack

import concourse.bass as bass
import numpy as np
from concourse import mybir

F32 = mybir.dt.float32
F16 = mybir.dt.float16
BF16 = mybir.dt.bfloat16
ALU = mybir.AluOpType
ACT = mybir.ActivationFunctionType
AX = mybir.AxisListType

P = 128
B, T, C = 4, 1024, 128
NT = B * T // P
TAUS = T // P
H, D = 16, 8
W = 64
NG = 4
NPAIR = H // 2
VW = 32
EPS0 = 1e-5
IL = 4
NEG = -1e30

ORD = 5
SW = C + H
E, FF = 8, 512
FB = FF // P
CHEB1, CHEB2 = 13, 5
ROUTE = 20
_ALPHA = np.arange(1, ORD + 2, dtype=np.float32) ** -1.5
_BETA = np.cumsum(_ALPHA[::-1])[::-1][1:].astype(np.float32)
BETA = [float(v) for v in _BETA / _BETA.sum()]
INV = float(D) ** -0.5
CLIP = 1.0 - 1e-6
PARTS = [(0, 0), (1, 0), (0, 1)]
MIX = [("up", 0), ("down", 0), ("up", 1), ("down", 1), ("up", 2), ("down", 2), ("up", 3), ("down", 3)]
TASKS_AT = ("down", 3)
WEIGHTS_AT, BIAS_AT = 1, 3
POOL_ORDER = [("low", 0), ("deviation", 0), ("low", 1), ("gate", 0), ("low", 2), ("result", 0), ("low", 3),
              ("low", 4), ("low", 5), ("low", 6), ("low", 7), ("parts", 0), ("gather", 0)]
SLOTS = [[], [("sums", 0), ("project", 1)], [("transpose", 0)], [("project_out", 0), ("sums", 1),
         ("project", 2)], [("transpose", 1)], [("project_out", 1), ("sums", 2), ("project", 3)],
         [("transpose", 2), ("project_out", 2)], [("sums", 3)]]
DVE_ORDER = [("keys", 0), ("residual", 0), ("sum", 0), ("gate", 0), ("sum", 1), ("out", 0), ("keys", 1),
             ("sum", 2), ("sum", 3), ("out", 1), ("keys", 2), ("sum", 4), ("sum", 5), ("out", 2), ("keys", 3),
             ("sum", 6), ("sum", 7), ("out", 3)]


class Tile:

    def __init__(self, t, m):
        self.static = isinstance(t, int)
        if self.static:
            t, m = (4 * t + m) // 4, (4 * t + m) % 4
        self.t, self.m = t, m
        self.batch = m % 4
        self.tau = t + m // 4
        self.index = t * 4 + m
        self.exists = not self.static or 0 <= self.index < NT
        self.first = self.static and self.tau == 0

    def before(self, lag):
        return Tile(self.t, self.m - lag)

    def count(self, per, k):
        return self.t * (4 * per) + (self.m * per + k)


class Stage:

    def __init__(self, sem, per=1):
        self.sem, self.per = sem, per

    def wait(self, engine, tile, k=None):
        if tile.static and tile.index < 0:
            return
        k = self.per if k is None else k
        if tile.static and tile.index >= NT:
            tile, k = Tile(TAUS - 1, 3), self.per
        engine.wait_ge(self.sem, tile.count(self.per, k))


def pipeline(engine, step, lags):
    for n in range(8):
        step(Tile(0, n))
    with engine.Fori(2, TAUS) as t:
        for k in range(4):
            step(Tile(t, k))
    for n in range(lags):
        step(Tile(TAUS, n))


class Round:

    def __init__(self, t, parity=0):
        self.static = isinstance(t, int)
        self.t, self.index, self.tiles = t, t, bass.ts(t, B)
        self.first = self.static and t == 0
        self.last = self.static and t == TAUS - 1
        self.parity = t % 2 if self.static else parity

    def before(self, rounds):
        return Round(self.t - rounds, (self.parity - rounds) % 2)

    def count(self, per, k):
        return self.t * per + k

    def at(self, i, items, each=1):
        return (self, (i + 1) * each) if i >= 0 else (self.before(1), (i + items + 1) * each)

    def at_acc(self, e):
        return (self, 1 + B * (e + 1)) if e >= 0 else (self.before(1), 1 + B * (e + E + 1))

    def wait_dma(self, engine, sem):
        if not self.first:
            engine.wait_ge(sem, self.t * 16)

    def wait_carry(self, engine, sems, b):
        if b >= 0:
            engine.wait_ge(sems[b], self.t * 16 + 16)
        else:
            self.wait_dma(engine, sems[b + B])


def rounds(engine, mix, buffers=2):
    mix(Round(0))
    if buffers == 1:
        with engine.Fori(1, TAUS) as t:
            mix(Round(t))
        return
    with engine.Fori(0, TAUS // 2 - 1) as t:
        mix(Round(t * 2 + 1, 1))
        mix(Round(t * 2 + 2, 0))
    mix(Round(TAUS - 1))


def turn(engine, sem):
    engine.sem_inc(sem, 1)


def program(nc, x, proj_w, ffn_w, alpha, bias0, out_w, rope, eye, win_max, win_exp, pair_sel,
            router_w, router_b, cheb_w, cheb_out_w, tri, descend, experts_w, b1, b2, ln_w, ln_b, out):
    ctx = ExitStack()
    with ctx:
        def sb(name, shape, dt=F32):
            return ctx.enter_context(nc.sbuf_tensor(name, shape, dt))

        def bank(name, shape, dt=F32):
            return ctx.enter_context(nc.psum_tensor(name, shape, dt))

        def sem(name):
            return ctx.enter_context(nc.semaphore(name))

        def stage(name, per=1):
            return Stage(sem(name), per)

        x_all = sb("x_all", [P, NT, C])
        xn1_all = sb("xn1_all", [P, NT, C])
        xn1t_all = sb("xn1t_all", [P, NT, P])
        logits = sb("logits", [P, NT, 8])

        wp = sb("wp", [P, 3 * C + C])
        wraw = sb("wraw", [P, C])
        wneg = sb("wneg", [P, C])
        wsum = sb("wsum", [P, 2])
        alpha_sb = sb("alpha_sb", [P, 1])
        bias0_sb = sb("bias0_sb", [P, C])
        wo = sb("wo", [P, C])
        rope_sb = sb("rope_sb", [P, TAUS, 2 * D])
        eye_sb = sb("eye_sb", [P, P])
        eye16_sb = sb("eye16_sb", [P, P], F16)
        eyeb_sb = sb("eyeb_sb", [P, P], BF16)
        ones_sb = sb("ones_sb", [P, P])
        winm_sb = sb("winm_sb", [P, NG, P], BF16)
        mm_sb = sb("mm_sb", [P, 4, 2 * P], BF16)
        hide_sb = sb("hide_sb", [P, NG, W], BF16)
        pair_sb = sb("pair_sb", [P, NPAIR, P], BF16)
        rw = sb("rw", [P, 8])
        rb = sb("rb", [P, 8])
        half_sb = sb("half_sb", [P, 1])

        stats = sb("stats", [P, 4, 6])
        mv = sb("mv", [P, 4, 2])
        rstd = sb("rstd", [P, 4, 2])
        xn = sb("xn", [P, 4, C])
        xnt = sb("xnt", [P, 4, P])
        rot = sb("rot", [P, 2, 2, 2 * C])
        xs = sb("xs", [P, 4, 2 * H, 4, D], F16)
        qt = sb("qt", [P, 4, NG, P], F16)
        kt = sb("kt", [P, 4, NG, W + P], F16)
        vd = sb("vd", [P, 4, 3, NPAIR, VW])
        mneg = sb("mneg", [P, 4, 2, NPAIR], BF16)
        pexp = sb("pexp", [P, 4, 2, 2 * P])
        yts = sb("yts", [P, 2 * P])
        rden = sb("rden", [P, H])
        yn = sb("yn", [P, C])
        ynt = sb("ynt", [P, P])
        z = sb("z", [P, 4, C])
        ez = sb("ez", [P, C])
        gd = sb("gd", [P, 3, C])
        sg = sb("sg", [P, C])
        stats1 = sb("stats1", [P, 4, 6])
        mv1 = sb("mv1", [P, 4, 2])
        rstd1 = sb("rstd1", [P, 4, 2])
        xn1 = sb("xn1", [P, 4, C])
        xn1t = sb("xn1t", [P, 4, P])

        w_in = sb("w_in", [P, 3 * C])
        w_out = sb("w_out", [P, C])
        tri_sb = sb("tri_sb", [P, P])
        desc_sb = sb("desc_sb", [P, E])
        experts_sb = sb("experts_sb", [P, 2 * E * FB, P])
        split_sb = sb("split_sb", [P, 2, 2, P], F16)
        b1_sb = sb("b1_sb", [P, E, FB])
        b2_sb = sb("b2_sb", [E, C])
        lnw_sb = sb("lnw_sb", [P, C])
        lnb_sb = sb("lnb_sb", [P, C])
        cw = sb("cw", [P, NT, E])
        rt = sb("rt", [P, 5, NT, E])
        rs = sb("rs", [P, 8, NT])
        xg = sb("xg", [P, B, P])
        xg16 = sb("xg16", [P, 2, 2, B * P], F16)
        cwg = sb("cwg", [P, B, E])
        cwt = sb("cwt", [E, B, P])
        vs = sb("vs", [P, 2, SW])
        xc = sb("xc", [P, 2 * C])
        kv = sb("kv", [P, 2, ORD * SW])
        pr = sb("pr", [P, ORD, SW])
        nd = sb("nd", [P, SW])
        dn = sb("dn", [P, 2, H])
        oc = sb("oc", [P, C])
        oct_ = sb("oct", [P, P])
        s1 = sb("s1", [P, B, C])
        last_sb = sb("last_sb", [P, 2, ORD * SW])
        carry = sb("carry", [1, B, ORD * SW])
        stats2 = sb("stats2", [P, B, 6])
        mv2 = sb("mv2", [P, B, 2])
        rstd2 = sb("rstd2", [P, 2, B])
        eps2_sb = sb("eps2_sb", [P, B])

        m_ps = [bank(f"m_ps{i}", [P, NG, P]) for i in range(2)]
        e_ps = [bank(f"e_ps{i}", [P, 2, 2 * P]) for i in range(2)]
        p_ps = bank("p_ps", [P, 4 * C])
        q_ps = bank("q_ps", [P, 2 * NG, P], F16)
        t_ps = bank("t_ps", [P, 4, P])
        y_ps = bank("y_ps", [P, 4, P])
        tb_ps = t_ps[:, :, :].rearrange("p a b -> p (a b)").bitcast(BF16)

        y2, e2, res, acc = (xs[:, i, :, :, :].rearrange("p h s d -> p (h s d)").bitcast(F32).rearrange("p (b c) -> p b c", b=B)
                            for i in range(4))
        tc = kt[:, :, :, :].rearrange("p b g t -> p (b g t)").bitcast(F32)[:, 0:ORD * 2 * SW].rearrange("p (j a w) -> p j a w", j=ORD, a=2)
        hid = [pexp[:, :, :, :].rearrange("p j a b -> p (j a b)"),
               vd[:, :, :, :, :].rearrange("p a b i w -> p (a b i w)")[:, 0:FB * B * P]]
        hid = [a.bitcast(F16).rearrange("p (s f t) -> p s f t", s=2, f=FB) for a in hid]
        gel = [rot[:, i, :, :].rearrange("p a b -> p (a b)") for i in range(2)] + \
              [qt[:, 2 * i:2 * i + 2, :, :].rearrange("p b g t -> p (b g t)").bitcast(F32) for i in range(2)]
        w16 = experts_sb[:, :, :].bitcast(F16).rearrange("p k (s c) -> p k s c", s=2)
        u_ps = [m_ps[i][:, :, :].rearrange("p a b -> p (a b)") for i in range(2)]
        d_ps = [e_ps[i][:, :, :].rearrange("p a (h b) -> p (a h) b", b=P) for i in range(2)]
        cc_ps = [y_ps[:, :, :].rearrange("p a b -> p (a b)"), q_ps[:, :, :].rearrange("p a b -> p (a b)").bitcast(F32)]

        s_carry = [sem(f"s_carry{b}") for b in range(B)]
        s_out = sem("s_out")
        s_late_weights = sem("s_late_weights")
        s_route_steps = sem("s_route_steps")
        s_route_exp = sem("s_route_exp")
        s_experts = sem("s_experts")

        s_x = [sem(f"s_x{i}") for i in range(3)]
        s_weights = sem("s_weights")
        s_masks = sem("s_masks")
        s_cleared = sem("s_cleared")
        s_values_cleared = sem("s_values_cleared")
        s_ternary_steps = sem("s_ternary_steps")
        s_abs_summed = sem("s_abs_summed")
        s_turn_pool, s_turn_dve = sem("s_turn_pool"), sem("s_turn_dve")

        xn_transposed = stage("xn_transposed")
        projected = stage("projected")
        qk_transposed = stage("qk_transposed")
        max_scored = stage("max_scored", 4)
        max_transposed = stage("max_transposed")
        scored = stage("scored", 4)
        weighted = stage("weighted", 4)
        y_transposed = stage("y_transposed")
        yn_transposed = stage("yn_transposed")
        out_projected = stage("out_projected")
        xn1_transposed = stage("xn1_transposed")
        routed = stage("routed")
        xnt_copied = stage("xnt_copied")
        high_ready = stage("high_ready")
        values_placed = stage("values_placed", 4)
        qk_copied = stage("qk_copied", 3)
        exp_ready = stage("exp_ready", 4)
        gate_exp_ready = stage("gate_exp_ready")
        yt_copied = stage("yt_copied")
        ynt_copied = stage("ynt_copied")
        xn1t_copied = stage("xn1t_copied")
        stats_ready = stage("stats_ready", 2)
        xn_ready = stage("xn_ready")
        maxima_ready = stage("maxima_ready", 4)
        maxima_placed = stage("maxima_placed", 2)
        rotated = stage("rotated", 6)
        gate_in_ready = stage("gate_in_ready")
        y_normed = stage("y_normed", 2)
        gate_steps = stage("gate_steps", 10)
        xn1_ready = stage("xn1_ready")
        logits_ready = stage("logits_ready")
        rstd_ready = stage("rstd_ready", 2)
        parts_doubled = stage("parts_doubled", 2)
        values_kept = stage("values_kept")
        rstd1_ready = stage("rstd1_ready", 2)
        xn1_stored = stage("xn1_stored", 2)
        weights_split = stage("weights_split", 3)
        cheb_projected = stage("cheb_projected", 4)
        prefix_summed = stage("prefix_summed", 4)
        cheb_transposed = stage("cheb_transposed", 4)
        cheb_out_projected = stage("cheb_out_projected", 4)
        weights_transposed = stage("weights_transposed", 2)
        hidden_ready = stage("hidden_ready", E * FB)
        expert_ready = stage("expert_ready", E)
        v_copied = stage("v_copied", 4)
        gelu_done = stage("gelu_done", 2 * E * FB)
        last_row_copied = stage("last_row_copied", 4)
        prefix_weighted = stage("prefix_weighted", 4)
        cheb_out_copied = stage("cheb_out_copied", 4)
        s1_copied = stage("s1_copied", 4)
        weights_copied = stage("weights_copied")
        tanh_ready = stage("tanh_ready")
        cheb_keys_done = stage("cheb_keys_done", 4 * CHEB1)
        cheb_out_done = stage("cheb_out_done", 4 * CHEB2)
        accumulated = stage("accumulated", 1 + 4 * E)
        norm_steps = stage("norm_steps", 15)
        gathered = stage("gathered", 4)
        low_ready = stage("low_ready", E * FB)
        rstd2_ready = stage("rstd2_ready", 2)
        s1_gated = stage("s1_gated")
        result_ready = stage("result_ready")

        block = ctx.enter_context(nc.Block())

        @block.sync
        def _(sp):
            xv = x.rearrange("b (t p) c -> p t b c", p=P)
            xo = x_all[:, :, :].rearrange("p (t b) c -> p t b c", b=B)
            weights = [(wp[:, 0:3 * C], proj_w), (wraw[:, :], ffn_w), (alpha_sb[:, :], alpha), (bias0_sb[:, :], bias0),
                       (wo[:, :], out_w), (rope_sb[:, :, :], rope), (eye_sb[:, :], eye), (rw[:, :], router_w),
                       (rb[:, :], router_b)]
            sp.dma_start(xo[:, 0, :, :], xv[:, 0, :, :]).then_inc(s_x[0], 16)
            for dst, src in weights:
                sp.dma_start(dst, src).then_inc(s_weights, 16)
            sp.dma_start(xo[:, 1, :, :], xv[:, 1, :, :]).then_inc(s_x[1], 16)
            for t in range(2, TAUS):
                sp.dma_start(xo[:, t, :, :], xv[:, t, :, :]).then_inc(s_x[2], 16)
            for dst, src in [(w_in[:, :], cheb_w), (w_out[:, :], cheb_out_w), (tri_sb[:, :], tri), (desc_sb[:, :], descend),
                             (b1_sb[:, :, :], b1), (b2_sb[:, :], b2),
                             (lnw_sb[:, :], ln_w), (lnb_sb[:, :], ln_b)]:
                sp.dma_start(dst, src).then_inc(s_late_weights, 16)
            for e in range(E):
                k = slice(2 * FB * e, 2 * FB * e + 2 * FB)
                sp.dma_start(experts_sb[:, k, :], experts_w[:, k, :]).then_inc(s_experts, 16)

            def move(n):
                for b in range(B):
                    last_row_copied.wait(sp, n, b + 1)
                    sp.dma_start(carry[0:1, b, :], last_sb[P - 1:P, b % 2, :]).then_inc(s_carry[b], 16)
                result_ready.wait(sp, n)
                sp.dma_start(out.rearrange("b (t p) c -> p t b c", p=P)[:, n.t, :, :], res[:, :, :]).then_inc(s_out, 16)

            rounds(sp, move, buffers=1)
            sp.wait_ge(s_out, 16 * TAUS)

        @block.gpsimd
        def _(pool):
            pool.dma_start(eye16_sb[:, :], eye).then_inc(s_masks, 16)
            pool.dma_start(eyeb_sb[:, :], eye).then_inc(s_masks, 16)
            pool.dma_start(winm_sb[:, :, :], win_max).then_inc(s_masks, 16)
            pool.dma_start(pair_sb[:, :, :], pair_sel).then_inc(s_masks, 16)
            for b in range(4):
                pool.dma_start(mm_sb[0:W, b, :], win_exp).then_inc(s_masks, 16)
            def step(head):
                n, l3, l5 = (head.before(i) for i in (1, 4, 6))
                if l5.exists:
                    xn1_ready.wait(pool, l5)
                    turn(pool, s_turn_pool)
                    nc.gpsimd.tensor_copy(xn1_all[:, l5.index, :].rearrange("p (a b) -> p a b", b=IL), xn1[:, l5.batch, :].rearrange("p (b a) -> p a b", b=IL)).then_inc(xn1_stored.sem, 1)
                    xn1t_copied.wait(pool, l5)
                    turn(pool, s_turn_pool)
                    nc.gpsimd.tensor_copy(xn1t_all[:, l5.index, :], xn1t[:, l5.batch, :]).then_inc(xn1_stored.sem, 1)
                if n.exists:
                    weighted.wait(pool, n.before(4))
                    values_placed.wait(pool, n.before(4))
                    turn(pool, s_turn_pool)
                    nc.gpsimd.tensor_copy(vd[:, n.batch, 0, :, :], vd[:, n.batch, 2, :, :]).then_inc(values_kept.sem, 1)
                    high_ready.wait(pool, n)
                    qk_transposed.wait(pool, n.before(4))
                    turn(pool, s_turn_pool)
                    nc.gpsimd.tensor_copy(xs[:, n.batch, 0:H, 2, :], xs[:, n.batch, 0:H, 0, :]).then_inc(parts_doubled.sem, 1)
                    turn(pool, s_turn_pool)
                    nc.gpsimd.tensor_copy(xs[:, n.batch, H:2 * H, 1, :], xs[:, n.batch, H:2 * H, 0, :]).then_inc(parts_doubled.sem, 1)
                if head.exists:
                    stats_ready.wait(pool, head)
                    turn(pool, s_turn_pool)
                    nc.gpsimd.tensor_scalar(rstd[:, head.batch, 0:1], mv[:, head.batch, 1:2], EPS0, None, ALU.add).then_inc(rstd_ready.sem, 1)
                    rstd_ready.wait(pool, head, 1)
                    nc.gpsimd.tensor_tensor(rstd[:, head.batch, 1:2], rstd[:, head.batch, 0:1], half_sb[:, 0:1], ALU.pow).then_inc(rstd_ready.sem, 1)
                if l3.exists:
                    if l3.static and l3.index == 0:
                        pool.wait_ge(s_experts, 16 * E)
                        nc.gpsimd.memset(carry[:, :, :], 0.0)
                    blocks = bass.ds(l3.index * 2, 2)
                    weights_split.wait(pool, l3.before(1))
                    turn(pool, s_turn_pool)
                    nc.gpsimd.tensor_copy(split_sb[:, :, 0, :], experts_sb[:, blocks, :]).then_inc(weights_split.sem, 1)
                    weights_split.wait(pool, l3, 1)
                    turn(pool, s_turn_pool)
                    nc.gpsimd.tensor_tensor(split_sb[:, :, 1, :], experts_sb[:, blocks, :], split_sb[:, :, 0, :], ALU.subtract).then_inc(weights_split.sem, 1)
                    weights_split.wait(pool, l3, 2)
                    turn(pool, s_turn_pool)
                    nc.gpsimd.tensor_copy(w16[:, blocks, :, :], split_sb[:, :, :, :]).then_inc(weights_split.sem, 1)
                    gate_steps.wait(pool, l3, 10)
                    turn(pool, s_turn_pool)
                    nc.gpsimd.tensor_scalar(rstd1[:, l3.batch, 0:1], mv1[:, l3.batch, 1:2], 1.0 / C, EPS0, ALU.mult, ALU.add).then_inc(rstd1_ready.sem, 1)
                    rstd1_ready.wait(pool, l3, 1)
                    nc.gpsimd.tensor_tensor(rstd1[:, l3.batch, 1:2], rstd1[:, l3.batch, 0:1], half_sb[:, 0:1], ALU.pow).then_inc(rstd1_ready.sem, 1)

            pipeline(pool, step, 6)

            def gate(n):
                norm_steps.wait(pool, n, 14)
                s1_copied.wait(pool, n)
                n.wait_dma(pool, s_out)
                nc.gpsimd.tensor_tensor(res[:, :, :], y2[:, :, :], s1[:, :, :], ALU.mult).then_inc(s1_gated.sem, 1)

            def result(n):
                norm_steps.wait(pool, n)
                turn(pool, s_turn_pool)
                nc.gpsimd.tensor_tensor(res[:, :, :], e2[:, :, :], x_all[:, n.tiles, :], ALU.add).then_inc(result_ready.sem, 1)

            def deviation(n):
                norm_steps.wait(pool, n, 8)
                turn(pool, s_turn_pool)
                nc.gpsimd.tensor_tensor(rstd2[:, 0, :], mv2[:, :, 1], eps2_sb[:, :], ALU.add).then_inc(rstd2_ready.sem, 1)
                rstd2_ready.wait(pool, n, 1)
                nc.gpsimd.tensor_tensor(rstd2[:, 1, :], rstd2[:, 0, :], half_sb[:, 0:1].to_broadcast([P, B]), ALU.pow).then_inc(rstd2_ready.sem, 1)

            def gather_parts(n):
                hidden_ready.wait(pool, n.before(2))
                turn(pool, s_turn_pool)
                nc.gpsimd.tensor_copy(xg16[:, n.parity, 0, :].rearrange("p (b t) -> p b t", b=B), xn1t_all[:, n.tiles, :]).then_inc(gathered.sem, 1)
                gathered.wait(pool, n, 1)
                turn(pool, s_turn_pool)
                nc.gpsimd.tensor_tensor(xg16[:, n.parity, 1, :].rearrange("p (b t) -> p b t", b=B), xn1t_all[:, n.tiles, :],
                                        xg16[:, n.parity, 0, :].rearrange("p (b t) -> p b t", b=B), ALU.subtract).then_inc(gathered.sem, 1)

            def gather(n):
                cheb_projected.wait(pool, n.before(1))
                turn(pool, s_turn_pool)
                nc.gpsimd.tensor_copy(xg[:, :, :], xn1t_all[:, n.tiles, :]).then_inc(gathered.sem, 1)

            def mix(n):
                def low_parts(e):
                    for f in range(FB):
                        i = e * FB + f
                        gelu_done.wait(pool, n, 2 * i + 2)
                        expert_ready.wait(pool, *n.at(e - 2, E))
                        turn(pool, s_turn_pool)
                        nc.gpsimd.tensor_tensor(hid[e % 2][:, 1, f, :], gel[i % 4], hid[e % 2][:, 0, f, :], ALU.subtract).then_inc(low_ready.sem, 1)

                if n.first:
                    gather_parts(n)
                    gather(n)
                weights_transposed.wait(pool, n.before(1), 1)
                accumulated.wait(pool, n.before(1))
                if n.first:
                    pool.wait_ge(s_route_steps, ROUTE)
                turn(pool, s_turn_pool)
                nc.gpsimd.tensor_copy(cwg[:, :, :], cw[:, n.tiles, :]).then_inc(gathered.sem, 1)
                for what, e in POOL_ORDER:
                    if what == "low":
                        low_parts(e)
                    elif what == "parts" and not n.last:
                        gather_parts(n.before(-1))
                    elif what == "gather" and not n.last:
                        gather(n.before(-1))
                    elif what == "deviation" and not n.first:
                        deviation(n.before(1))
                    elif what == "gate" and not n.first:
                        gate(n.before(1))
                    elif what == "result" and not n.first:
                        result(n.before(1))

            pool.wait_ge(xn1_stored.sem, 2 * NT)
            rounds(pool, mix)
            deviation(Round(TAUS - 1))
            gate(Round(TAUS - 1))
            result(Round(TAUS - 1))

        @block.scalar
        def _(act):
            def step(head):
                n, l2, l3, l5 = (head.before(i) for i in (1, 3, 4, 6))

                def exponentials(j):
                    scored.wait(act, l2, j + 1)
                    weighted.wait(act, l2.before(1), j + 1)
                    nc.scalar.activation(pexp[:, j, :, :], e_ps[j % 2][:, :, :], ACT.Exp,
                                         scale=float(D) ** -0.5).then_inc(exp_ready.sem, 1)

                if l3.exists:
                    gate_in_ready.wait(act, l3)
                    gate_steps.wait(act, l3.before(1), 1)
                    nc.scalar.activation(ez[:, :], z[:, l3.batch, :], ACT.Exp, scale=-1.0).then_inc(gate_exp_ready.sem, 1)
                if l2.exists:
                    exponentials(0)
                xn_transposed.wait(act, n)
                if l5.exists:
                    xn1_transposed.wait(act, l5)
                    routed.wait(act, l5.before(2))
                    xn1_stored.wait(act, l5.before(2))
                    nc.scalar.copy(xn1t[:, l5.batch, :], t_ps[:, 0, :]).then_inc(xn1t_copied.sem, 1)
                if n.exists:
                    projected.wait(act, n.before(4))
                    nc.scalar.copy(xnt[:, n.batch, :], t_ps[:, 1, :]).then_inc(xnt_copied.sem, 1)
                if l2.exists:
                    exponentials(1)
                if n.exists:
                    gate_in_ready.wait(act, n)
                    values_kept.wait(act, n)
                    for blk in range(2):
                        for a in range(2):
                            src = p_ps[W * blk:W * blk + W, 2 * C:3 * C].rearrange("p (i a d) -> p i a d", a=2, d=D)
                            nc.scalar.copy(vd[W * a:W * a + W, n.batch, 1 + blk, :, 9 * a:9 * a + D],
                                           src[:, :, a, :]).then_inc(values_placed.sem, 1)
                    rotated.wait(act, n, 4)
                    qk_transposed.wait(act, n.before(4))
                    parts_doubled.wait(act, n.before(4))
                    nc.scalar.copy(xs[:, n.batch, :, 0, :],
                                   rot[:, n.batch % 2, 0, :].rearrange("p (h d) -> p h d", d=D)).then_inc(high_ready.sem, 1)
                if l2.exists:
                    exponentials(2)
                if l3.exists:
                    yn_transposed.wait(act, l3)
                    out_projected.wait(act, l3.before(1))
                    nc.scalar.copy(ynt[:, :], t_ps[:, 3, :]).then_inc(ynt_copied.sem, 1)
                if l2.exists:
                    exponentials(3)
                if n.exists:
                    scored.wait(act, n.before(4))
                    qk_copied.wait(act, n.before(4))
                    nc.scalar.copy(kt[:, n.batch, :, 0:W], kt[:, n.batch, :, P:W + P]).then_inc(qk_copied.sem, 1) if not n.first else \
                        nc.scalar.copy(kt[:, n.batch, :, 0:W], kt[:, n.batch, :, 0:W]).then_inc(qk_copied.sem, 1)
                    qk_transposed.wait(act, n)
                    nc.scalar.copy(qt[:, n.batch, :, :], q_ps[:, 0:NG, :]).then_inc(qk_copied.sem, 1)
                    qk_copied.wait(act, n, 1)
                    nc.scalar.copy(kt[:, n.batch, :, W:W + P], q_ps[:, NG:2 * NG, :]).then_inc(qk_copied.sem, 1)
                if l2.exists:
                    weighted.wait(act, l2)
                    y_transposed.wait(act, l2.before(1))
                    nc.scalar.copy(yts[:, :], y_ps[:, 0:2, :].rearrange("p a b -> p (a b)")).then_inc(yt_copied.sem, 1)

            act.wait_ge(s_cleared, 1)
            nc.scalar.activation(ez[:, 0:1], ones_sb[:, 0:1], ACT.Exp)
            act.wait_ge(s_values_cleared, 2)
            pipeline(act, step, 6)

            act.wait_ge(s_route_steps, 8)
            nc.scalar.activation(rs[:, 5, :], rs[:, 4, :], ACT.Exp).then_inc(s_route_exp, 1)
            act.wait_ge(s_late_weights, 16 * 8)
            weighted.wait(act, Tile(TAUS, 0))
            values_kept.wait(act, Tile(TAUS, 0))

            def oct_copy(n, b):
                cheb_transposed.wait(act, n, b + 1)
                cheb_out_projected.wait(act, *n.at(b - 1, 4))
                nc.scalar.copy(oct_[:, :], t_ps[:, 0, :]).then_inc(cheb_out_copied.sem, 1)

            def s1_copy(n, b):
                cheb_out_projected.wait(act, n, b + 1)
                s1_gated.wait(act, n.before(1))
                nc.scalar.mul(s1[:, b, :], t_ps[:, 1, :], 0.5).then_inc(s1_copied.sem, 1)

            def finish(n):
                oct_copy(n, B - 1)
                s1_copy(n, B - 1)

            def silu_tanh(n):
                norm_steps.wait(act, n, 14)
                result_ready.wait(act, n.before(1))
                nc.scalar.activation(e2[:, :, :], y2[:, :, :], ACT.Tanh, scale=0.5).then_inc(tanh_ready.sem, 1)

            def mix(n):
                def gelus(e, blocks=range(FB)):
                    for f in blocks:
                        hidden_ready.wait(act, n, e * FB + f + 1)
                        low_ready.wait(act, *n.at(e * FB + f - 4, E * FB))
                        nc.scalar.activation(gel[f], u_ps[f % 2], ACT.Gelu, bias=b1_sb[:, e, f:f + 1]).then_inc(gelu_done.sem, 1)
                        expert_ready.wait(act, *n.at(e - 2, E))
                        nc.scalar.activation(hid[e % 2][:, 0, f, :], u_ps[f % 2], ACT.Gelu, bias=b1_sb[:, e, f:f + 1]).then_inc(gelu_done.sem, 1)

                def task(what, b):
                    if what == "project":
                        cheb_projected.wait(act, n, b + 1)
                        cheb_keys_done.wait(act, *n.at(b - 2, 4, CHEB1))
                        nc.scalar.copy(vs[:, b % 2, 0:C], p_ps[:, 2 * C:3 * C]).then_inc(v_copied.sem, 1)
                    if what == "sums":
                        prefix_summed.wait(act, n, b + 1)
                        n.wait_carry(act, s_carry, b - 2)
                        nc.scalar.copy(last_sb[96:P, b % 2, 0:3 * SW], cc_ps[0][96:P, 0:3 * SW])
                        nc.scalar.copy(last_sb[96:P, b % 2, 3 * SW:5 * SW], cc_ps[1][96:P, 0:2 * SW]).then_inc(last_row_copied.sem, 1)
                        cheb_out_done.wait(act, *n.at(b - 1, 4, CHEB2))
                        for j in range(ORD):
                            at = j % 3 * SW
                            last = nc.scalar.mul(pr[:, j, :], cc_ps[j // 3][:, at:at + SW], BETA[j])
                        last.then_inc(prefix_weighted.sem, 1)
                    if what == "transpose":
                        oct_copy(n, b)
                    if what == "project_out":
                        s1_copy(n, b)

                task("project", 0)
                gelus(0)
                if not n.first:
                    finish(n.before(1))
                gelus(1, (0, 1))
                weights_transposed.wait(act, n, 1)
                weights_transposed.wait(act, n.before(1), 2)
                nc.scalar.copy(cwt[:, :, :], t_ps[0:E, :, :]).then_inc(weights_copied.sem, 1)
                gelus(1, (2, 3))
                if not n.first:
                    silu_tanh(n.before(1))
                for e in range(E):
                    if 0 < e < E - 1:
                        gelus(e + 1)
                    for what, b in SLOTS[e]:
                        task(what, b)

            rounds(act, mix)
            finish(Round(TAUS - 1))
            silu_tanh(Round(TAUS - 1))

        @block.tensor
        def _(pe):
            pe.wait_ge(s_ternary_steps, 1)
            pe.wait_ge(s_cleared, 1)
            nc.tensor.matmul(t_ps[:, 0, 0:1], ones_sb[:, :], wsum[:, 0:1], start=True, stop=True).then_inc(s_abs_summed, 1)
            pe.wait_ge(s_ternary_steps, 5)
            pe.wait_ge(s_weights, 16 * 9)

            def max_scores(n, j):
                c, jp = j // 2, j % 2
                ps = m_ps[j % 2]
                qk_copied.wait(pe, n)
                maxima_ready.wait(pe, n.before(1), 3 + j) if j < 2 else maxima_ready.wait(pe, n, j - 1)
                nc.tensor.matmul(ps[:, :, :], eyeb_sb[:, :], winm_sb[:, :, :], start=True, stop=True)
                lo = W if n.first and c == 0 else 0
                if lo:
                    nc.tensor.matmul(ps[:, :, 0:W], eyeb_sb[:, :], hide_sb[:, :, :], start=False, stop=True, skip_group_check=True)
                for g in range(NG):
                    for a in range(2):
                        r = 32 * (2 * jp + a)
                        last = nc.tensor.matmul(ps[W * a:W * a + W, g, lo:P],
                                                qt[r:r + 32, n.batch, g, c * W:c * W + W],
                                                kt[r:r + 32, n.batch, g, c * W + lo:c * W + P],
                                                start=False, stop=True, skip_group_check=True)
                last.then_inc(max_scored.sem, 1)

            def scores(n, j):
                jp, gg = j // 2, j % 2
                ps = e_ps[j % 2]
                maxima_placed.wait(pe, n)
                exp_ready.wait(pe, n.before(1), 3 + j) if j < 2 else exp_ready.wait(pe, n, j - 1)
                for i in range(2):
                    g = 2 * gg + i
                    nc.tensor.matmul(ps[:, i, :], pair_sb[:, jp * NG + g, :], mm_sb[:, n.batch, :],
                                     start=True, stop=True, skip_group_check=True)
                    if n.first:
                        nc.tensor.matmul(ps[:, i, P:P + W], eyeb_sb[:, :], hide_sb[:, 0, :], start=False, stop=True, skip_group_check=True)
                    for a in range(2):
                        r = 32 * (2 * jp + a)
                        o = ps[W * a:W * a + W, i, :]
                        q, k = qt[r:r + 32, n.batch, g, :], kt[r:r + 32, n.batch, g, :]
                        nc.tensor.matmul(o[:, 0:P], k[:, W:2 * W], q[:, 0:P], start=False, stop=True, skip_group_check=True)
                        if not n.first:
                            nc.tensor.matmul(o[:, P:P + W], k[:, 0:W], q[:, 0:W], start=False, stop=True, skip_group_check=True)
                        last = nc.tensor.matmul(o[:, P + W:2 * P], k[:, 2 * W:3 * W], q[:, W:P], start=False, stop=True, skip_group_check=True)
                last.then_inc(scored.sem, 1)

            def weigh(n, j):
                jp, gg = j // 2, j % 2
                exp_ready.wait(pe, n, j + 1)
                values_placed.wait(pe, n)
                yt_copied.wait(pe, n.before(1))
                for part in range(3):
                    for i in range(2):
                        g = 2 * gg + i
                        o = y_ps[VW * g:VW * g + VW, jp, :]
                        v = vd[:, n.batch, :, jp * NG + g, :]
                        w = pexp[:, j, i, :]
                        if part == 0:
                            nc.tensor.matmul(o, v[:, 1, :], w[:, 0:P], start=True, stop=True, skip_group_check=True)
                        elif part == 1:
                            if not n.first:
                                nc.tensor.matmul(o[:, 0:W], v[:, 0, :], w[:, P:P + W], start=False, stop=True, skip_group_check=True)
                        else:
                            last = nc.tensor.matmul(o[:, W:P], v[:, 2, :], w[:, P + W:2 * P], start=False, stop=True, skip_group_check=True)
                last.then_inc(weighted.sem, 1)

            def step(head):
                n, l1, l2, l3, l5 = (head.before(i) for i in (1, 2, 3, 4, 6))
                if l1.exists:
                    max_scores(l1, 0)
                if l2.exists:
                    scores(l2, 0)
                if l1.exists:
                    max_scores(l1, 1)
                logits_ready.wait(pe, l5.before(1))
                maxima_placed.wait(pe, l1.before(1))
                if head.static:
                    ynt_copied.wait(pe, l3.before(1))
                if l5.exists:
                    xn1_ready.wait(pe, l5)
                    nc.tensor.transpose(t_ps[:, 0, :], xn1[:, l5.batch, :], eye_sb[:, :]).then_inc(xn1_transposed.sem, 1)
                if n.exists:
                    xn_ready.wait(pe, n)
                    nc.tensor.transpose(t_ps[:, 1, :], xn[:, n.batch, :], eye_sb[:, :]).then_inc(xn_transposed.sem, 1)
                if l2.exists:
                    weigh(l2, 0)
                if n.exists:
                    xnt_copied.wait(pe, n)
                    gate_steps.wait(pe, l3.before(1), 4)
                    nc.tensor.matmul(p_ps[:, :], xnt[:, n.batch, :], wp[:, :], start=True, stop=True).then_inc(projected.sem, 1)
                if l2.exists:
                    scores(l2, 1)
                xnt_copied.wait(pe, n)
                xn1t_copied.wait(pe, l5)
                if l3.exists:
                    yt_copied.wait(pe, l3)
                    nc.tensor.transpose(t_ps[:, 2, :], yts[:, 0:P], eye_sb[:, :])
                    nc.tensor.transpose(t_ps[:, 3, :], yts[:, P:2 * P], eye_sb[:, :]).then_inc(y_transposed.sem, 1)
                if l1.exists:
                    max_scores(l1, 2)
                if l2.exists:
                    scores(l2, 2)
                    weigh(l2, 1)
                if l3.exists:
                    y_normed.wait(pe, l3)
                    nc.tensor.transpose(t_ps[:, 3, :], yn[:, :], eye_sb[:, :]).then_inc(yn_transposed.sem, 1)
                if l1.exists:
                    max_scores(l1, 3)
                if l2.exists:
                    scores(l2, 3)
                if n.exists:
                    rotated.wait(pe, n)
                    parts_doubled.wait(pe, n)
                    high_ready.wait(pe, n)
                    qk_copied.wait(pe, l1)
                    if n.static and n.index == 0:
                        pe.wait_ge(s_masks, 16 * 8)
                    for i in range(2 * NG):
                        last = nc.tensor.transpose(q_ps[:, i, :], xs[:, n.batch, 4 * i:4 * i + 4, :, :].rearrange("p h s d -> p (h s d)"),
                                                   eye16_sb[:, :])
                    last.then_inc(qk_transposed.sem, 1)
                if l5.exists:
                    xnt_copied.wait(pe, n)
                    xn1t_copied.wait(pe, l5)
                    ynt_copied.wait(pe, l3)
                    nc.tensor.matmul(t_ps[:, 1, 0:8], xn1t[:, l5.batch, :], rw[:, :], start=True, stop=True).then_inc(routed.sem, 1)
                if l3.exists:
                    ynt_copied.wait(pe, l3)
                    rotated.wait(pe, n, 3)
                    values_placed.wait(pe, n)
                    gate_in_ready.wait(pe, n)
                    nc.tensor.matmul(p_ps[:, 0:C], ynt[:, :], wo[:, :], start=True, stop=True).then_inc(out_projected.sem, 1)
                if l1.exists:
                    maxima_ready.wait(pe, l1)
                    ynt_copied.wait(pe, l3)
                    for c in range(2):
                        last = nc.tensor.transpose(tb_ps[0:NPAIR, c * P:c * P + P], mneg[:, l1.batch, c, :], eyeb_sb[:, :])
                    last.then_inc(max_transposed.sem, 1)
                if l2.exists:
                    weigh(l2, 2)
                    weigh(l2, 3)

            pipeline(pe, step, 6)

            def transpose_out(n, b):
                cheb_out_done.wait(pe, n, CHEB2 * (b + 1))
                s1_copied.wait(pe, *n.at(b - 1, 4))
                accumulated.wait(pe, n, 1)
                nc.tensor.transpose(t_ps[:, 0, :], oc[:, :], eye_sb[:, :]).then_inc(cheb_transposed.sem, 1)

            def project_out(n, b):
                cheb_out_copied.wait(pe, n, b + 1)
                nc.tensor.matmul(t_ps[:, 1, :], oct_[:, :], w_out[:, :], start=True, stop=True).then_inc(cheb_out_projected.sem, 1)

            def finish(n):
                transpose_out(n, B - 1)
                project_out(n, B - 1)

            def mix(n):
                def up(e, f):
                    gelu_done.wait(pe, *n.at(e * FB + f - 2, E * FB, 2))
                    for i, (a, b) in enumerate(PARTS):
                        last = nc.tensor.matmul(u_ps[f % 2], w16[:, 2 * FB * e + f, a, :], xg16[:, n.parity, b, :],
                                                start=i == 0, stop=i == len(PARTS) - 1)
                    last.then_inc(hidden_ready.sem, 1)

                def down(e, b):
                    low_ready.wait(pe, n, e * FB + FB)
                    if b == 0:
                        accumulated.wait(pe, *n.at_acc(e - 2))
                    for f in range(FB):
                        for i, (w, x) in enumerate(PARTS):
                            last = nc.tensor.matmul(d_ps[e % 2][:, b, :], hid[e % 2][:, x, f, b * P:b * P + P], w16[:, 2 * FB * e + FB + f, w, :],
                                                    start=f == 0 and i == 0, stop=f == FB - 1 and i == len(PARTS) - 1)
                    if b == B - 1:
                        last.then_inc(expert_ready.sem, 1)

                def task(what, b):
                    if what == "project":
                        v_copied.wait(pe, *n.at(b - 1, 4))
                        cheb_keys_done.wait(pe, n if b else n.before(1), CHEB1 * ((b - 1) % B) + 1)
                        nc.tensor.matmul(p_ps[:, 0:3 * C], xg[:, b, :], w_in[:, :], start=True, stop=True).then_inc(cheb_projected.sem, 1)
                    if what == "sums":
                        cheb_keys_done.wait(pe, n, CHEB1 * (b + 1))
                        prefix_weighted.wait(pe, *n.at(b - 1, 4))
                        nc.tensor.matmul(cc_ps[0][:, 0:3 * SW], tri_sb[:, :], kv[:, b % 2, 0:3 * SW], start=True, stop=True)
                        nc.tensor.matmul(cc_ps[1][:, 0:2 * SW], tri_sb[:, :], kv[:, b % 2, 3 * SW:5 * SW], start=True, stop=True).then_inc(prefix_summed.sem, 1)
                    if what == "transpose":
                        transpose_out(n, b)
                    if what == "project_out":
                        project_out(n, b)

                gathered.wait(pe, n, 3)
                task("project", 0)
                for f in range(FB):
                    up(0, f)
                if not n.first:
                    finish(n.before(1))
                for e in range(E):
                    for half, block in MIX:
                        if half == "up" and e + 1 < E:
                            up(e + 1, block)
                        if half == "down":
                            down(e, block)
                        if e == 0 and half == "up" and block == WEIGHTS_AT:
                            gathered.wait(pe, n)
                            s1_copied.wait(pe, n.before(1))
                            for b in range(B):
                                last = nc.tensor.transpose(t_ps[0:E, b, :], cwg[:, b, :], eye_sb[:, :])
                            last.then_inc(weights_transposed.sem, 1)
                        if e == 0 and half == "up" and block == BIAS_AT:
                            weights_copied.wait(pe, n)
                            for b in range(B):
                                last = nc.tensor.matmul(t_ps[:, b, :], cwt[:, b, :], b2_sb[:, :], start=True, stop=True)
                            last.then_inc(weights_transposed.sem, 1)
                        for what, b in SLOTS[e] if (half, block) == TASKS_AT else []:
                            task(what, b)

            pe.wait_ge(s_late_weights, 16 * 8)
            weights_split.wait(pe, Tile(TAUS, 0))
            logits_ready.wait(pe, Tile(TAUS, 0))
            rounds(pe, mix)
            finish(Round(TAUS - 1))

        @block.vector
        def _(dve):
            nc.vector.memset(ones_sb[:, :], 1.0)
            nc.vector.memset(half_sb[:, :], -0.5)
            nc.vector.memset(vs[:, :, C:SW], 1.0)
            nc.vector.memset(xs[:, :, :, 3, :], 0.0)
            nc.vector.memset(kt[:, :, :, 0:W], 0.0)
            nc.vector.memset(mm_sb[W:P, :, :], 0.0)
            nc.vector.memset(hide_sb[:, :, :], NEG).then_inc(s_cleared, 1)
            nc.vector.memset(vd[:, :, :, :, :], 0.0).then_inc(s_values_cleared, 1)
            dve.wait_ge(s_values_cleared, 1)
            nc.vector.memset(vd[0:W, :, :, :, 8:9], 1.0)
            nc.vector.memset(vd[W:P, :, :, :, 17:18], 1.0).then_inc(s_values_cleared, 1)
            dve.wait_ge(s_weights, 16 * 9)
            nc.vector.tensor_reduce(wsum[:, 0:1], wraw[:, :], AX.X, ALU.add, apply_absolute_value=True).then_inc(s_ternary_steps, 1)
            dve.wait_ge(s_abs_summed, 1)
            nc.vector.tensor_scalar(wsum[:, 1:2], t_ps[:, 0, 0:1], 1.0 / (C * C), 0.7, ALU.mult, ALU.mult).then_inc(s_ternary_steps, 1)
            dve.wait_ge(s_ternary_steps, 2)
            nc.vector.tensor_scalar(wneg[:, :], wraw[:, :], -1.0, wsum[:, 1:2], ALU.mult, ALU.is_gt).then_inc(s_ternary_steps, 1)
            dve.wait_ge(s_ternary_steps, 3)
            nc.vector.scalar_tensor_tensor(wneg[:, :], wraw[:, :], wsum[:, 1:2], wneg[:, :], ALU.is_gt, ALU.subtract).then_inc(s_ternary_steps, 1)
            dve.wait_ge(s_ternary_steps, 4)
            nc.vector.tensor_scalar(wp[:, 3 * C:4 * C], wneg[:, :], alpha_sb[:, 0:1], None, ALU.mult).then_inc(s_ternary_steps, 1)

            def maxima(n, j):
                max_scored.wait(dve, n, j + 1)
                max_transposed.wait(dve, n.before(4))
                nc.vector.tensor_reduce(mneg[:, n.batch, j // 2, (j % 2) * NG:(j % 2) * NG + NG], m_ps[j % 2][:, :, :],
                                        AX.X, ALU.max, negate=True).then_inc(maxima_ready.sem, 1)

            def step(head):
                n, l1, l3, l5 = (head.before(i) for i in (1, 2, 4, 6))
                if l5.exists:
                    rstd1_ready.wait(dve, l5)
                    nc.vector.tensor_scalar(xn1[:, l5.batch, :], xn1[:, l5.batch, :], rstd1[:, l5.batch, 1:2], None,
                                            ALU.mult).then_inc(xn1_ready.sem, 1)
                if l1.exists:
                    maxima(l1, 0)
                    maxima(l1, 1)
                if head.exists:
                    if head.static and head.batch == 0:
                        dve.wait_ge(s_x[head.tau], 16)
                    turn(dve, s_turn_dve)
                    nc.vector.bn_stats(stats[:, head.batch, :], x_all[:, head.index, :]).then_inc(stats_ready.sem, 1)
                    stats_ready.wait(dve, head, 1)
                    rstd_ready.wait(dve, head.before(4), 1)
                    turn(dve, s_turn_dve)
                    nc.vector.bn_aggr(mv[:, head.batch, :], stats[:, head.batch, :]).then_inc(stats_ready.sem, 1)
                if n.exists:
                    projected.wait(dve, n)
                    r = n.batch % 2
                    qk = p_ps[:, 0:2 * C].rearrange("p (h e f) -> p h e f", e=2, f=D // 2)
                    ra = rot[:, r, 0, :].rearrange("p (h d) -> p h d", d=D)
                    rbt = rot[:, r, 1, :].rearrange("p (h e f) -> p h e f", e=2, f=D // 2)
                    cos = rope_sb[:, n.tau, 0:D].unsqueeze(1).to_broadcast([P, 2 * H, D])
                    high_ready.wait(dve, n.before(2))
                    nc.vector.tensor_tensor(ra, p_ps[:, 0:2 * C].rearrange("p (h d) -> p h d", d=D), cos, ALU.mult).then_inc(rotated.sem, 1)
                    for e in range(2):
                        sin = rope_sb[:, n.tau, D + 4 * e:D + 4 * e + 4].unsqueeze(1).to_broadcast([P, 2 * H, D // 2])
                        nc.vector.tensor_tensor(rbt[:, :, e, :], qk[:, :, 1 - e, :], sin, ALU.mult).then_inc(rotated.sem, 1)
                    gate_steps.wait(dve, n.before(4), 3)
                    nc.vector.tensor_tensor(z[:, n.batch, :], p_ps[:, 3 * C:4 * C], bias0_sb[:, :], ALU.add).then_inc(gate_in_ready.sem, 1)
                    rotated.wait(dve, n, 3)
                    nc.vector.tensor_tensor(rot[:, r, 0, :], rot[:, r, 0, :], rot[:, r, 1, :], ALU.add).then_inc(rotated.sem, 1)
                if l3.exists:
                    y_transposed.wait(dve, l3)
                    yn_transposed.wait(dve, l3.before(1))
                    yv = t_ps[:, 2:4, :].rearrange("p j (g w) -> p (j g) w", w=VW)[:, :, 0:18].rearrange("p i (a e) -> p i a e", a=2)
                    nc.vector.reciprocal(rden[:, :].rearrange("p (i a) -> p i a", a=2), yv[:, :, :, 8]).then_inc(y_normed.sem, 1)
                    y_normed.wait(dve, l3, 1)
                    nc.vector.tensor_tensor(yn[:, :].rearrange("p (i a d) -> p i a d", a=2, d=D), yv[:, :, :, 0:8],
                                            rden[:, :].rearrange("p (i a) -> p i a", a=2).unsqueeze(3).to_broadcast([P, NPAIR, 2, D]),
                                            ALU.mult).then_inc(y_normed.sem, 1)
                if l1.exists:
                    maxima(l1, 2)
                if n.exists:
                    high_ready.wait(dve, n)
                    rv = rot[:, r, 0, :].rearrange("p (h d) -> p h d", d=D)
                    nc.vector.tensor_tensor(xs[:, n.batch, 0:H, 1, :], rv[:, 0:H, :], xs[:, n.batch, 0:H, 0, :], ALU.subtract).then_inc(rotated.sem, 1)
                    nc.vector.tensor_tensor(xs[:, n.batch, H:2 * H, 2, :], rv[:, H:2 * H, :], xs[:, n.batch, H:2 * H, 0, :], ALU.subtract).then_inc(rotated.sem, 1)
                if l3.exists:
                    gate_exp_ready.wait(dve, l3)
                    nc.vector.tensor_scalar(gd[:, 0, :], ez[:, :], 1.0, None, ALU.add).then_inc(gate_steps.sem, 1)
                    gate_steps.wait(dve, l3, 1)
                    nc.vector.reciprocal(gd[:, 1, :], gd[:, 0, :]).then_inc(gate_steps.sem, 1)
                    gate_steps.wait(dve, l3, 2)
                    nc.vector.tensor_tensor(gd[:, 2, :], z[:, l3.batch, :], gd[:, 1, :], ALU.mult).then_inc(gate_steps.sem, 1)
                if l1.exists:
                    maxima(l1, 3)
                if l3.exists:
                    out_projected.wait(dve, l3)
                    gate_steps.wait(dve, l3, 3)
                    nc.vector.tensor_tensor(sg[:, :], p_ps[:, 0:C], gd[:, 2, :], ALU.mult).then_inc(gate_steps.sem, 1)
                    gate_steps.wait(dve, l3, 4)
                    nc.vector.tensor_tensor(x_all[:, l3.index, :], x_all[:, l3.index, :], sg[:, :], ALU.add).then_inc(gate_steps.sem, 1)
                    gate_steps.wait(dve, l3, 5)
                    turn(dve, s_turn_dve)
                    nc.vector.bn_stats(stats1[:, l3.batch, :], x_all[:, l3.index, :]).then_inc(gate_steps.sem, 1)
                if l1.exists:
                    max_transposed.wait(dve, l1)
                    scored.wait(dve, l1.before(4))
                    if l1.static:
                        dve.wait_ge(s_masks, 16 * 8)
                    mt = tb_ps[0:NPAIR, 0:2 * P].rearrange("p (c a q) -> p a c q", c=2, a=2)
                    for a in range(2):
                        nc.vector.tensor_copy(mm_sb[W + 32 * a:W + 32 * a + NPAIR, l1.batch, :].rearrange("p (r c q) -> p r c q", r=2, c=2),
                                              mt[:, a, :, :].unsqueeze(1).to_broadcast([NPAIR, 2, 2, W])).then_inc(maxima_placed.sem, 1)
                if head.exists:
                    rstd_ready.wait(dve, head)
                    xn_transposed.wait(dve, head.before(4))
                    nc.vector.tensor_scalar(xn[:, head.batch, :], x_all[:, head.index, :], mv[:, head.batch, 0:1], rstd[:, head.batch, 1:2],
                                            ALU.subtract, ALU.mult).then_inc(xn_ready.sem, 1)
                if l5.exists:
                    routed.wait(dve, l5)
                    max_transposed.wait(dve, l1)
                    nc.vector.tensor_tensor(logits[:, l5.index, :], t_ps[:, 1, 0:8], rb[:, :], ALU.add).then_inc(logits_ready.sem, 1)
                if l3.exists:
                    gate_steps.wait(dve, l3, 6)
                    turn(dve, s_turn_dve)
                    nc.vector.bn_aggr(mv1[:, l3.batch, :], stats1[:, l3.batch, :]).then_inc(gate_steps.sem, 1)
                    gate_steps.wait(dve, l3, 7)
                    xn1_stored.wait(dve, l3.before(4))
                    xn1_transposed.wait(dve, l3.before(4))
                    nc.vector.tensor_scalar(xn1[:, l3.batch, :].rearrange("p (b a) -> p a b", b=IL), x_all[:, l3.index, :].rearrange("p (a b) -> p a b", b=IL), mv1[:, l3.batch, 0:1], None, ALU.subtract).then_inc(gate_steps.sem, 1)
                    gate_steps.wait(dve, l3, 8)
                    nc.vector.tensor_tensor(sg[:, :], xn1[:, l3.batch, :], xn1[:, l3.batch, :], ALU.mult).then_inc(gate_steps.sem, 1)
                    gate_steps.wait(dve, l3, 9)
                    nc.vector.tensor_reduce(mv1[:, l3.batch, 1:2], sg[:, :], AX.X, ALU.add).then_inc(gate_steps.sem, 1)

            for n in range(8):
                step(Tile(0, n))
            dve.wait_ge(s_x[2], 16 * (TAUS - 2))
            with dve.Fori(2, TAUS) as t:
                for k in range(4):
                    step(Tile(t, k))
            for n in range(6):
                step(Tile(TAUS, n))

            route = [0]

            def link(ins):
                route[0] += 1
                ins.then_inc(s_route_steps, 1)
                dve.wait_ge(s_route_steps, route[0])

            def wide(ap):
                return ap.unsqueeze(2).to_broadcast([P, NT, E])

            logits_ready.wait(dve, Tile(TAUS, 0))
            dve.wait_ge(s_late_weights, 16 * 8)
            left = logits[:, :, :]
            for k in range(2):
                link(nc.vector.tensor_reduce(rs[:, 2 * k, :], left, AX.X, ALU.max))
                link(nc.vector.tensor_tensor(rt[:, 0, :, :], left, wide(rs[:, 2 * k, :]), ALU.is_equal))
                link(nc.vector.tensor_tensor(rt[:, 1, :, :], rt[:, 0, :, :], desc_sb[:, :].unsqueeze(1).to_broadcast([P, NT, E]), ALU.mult))
                link(nc.vector.tensor_reduce(rs[:, 1, :], rt[:, 1, :, :], AX.X, ALU.max))
                link(nc.vector.tensor_tensor(rt[:, 2 + k, :, :], rt[:, 1, :, :], wide(rs[:, 1, :]), ALU.is_equal))
                if k == 0:
                    link(nc.vector.scalar_tensor_tensor(rt[:, 4, :, :], rt[:, 2, :, :], -3e38, logits[:, :, :], ALU.mult, ALU.add))
                    left = rt[:, 4, :, :]
                    link(nc.vector.tensor_reduce(rs[:, 3, :], left, AX.X, ALU.max))
                    link(nc.vector.tensor_tensor(rs[:, 4, :], rs[:, 3, :], rs[:, 0, :], ALU.subtract))
            dve.wait_ge(s_route_exp, 1)
            link(nc.vector.tensor_scalar(rs[:, 6, :], rs[:, 5, :], 1.0, None, ALU.add))
            link(nc.vector.reciprocal(rs[:, 7, :], rs[:, 6, :]))
            link(nc.vector.tensor_tensor(rs[:, 6, :], rs[:, 5, :], rs[:, 7, :], ALU.mult))
            link(nc.vector.tensor_tensor(rt[:, 2, :, :], rt[:, 2, :, :], wide(rs[:, 7, :]), ALU.mult))
            link(nc.vector.tensor_tensor(rt[:, 3, :, :], rt[:, 3, :, :], wide(rs[:, 6, :]), ALU.mult))
            link(nc.vector.tensor_tensor(cw[:, :, :], rt[:, 2, :, :], rt[:, 3, :, :], ALU.add))
            link(nc.vector.memset(eps2_sb[:, :], 1e-12))
            assert route[0] == ROUTE

            def final_step(n, at, ins, wait=True):
                ins.then_inc(norm_steps.sem, 1)
                if wait:
                    norm_steps.wait(dve, n, at)

            def normalise(n):
                accumulated.wait(dve, n)
                for b in range(B):
                    final_step(n, b + 1, nc.vector.bn_stats(stats2[:, b, :], acc[:, b, :]), b == B - 1)
                for b in range(B):
                    turn(dve, s_turn_dve)
                    final_step(n, B + b + 1, nc.vector.bn_aggr(mv2[:, b, :], stats2[:, b, :]), False)
                rstd2_ready.wait(dve, n)
                s1_gated.wait(dve, n.before(1))
                for b in range(B):
                    final_step(n, 2 * B + b + 1, nc.vector.tensor_scalar(y2[:, b, :], acc[:, b, :], mv2[:, b, 0:1], rstd2[:, 1, b:b + 1],
                                                                         ALU.subtract, ALU.mult), b == B - 1)
                final_step(n, 13, nc.vector.tensor_tensor(y2[:, :, :], y2[:, :, :], lnw_sb[:, :].unsqueeze(1).to_broadcast([P, B, C]), ALU.mult))
                final_step(n, 14, nc.vector.tensor_tensor(y2[:, :, :], y2[:, :, :], lnb_sb[:, :].unsqueeze(1).to_broadcast([P, B, C]), ALU.add))

            def gate(n):
                tanh_ready.wait(dve, n)
                s1_gated.wait(dve, n, 1)
                final_step(n, 15, nc.vector.scalar_tensor_tensor(e2[:, :, :], e2[:, :, :], 1.0, res[:, :, :], ALU.add, ALU.mult), False)

            def mix(n):
                def cheb_keys(b):
                    at = [CHEB1 * b]

                    def done(ins, wait=True):
                        at[0] += 1
                        ins.then_inc(cheb_keys_done.sem, 1)
                        if wait:
                            cheb_keys_done.wait(dve, n, at[0])

                    v_copied.wait(dve, n, b + 1)
                    x, x2 = tc[:, 0, :, 0:C], xc[:, :].rearrange("p (a c) -> p a c", a=2)
                    done(nc.vector.tensor_scalar(x2, p_ps[:, 0:2 * C].rearrange("p (a c) -> p a c", a=2), INV, CLIP, ALU.mult, ALU.min))
                    done(nc.vector.tensor_scalar(x, x2, -CLIP, None, ALU.max))
                    done(nc.vector.scalar_tensor_tensor(x2, x, 2.0, x, ALU.mult, ALU.mult))
                    done(nc.vector.tensor_scalar(tc[:, 1, :, 0:C], x2, 1.0, None, ALU.subtract))
                    for j in range(2, ORD):
                        done(nc.vector.scalar_tensor_tensor(x2, x, 2.0, tc[:, j - 1, :, 0:C], ALU.mult, ALU.mult))
                        done(nc.vector.tensor_tensor(tc[:, j, :, 0:C], x2, tc[:, j - 2, :, 0:C], ALU.subtract))
                    done(nc.vector.tensor_reduce(tc[:, :, :, C:SW].rearrange("p j a h -> p (j a) h"),
                                                 tc[:, :, :, 0:C].rearrange("p j a (h d) -> p (j a) h d", d=D), AX.X, ALU.add))
                    prefix_summed.wait(dve, *n.at(b - 2, 4))
                    done(nc.vector.tensor_tensor(kv[:, b % 2, :].rearrange("p (j w) -> p j w", w=SW), tc[:, :, 1, :],
                                                 vs[:, b % 2, :].unsqueeze(1).to_broadcast([P, ORD, SW]), ALU.mult))
                    n.wait_dma(dve, s_carry[b])
                    done(nc.vector.tensor_tensor(kv[0:1, b % 2, :], kv[0:1, b % 2, :], carry[0:1, b, :], ALU.add), False)
                    assert at[0] == CHEB1 * (b + 1)

                def cheb_out(b):
                    at = [CHEB2 * b]

                    def done(ins, wait=True):
                        at[0] += 1
                        ins.then_inc(cheb_out_done.sem, 1)
                        if wait:
                            cheb_out_done.wait(dve, n, at[0])

                    prefix_weighted.wait(dve, n, b + 1)
                    done(nc.vector.tensor_tensor(pr[:, :, :], tc[:, :, 0, :], pr[:, :, :], ALU.mult))
                    done(nc.vector.tensor_reduce(nd[:, :], pr[:, :, :].rearrange("p j w -> p w j"), AX.X, ALU.add))
                    done(nc.vector.tensor_scalar(dn[:, 0, :], nd[:, C:SW], 1e-7, None, ALU.add))
                    done(nc.vector.reciprocal(dn[:, 1, :], dn[:, 0, :]))
                    cheb_transposed.wait(dve, *n.at(b - 1, 4))
                    done(nc.vector.tensor_tensor(oc[:, :].rearrange("p (h d) -> p h d", d=D), nd[:, 0:C].rearrange("p (h d) -> p h d", d=D),
                                                 dn[:, 1, :].unsqueeze(2).to_broadcast([P, H, D]), ALU.mult))
                    assert at[0] == CHEB2 * (b + 1)

                def accumulate(e):
                    expert_ready.wait(dve, n, e + 1)
                    for b in range(B):
                        accumulated.wait(dve, n, 1 if e == 0 else 1 + 4 * (e - 1) + b + 1)
                        nc.vector.scalar_tensor_tensor(acc[:, b, :], d_ps[e % 2][:, b, :], cwg[:, b, e:e + 1], acc[:, b, :],
                                                       ALU.mult, ALU.add).then_inc(accumulated.sem, 1)

                def residual():
                    weights_transposed.wait(dve, n, 2)
                    norm_steps.wait(dve, n.before(1), 12)
                    nc.vector.tensor_tensor(acc[:, :, :], xn1_all[:, n.tiles, :], t_ps[:, :, :], ALU.add).then_inc(accumulated.sem, 1)

                for what, i in DVE_ORDER:
                    if what == "keys":
                        cheb_keys(i)
                    elif what == "residual":
                        residual()
                    elif what == "sum":
                        accumulate(i)
                    elif what == "out":
                        cheb_out(i)
                    elif what == "gate" and not n.first:
                        gate(n.before(1))
                normalise(n)

            rounds(dve, mix)
            gate(Round(TAUS - 1))


def constants():
    import numpy as np
    inv = (1.0 / np.float32(10000.0) ** (np.arange(0, D, 2, dtype=np.float32) / np.float32(D))).astype(np.float32)
    ang = np.outer(np.arange(T, dtype=np.float32), inv).astype(np.float32)
    cos, sin = np.cos(ang), np.sin(ang)
    rope = np.concatenate([cos, cos, sin, -sin], 1).astype(np.float32).reshape(TAUS, P, 2 * D).transpose(1, 0, 2)
    q, k = np.arange(W)[:, None], np.arange(W)[None, :]
    before, own = np.where(k >= q, 0, NEG), np.where(k <= q, 0, NEG)
    win_max = np.tile(np.concatenate([before, own], 1)[:, None, :], (2, NG, 1))
    win_exp = np.concatenate([own.T, before.T, before.T, own.T], 1)
    sel = np.zeros((P, NPAIR, P))
    for r in range(W):
        sel[r, :, r] = sel[r, :, W + r] = 1
    for i in range(NPAIR):
        sel[W + i, i, 0:W] = sel[W + 32 + i, i, W:P] = 1
    f = np.float32
    return {"rope": np.ascontiguousarray(rope), "eye": np.eye(P, dtype=f), "win_max": win_max.astype(f),
            "win_exp": win_exp.astype(f), "pair_sel": sel.astype(f),
            "tri": np.triu(np.ones((P, P), f)), "descend": np.tile(np.arange(E, 0, -1).astype(f), (P, 1))}


def kernel(L0_attn_x, L0_attn_w_attn, L0_attn_w_proj, L0_ffn_weight, L0_ffn_alpha, L0_ffn_bias, L1_attn_W_in,
           L1_attn_W_out, L1_ffn_router_w, L1_ffn_router_b, L1_ffn_w1, L1_ffn_b1, L1_ffn_w2, L1_ffn_b2, L1_ffn_ln_w,
           L1_ffn_ln_b):
    import numpy as np
    import concourse.bacc as bacc
    from concourse.bass_utils import run_bass_kernel_spmd

    order = [(4 * g + 2 * jp + a) * D + d for jp in range(2) for g in range(NG) for a in range(2) for d in range(D)]
    w_attn = np.asarray(L0_attn_w_attn)

    runs = np.arange(C).reshape(-1, IL).T.reshape(-1)

    w1 = np.asarray(L1_ffn_w1).transpose(2, 0, 1)[runs].reshape(P, E, FB, P)
    w2 = np.asarray(L1_ffn_w2).reshape(E, C, FB, P).transpose(3, 0, 2, 1)

    def rows(a):
        return np.tile(np.asarray(a)[None, :], (P, 1))

    arrays = {
        "x": np.asarray(L0_attn_x),
        "proj_w": np.concatenate([w_attn[0:2 * C], w_attn[2 * C:3 * C][order]]).T,
        "ffn_w": np.asarray(L0_ffn_weight).T,
        "alpha": rows(L0_ffn_alpha),
        "bias0": rows(L0_ffn_bias),
        "out_w": np.asarray(L0_attn_w_proj).T[order],
        "router_w": np.asarray(L1_ffn_router_w).T[runs],
        "router_b": rows(L1_ffn_router_b),
        "cheb_w": np.asarray(L1_attn_W_in).T[runs],
        "cheb_out_w": np.asarray(L1_attn_W_out).T,
        "experts_w": np.concatenate([w1, w2], 2).reshape(P, 2 * E * FB, P),
        "b1": np.asarray(L1_ffn_b1).reshape(E, FB, P).transpose(2, 0, 1),
        "b2": np.asarray(L1_ffn_b2),
        "ln_w": rows(L1_ffn_ln_w),
        "ln_b": rows(L1_ffn_ln_b),
        **constants(),
    }
    nc = bacc.Bacc("TRN2", target_bir_lowering=False, num_devices=1)
    given, args = {}, {}
    for name, a in arrays.items():
        given[f"in_{name}"] = a = np.ascontiguousarray(a)
        args[name] = nc.dram_tensor(f"in_{name}", a.shape, mybir.dt.from_np(a.dtype), kind="ExternalInput").ap()
    args["out"] = nc.dram_tensor("out_0", (B, T, C), F32, kind="ExternalOutput").ap()
    program(nc, **args)
    return run_bass_kernel_spmd(nc, [given], core_ids=[0]).results[0]["out_0"]
```
